# Optimizing a Trainium2 kernel written in Bass

```python
import numpy as np
import jax
import jax.numpy as jnp

def _softmax(x, axis=-1):
    return jax.nn.softmax(x, axis=axis)

def _gelu(x):
    return jax.nn.gelu(x, approximate=True)

def _silu(x):
    return jax.nn.silu(x)

def _sigmoid(x):
    return jax.nn.sigmoid(x)

def _layernorm(x, axis=-1, eps=1e-05):
    m = jnp.mean(x, axis=axis, keepdims=True)
    v = jnp.var(x, axis=axis, keepdims=True)
    return (x - m) / jnp.sqrt(v + eps)

def _scatter_add(tgt, idx, src, axis=0):
    return tgt.at[idx].add(src)

def _segment_sum(src, seg, n):
    return jax.ops.segment_sum(src, seg, n)
kernel_name = 'mk_xattn_ffn_d4_seqx_r4_cdc0a5'

def setup_inputs(seed: int=0):
    np.random.seed(seed)
    _w = jnp.asarray

    def _rec_inputs():
        import jax
        import jax.numpy as jnp
        _rk = jax.random.key(seed)
        x = -0.0002928 + 1 * jax.random.normal(jax.random.fold_in(_rk, 1), (4, 512, 256), jnp.float32)
        _lenS = 512 - jax.random.randint(jax.random.fold_in(_rk, 7), (4,), 0, max(1, 512 // 4) + 1, jnp.int32)
        _lenS2 = 512 - jax.random.randint(jax.random.fold_in(_rk, 8), (4,), 0, max(1, 512 // 4) + 1, jnp.int32)
        _ctx_1024P = jax.random.normal(jax.random.fold_in(_rk, 11), (4, 16, 256), jnp.float32)
        _ctx_1024c = jax.random.dirichlet(jax.random.fold_in(_rk, 511), 0.3 * jnp.ones((16,), jnp.float32), (4, 512))
        _ctx_1024t = jnp.einsum('bsk,bkd->bsd', _ctx_1024c, _ctx_1024P)
        _ctx_1024t = _ctx_1024t * jax.lax.rsqrt(jnp.mean(jnp.square(_ctx_1024t)) + 1e-12) * 0.953939
        ctx_1024 = -1.39393e-06 + 0.999914 * (_ctx_1024t + 0.3 * jax.random.normal(jax.random.fold_in(_rk, 611), (4, 512, 256), jnp.float32))
        fside_BxSxS2_0 = -1.47943e-05 + 1.00017 * jax.random.normal(jax.random.fold_in(_rk, 13), (4, 512, 512), jnp.float32)
        _validS = jnp.arange(512)[None, :] < _lenS[:, None]
        _validS2 = jnp.arange(512)[None, :] < _lenS2[:, None]
        _causal = jnp.tril(jnp.ones((512, 512), dtype=bool))
        mask_Bx1xSxS2_ik0 = jnp.where(jnp.broadcast_to(_validS2[:, None, None, :], (4, 1, 512, 512)), 0, 1).astype(jnp.int32)
        return (x, ctx_1024, fside_BxSxS2_0, mask_Bx1xSxS2_ik0)
    x, ctx_1024, fside_BxSxS2_0, mask_Bx1xSxS2_ik0 = _rec_inputs()

    def _L0_xattn_setup():
        import jax, jax.numpy as jnp
        import numpy as np
        H = 16
        D_MODEL = 256
        D_K = D_MODEL // H
        key = jax.random.key(seed)
        ks = jax.random.split(key, 11)
        B, T = (2, 512)
        s = 1.0 / np.sqrt(D_MODEL)
        return {'query': jax.random.normal(ks[0], (B, T, D_MODEL), dtype=jnp.float32), 'key': jax.random.normal(ks[1], (B, T, D_MODEL), dtype=jnp.float32), 'value': jax.random.normal(ks[2], (B, T, D_MODEL), dtype=jnp.float32), 'Wq': jax.random.normal(ks[3], (D_MODEL, D_MODEL), dtype=jnp.float32) * s, 'bq': jnp.zeros((D_MODEL,), dtype=jnp.float32), 'Wk': jax.random.normal(ks[4], (D_MODEL, D_MODEL), dtype=jnp.float32) * s, 'bk': jnp.zeros((D_MODEL,), dtype=jnp.float32), 'Wv': jax.random.normal(ks[5], (D_MODEL, D_MODEL), dtype=jnp.float32) * s, 'bv': jnp.zeros((D_MODEL,), dtype=jnp.float32), 'Wo': jax.random.normal(ks[6], (D_MODEL, D_MODEL), dtype=jnp.float32) * s, 'bo': jnp.zeros((D_MODEL,), dtype=jnp.float32)}
    _L0_xattn_all = _L0_xattn_setup()
    _L0_xattn_in = {k: v for k, v in _L0_xattn_all.items() if k in ('Wq', 'bq', 'Wk', 'bk', 'Wv', 'bv', 'Wo', 'bo')}
    del _L0_xattn_all

    def _L0_ffn_setup():
        import jax, jax.numpy as jnp
        import numpy as np
        D_MODEL = 256
        D_FF = 1024
        NUM_EXPERTS = 8
        key = jax.random.key(seed)
        ks = jax.random.split(key, 8)
        scale_in = 1.0 / np.sqrt(D_MODEL)
        scale_ff = 1.0 / np.sqrt(D_FF)
        x = jax.random.normal(ks[0], (4, 512, D_MODEL), dtype=jnp.float32)
        gate_w = jax.random.uniform(ks[1], (NUM_EXPERTS, D_MODEL), jnp.float32, -scale_in, scale_in)
        gate_b = jax.random.uniform(ks[2], (NUM_EXPERTS,), jnp.float32, -scale_in, scale_in)
        expert_bias = jnp.zeros((NUM_EXPERTS,), dtype=jnp.float32)
        w1 = jax.random.uniform(ks[3], (NUM_EXPERTS, D_MODEL, D_FF), jnp.float32, -scale_in, scale_in)
        b1 = jax.random.uniform(ks[4], (NUM_EXPERTS, D_FF), jnp.float32, -scale_in, scale_in)
        w2 = jax.random.uniform(ks[5], (NUM_EXPERTS, D_FF, D_MODEL), jnp.float32, -scale_ff, scale_ff)
        b2 = jax.random.uniform(ks[6], (NUM_EXPERTS, D_MODEL), jnp.float32, -scale_ff, scale_ff)
        return {'x': x, 'gate_w': gate_w, 'gate_b': gate_b, 'expert_bias': expert_bias, 'w1': w1, 'b1': b1, 'w2': w2, 'b2': b2}
    _L0_ffn_all = _L0_ffn_setup()
    _L0_ffn_in = {k: v for k, v in _L0_ffn_all.items() if k in ('gate_w', 'gate_b', 'expert_bias', 'w1', 'b1', 'w2', 'b2')}
    del _L0_ffn_all

    def _L1_xattn_setup():
        import jax, jax.numpy as jnp
        import numpy as np
        DIM = 256
        N_HEADS = 16
        HEAD_DIM = DIM // N_HEADS
        GAMMA = 10.0

        def larope_cos_sin(seq_len, gamma, head_dim):
            inv_freq = 1.0 / 10000.0 ** (jnp.arange(0, head_dim, 2, dtype=jnp.float32) / head_dim)
            t = jnp.arange(seq_len, dtype=jnp.float32)
            freqs = jnp.outer(gamma * (t / seq_len), inv_freq)
            emb = jnp.concatenate([freqs, freqs], axis=-1)
            return (jnp.cos(emb), jnp.sin(emb))

        def apply_rope(x, cos, sin):
            d = x.shape[-1] // 2
            x1, x2 = (x[..., :d], x[..., d:])
            c = cos[None, None, :, :d]
            s = sin[None, None, :, :d]
            return jnp.concatenate([x1 * c - x2 * s, x1 * s + x2 * c], axis=-1)
        key = jax.random.key(seed)
        ks = jax.random.split(key, 11)
        B, Lq, Lk = (4, 512, 256)
        std = 1.0 / np.sqrt(DIM)
        inp = {'query': jax.random.normal(ks[0], (B, Lq, DIM), dtype=jnp.float32), 'key': jax.random.normal(ks[1], (B, Lk, DIM), dtype=jnp.float32), 'value': jax.random.normal(ks[2], (B, Lk, DIM), dtype=jnp.float32), 'Wq': jax.random.normal(ks[3], (DIM, DIM), dtype=jnp.float32) * std, 'bq': jnp.zeros((DIM,), dtype=jnp.float32), 'Wk': jax.random.normal(ks[4], (DIM, DIM), dtype=jnp.float32) * std, 'bk': jnp.zeros((DIM,), dtype=jnp.float32), 'Wv': jax.random.normal(ks[5], (DIM, DIM), dtype=jnp.float32) * std, 'bv': jnp.zeros((DIM,), dtype=jnp.float32), 'Wo': jax.random.normal(ks[6], (DIM, DIM), dtype=jnp.float32) * std, 'bo': jnp.zeros((DIM,), dtype=jnp.float32)}
        return inp
    _L1_xattn_all = _L1_xattn_setup()
    _L1_xattn_in = {k: v for k, v in _L1_xattn_all.items() if k in ('Wq', 'bq', 'Wk', 'bk', 'Wv', 'bv', 'Wo', 'bo')}
    del _L1_xattn_all

    def _L1_ffn_setup():
        import jax, jax.numpy as jnp
        import numpy as np
        E = 32
        H = 256
        I = 128
        G = 8
        TKG = 4
        TOPK = 8
        NSH = 2
        SCALE = 2.5
        key = jax.random.key(seed)
        ks = jax.random.split(key, 10)
        s = 0.02
        return {'hidden_states': jax.random.normal(ks[0], (2, 256, H), jnp.float32), 'gate_w': jax.random.normal(ks[1], (E, H), jnp.float32) * s, 'gate_bias': jax.random.normal(ks[2], (E,), jnp.float32) * s, 'w_gate': jax.random.normal(ks[3], (E, I, H), jnp.float32) * s, 'w_up': jax.random.normal(ks[4], (E, I, H), jnp.float32) * s, 'w_down': jax.random.normal(ks[5], (E, H, I), jnp.float32) * s, 'sh_gate': jax.random.normal(ks[6], (I * NSH, H), jnp.float32) * s, 'sh_up': jax.random.normal(ks[7], (I * NSH, H), jnp.float32) * s, 'sh_down': jax.random.normal(ks[8], (H, I * NSH), jnp.float32) * s}
    _L1_ffn_all = _L1_ffn_setup()
    _L1_ffn_in = {k: v for k, v in _L1_ffn_all.items() if k in ('gate_w', 'gate_bias', 'w_gate', 'w_up', 'w_down', 'sh_gate', 'sh_up', 'sh_down')}
    del _L1_ffn_all

    def _L2_xattn_setup():
        import jax, jax.numpy as jnp
        import numpy as np
        import math
        B, S, D, H = (2, 512, 256, 16)
        DK = D // H

        def _split_heads(x):
            b, s, _ = x.shape
            return x.reshape(b, s, H, DK).transpose(0, 2, 1, 3)
        key = jax.random.key(seed)
        ks = jax.random.split(key, 12)

        def xavier(k, shape):
            fan_in, fan_out = (shape[1], shape[0])
            limit = math.sqrt(6.0 / (fan_in + fan_out))
            return jax.random.uniform(k, shape, jnp.float32, -limit, limit)
        inp = {'query': jax.random.normal(ks[0], (B, S, D), jnp.float32), 'key': jax.random.normal(ks[1], (B, S, D), jnp.float32), 'value': jax.random.normal(ks[2], (B, S, D), jnp.float32), 'mask': jnp.broadcast_to(jnp.tril(jnp.ones((S, S), jnp.int32)), (B, 1, S, S)), 'Wq': xavier(ks[3], (D, D)), 'bq': jnp.zeros((D,), jnp.float32), 'Wk': xavier(ks[4], (D, D)), 'bk': jnp.zeros((D,), jnp.float32), 'Wv': xavier(ks[5], (D, D)), 'bv': jnp.zeros((D,), jnp.float32), 'Wo': xavier(ks[6], (D, D)), 'bo': jnp.zeros((D,), jnp.float32)}
        return inp
    _L2_xattn_all = _L2_xattn_setup()
    _L2_xattn_in = {k: v for k, v in _L2_xattn_all.items() if k in ('Wq', 'bq', 'Wk', 'bk', 'Wv', 'bv', 'Wo', 'bo')}
    del _L2_xattn_all

    def _L2_ffn_setup():
        import jax, jax.numpy as jnp
        import numpy as np
        E = 8
        K = 2
        CAPACITY_FACTOR = 1.25
        key = jax.random.key(seed)
        ks = jax.random.split(key, 4)
        B, T, C, H = (8, 512, 256, 1024)
        x = jax.random.normal(ks[0], (B, T, C), jnp.float32)
        Wr = jax.random.normal(ks[1], (C, E), jnp.float32) * 0.02
        br = jnp.zeros((E,), jnp.float32)
        W1 = jax.random.normal(ks[2], (E, C, H), jnp.float32) * 0.02
        b1 = jnp.zeros((E, H), jnp.float32)
        W2 = jax.random.normal(ks[3], (E, H, C), jnp.float32) * 0.02
        b2 = jnp.zeros((E, C), jnp.float32)
        return {'x': x, 'Wr': Wr, 'br': br, 'W1': W1, 'b1': b1, 'W2': W2, 'b2': b2}
    _L2_ffn_all = _L2_ffn_setup()
    _L2_ffn_in = {k: v for k, v in _L2_ffn_all.items() if k in ('Wr', 'br', 'W1', 'b1', 'W2', 'b2')}
    del _L2_ffn_all

    def _L3_xattn_setup():
        import jax, jax.numpy as jnp
        import numpy as np
        D = 256
        key = jax.random.key(seed)
        ks = jax.random.split(key, 13)
        B, S, d = (4, 512, D)
        inp = {'q_in': jax.random.normal(ks[0], (B, S, d), jnp.float32), 'k_in': jax.random.normal(ks[1], (B, S, d), jnp.float32), 'v_in': jax.random.normal(ks[2], (B, S, d), jnp.float32), 'phi_risk': jax.random.normal(ks[3], (B, S, S), jnp.float32), 'phi_prio': jax.random.normal(ks[4], (B, S, S), jnp.float32), 'phi_impl': jax.random.normal(ks[5], (B, S, S), jnp.float32), 'Wq': jax.random.normal(ks[6], (d, d), jnp.float32) / np.sqrt(d), 'bq': jax.random.normal(ks[7], (d,), jnp.float32) * 0.01, 'Wk': jax.random.normal(ks[8], (d, d), jnp.float32) / np.sqrt(d), 'bk': jax.random.normal(ks[9], (d,), jnp.float32) * 0.01, 'Wv': jax.random.normal(ks[10], (d, d), jnp.float32) / np.sqrt(d), 'bv': jax.random.normal(ks[11], (d,), jnp.float32) * 0.01, 'beta_risk': jnp.float32(0.1), 'beta_prio': jnp.float32(0.1), 'beta_impl': jnp.float32(0.1)}
        return inp
    _L3_xattn_all = _L3_xattn_setup()
    _L3_xattn_in = {k: v for k, v in _L3_xattn_all.items() if k in ('Wq', 'bq', 'Wk', 'bk', 'Wv', 'bv', 'beta_risk', 'beta_prio', 'beta_impl')}
    del _L3_xattn_all

    def _L3_ffn_setup():
        import jax, jax.numpy as jnp
        import numpy as np
        N_EXP = 8
        TOP_K = 2
        CAP_FACTOR = 1.25
        NEG_INF = -1000000000.0

        def _moe_forward(x, w_g, c_fc, c_proj):
            B, T, D = x.shape
            N = B * T
            xf = x.reshape(N, D)
            logits = xf @ w_g
            topv, topi = jax.lax.top_k(logits, TOP_K)
            full = jnp.full_like(logits, NEG_INF)
            full = full.at[jnp.arange(N)[:, None], topi].set(topv)
            probs = jax.nn.softmax(full, axis=-1)
            capacity = int(TOP_K * CAP_FACTOR * N / N_EXP)
            capacity += capacity % 2
            mask = jax.nn.one_hot(jnp.swapaxes(topi, 0, 1), N_EXP, dtype=jnp.int32)
            rank = jnp.cumsum(mask.reshape(TOP_K * N, N_EXP), axis=0).reshape(TOP_K, N, N_EXP) - 1
            mask = mask * (rank < capacity)
            rank_sel = jnp.sum(mask * rank, axis=-1)
            wts = jnp.sum(mask * probs[None], axis=-1)
            cb = jnp.zeros((N, N_EXP, capacity), x.dtype)
            tok = jnp.arange(N)
            for k in range(TOP_K):
                cb = cb.at[tok, topi[:, k], rank_sel[k]].add(wts[k])
            sec_mask = (cb != 0).astype(x.dtype)
            exp_batches = jnp.einsum('nec,nd->ecd', sec_mask, xf)
            h = jax.nn.gelu(jnp.einsum('ecd,edh->ech', exp_batches, c_fc), approximate=False)
            exp_out = jnp.einsum('ech,ehd->ecd', h, c_proj)
            out = jnp.einsum('nec,ecd->nd', cb, exp_out)
            return out.reshape(B, T, D)
        key = jax.random.key(seed)
        k1, k2, k3, k4 = jax.random.split(key, 4)
        B, T, D = (4, 128, 256)
        H = 4 * D
        x = jax.random.normal(k1, (B, T, D), jnp.float32)
        w_g = jax.random.normal(k2, (D, N_EXP), jnp.float32) * 0.02
        c_fc = jax.random.normal(k3, (N_EXP, D, H), jnp.float32) * 0.02
        c_proj = jax.random.normal(k4, (N_EXP, H, D), jnp.float32) * 0.02
        return {'x': x, 'w_g': w_g, 'c_fc': c_fc, 'c_proj': c_proj}
    _L3_ffn_all = _L3_ffn_setup()
    _L3_ffn_in = {k: v for k, v in _L3_ffn_all.items() if k in ('w_g', 'c_fc', 'c_proj')}
    del _L3_ffn_all
    return {'x': x, 'ctx_1024': ctx_1024, 'fside_BxSxS2_0': fside_BxSxS2_0, 'mask_Bx1xSxS2_ik0': mask_Bx1xSxS2_ik0, 'L0_xattn_Wq': _L0_xattn_in['Wq'], 'L0_xattn_bq': _L0_xattn_in['bq'], 'L0_xattn_Wk': _L0_xattn_in['Wk'], 'L0_xattn_bk': _L0_xattn_in['bk'], 'L0_xattn_Wv': _L0_xattn_in['Wv'], 'L0_xattn_bv': _L0_xattn_in['bv'], 'L0_xattn_Wo': _L0_xattn_in['Wo'], 'L0_xattn_bo': _L0_xattn_in['bo'], 'L0_ffn_gate_w': _L0_ffn_in['gate_w'], 'L0_ffn_gate_b': _L0_ffn_in['gate_b'], 'L0_ffn_expert_bias': _L0_ffn_in['expert_bias'], 'L0_ffn_w1': _L0_ffn_in['w1'], 'L0_ffn_b1': _L0_ffn_in['b1'], 'L0_ffn_w2': _L0_ffn_in['w2'], 'L0_ffn_b2': _L0_ffn_in['b2'], 'L1_xattn_Wq': _L1_xattn_in['Wq'], 'L1_xattn_bq': _L1_xattn_in['bq'], 'L1_xattn_Wk': _L1_xattn_in['Wk'], 'L1_xattn_bk': _L1_xattn_in['bk'], 'L1_xattn_Wv': _L1_xattn_in['Wv'], 'L1_xattn_bv': _L1_xattn_in['bv'], 'L1_xattn_Wo': _L1_xattn_in['Wo'], 'L1_xattn_bo': _L1_xattn_in['bo'], 'L1_ffn_gate_w': _L1_ffn_in['gate_w'], 'L1_ffn_gate_bias': _L1_ffn_in['gate_bias'], 'L1_ffn_w_gate': _L1_ffn_in['w_gate'], 'L1_ffn_w_up': _L1_ffn_in['w_up'], 'L1_ffn_w_down': _L1_ffn_in['w_down'], 'L1_ffn_sh_gate': _L1_ffn_in['sh_gate'], 'L1_ffn_sh_up': _L1_ffn_in['sh_up'], 'L1_ffn_sh_down': _L1_ffn_in['sh_down'], 'L2_xattn_Wq': _L2_xattn_in['Wq'], 'L2_xattn_bq': _L2_xattn_in['bq'], 'L2_xattn_Wk': _L2_xattn_in['Wk'], 'L2_xattn_bk': _L2_xattn_in['bk'], 'L2_xattn_Wv': _L2_xattn_in['Wv'], 'L2_xattn_bv': _L2_xattn_in['bv'], 'L2_xattn_Wo': _L2_xattn_in['Wo'], 'L2_xattn_bo': _L2_xattn_in['bo'], 'L2_ffn_Wr': _L2_ffn_in['Wr'], 'L2_ffn_br': _L2_ffn_in['br'], 'L2_ffn_W1': _L2_ffn_in['W1'], 'L2_ffn_b1': _L2_ffn_in['b1'], 'L2_ffn_W2': _L2_ffn_in['W2'], 'L2_ffn_b2': _L2_ffn_in['b2'], 'L3_xattn_Wq': _L3_xattn_in['Wq'], 'L3_xattn_bq': _L3_xattn_in['bq'], 'L3_xattn_Wk': _L3_xattn_in['Wk'], 'L3_xattn_bk': _L3_xattn_in['bk'], 'L3_xattn_Wv': _L3_xattn_in['Wv'], 'L3_xattn_bv': _L3_xattn_in['bv'], 'L3_xattn_beta_risk': _L3_xattn_in['beta_risk'], 'L3_xattn_beta_prio': _L3_xattn_in['beta_prio'], 'L3_xattn_beta_impl': _L3_xattn_in['beta_impl'], 'L3_ffn_w_g': _L3_ffn_in['w_g'], 'L3_ffn_c_fc': _L3_ffn_in['c_fc'], 'L3_ffn_c_proj': _L3_ffn_in['c_proj']}

def reference(x, ctx_1024, fside_BxSxS2_0, mask_Bx1xSxS2_ik0, L0_xattn_Wq, L0_xattn_bq, L0_xattn_Wk, L0_xattn_bk, L0_xattn_Wv, L0_xattn_bv, L0_xattn_Wo, L0_xattn_bo, L0_ffn_gate_w, L0_ffn_gate_b, L0_ffn_expert_bias, L0_ffn_w1, L0_ffn_b1, L0_ffn_w2, L0_ffn_b2, L1_xattn_Wq, L1_xattn_bq, L1_xattn_Wk, L1_xattn_bk, L1_xattn_Wv, L1_xattn_bv, L1_xattn_Wo, L1_xattn_bo, L1_ffn_gate_w, L1_ffn_gate_bias, L1_ffn_w_gate, L1_ffn_w_up, L1_ffn_w_down, L1_ffn_sh_gate, L1_ffn_sh_up, L1_ffn_sh_down, L2_xattn_Wq, L2_xattn_bq, L2_xattn_Wk, L2_xattn_bk, L2_xattn_Wv, L2_xattn_bv, L2_xattn_Wo, L2_xattn_bo, L2_ffn_Wr, L2_ffn_br, L2_ffn_W1, L2_ffn_b1, L2_ffn_W2, L2_ffn_b2, L3_xattn_Wq, L3_xattn_bq, L3_xattn_Wk, L3_xattn_bk, L3_xattn_Wv, L3_xattn_bv, L3_xattn_beta_risk, L3_xattn_beta_prio, L3_xattn_beta_impl, L3_ffn_w_g, L3_ffn_c_fc, L3_ffn_c_proj):
    import jax
    import jax.numpy as jnp

    def _L0_xattn_ref(query, key, value, Wq, bq, Wk, bk, Wv, bv, Wo, bo):
        import jax, jax.numpy as jnp
        import numpy as np
        H = 16
        D_MODEL = 256
        D_K = D_MODEL // H
        B, T, _ = query.shape

        def proj(x, W, b):
            return (x @ W.T + b).reshape(B, T, H, D_K).transpose(0, 2, 1, 3)
        q = proj(query, Wq, bq)
        k = proj(key, Wk, bk)
        v = proj(value, Wv, bv)
        scores = jnp.einsum('bhqd,bhkd->bhqk', q, k) / jnp.sqrt(jnp.float32(D_K))
        p_attn = jax.nn.softmax(scores, axis=-1)
        attn_out = jnp.einsum('bhqk,bhkd->bhqd', p_attn, v)
        x = attn_out.transpose(0, 2, 1, 3).reshape(B, T, D_MODEL)
        return x @ Wo.T + bo

    def _L0_ffn_ref(x, gate_w, gate_b, expert_bias, w1, b1, w2, b2):
        import jax, jax.numpy as jnp
        import numpy as np
        D_MODEL = 256
        D_FF = 1024
        NUM_EXPERTS = 8
        gate_logits = jnp.einsum('bsd,ed->bse', x, gate_w) + gate_b + expert_bias
        top_idx = jnp.argmax(gate_logits, axis=-1)
        out = jnp.zeros_like(x)
        for e in range(NUM_EXPERTS):
            mask = (top_idx == e)[..., None].astype(x.dtype)
            h = jax.nn.relu(jnp.einsum('bsd,df->bsf', x, w1[e]) + b1[e])
            y = jnp.einsum('bsf,fd->bsd', h, w2[e]) + b2[e]
            out = out + mask * y
        return out

    def _L1_xattn_ref(query, key, value, Wq, bq, Wk, bk, Wv, bv, Wo, bo):
        import jax, jax.numpy as jnp
        import numpy as np
        DIM = 256
        N_HEADS = 16
        HEAD_DIM = DIM // N_HEADS
        GAMMA = 10.0

        def larope_cos_sin(seq_len, gamma, head_dim):
            inv_freq = 1.0 / 10000.0 ** (jnp.arange(0, head_dim, 2, dtype=jnp.float32) / head_dim)
            t = jnp.arange(seq_len, dtype=jnp.float32)
            freqs = jnp.outer(gamma * (t / seq_len), inv_freq)
            emb = jnp.concatenate([freqs, freqs], axis=-1)
            return (jnp.cos(emb), jnp.sin(emb))

        def apply_rope(x, cos, sin):
            d = x.shape[-1] // 2
            x1, x2 = (x[..., :d], x[..., d:])
            c = cos[None, None, :, :d]
            s = sin[None, None, :, :d]
            return jnp.concatenate([x1 * c - x2 * s, x1 * s + x2 * c], axis=-1)
        B, Lq, _ = query.shape
        Lk = key.shape[1]
        scale = HEAD_DIM ** (-0.5)

        def proj(x, W, b, L):
            y = x @ W.T + b
            return y.reshape(B, L, N_HEADS, HEAD_DIM).transpose(0, 2, 1, 3)
        q = proj(query, Wq, bq, Lq)
        k = proj(key, Wk, bk, Lk)
        v = proj(value, Wv, bv, Lk)
        q_cos, q_sin = larope_cos_sin(Lq, GAMMA, HEAD_DIM)
        k_cos, k_sin = larope_cos_sin(Lk, GAMMA, HEAD_DIM)
        q = apply_rope(q, q_cos, q_sin)
        k = apply_rope(k, k_cos, k_sin)
        scores = jnp.einsum('bhqd,bhkd->bhqk', q, k) * scale
        attn = jax.nn.softmax(scores, axis=-1)
        out = jnp.einsum('bhqk,bhkd->bhqd', attn, v)
        out = out.transpose(0, 2, 1, 3).reshape(B, Lq, DIM)
        return out @ Wo.T + bo

    def _L1_ffn_ref(hidden_states, gate_w, gate_bias, w_gate, w_up, w_down, sh_gate, sh_up, sh_down):
        import jax, jax.numpy as jnp
        import numpy as np
        E = 32
        H = 256
        I = 128
        G = 8
        TKG = 4
        TOPK = 8
        NSH = 2
        SCALE = 2.5
        B, S, Hd = hidden_states.shape
        h = hidden_states.reshape(-1, Hd)
        logits = h.astype(jnp.float32) @ gate_w.T
        scores = jax.nn.sigmoid(logits)
        sc = scores + gate_bias
        grp = sc.reshape(-1, G, E // G)
        group_scores = jax.lax.top_k(grp, 2)[0].sum(-1)
        gidx = jax.lax.top_k(group_scores, TKG)[1]
        gmask = jnp.sum(jax.nn.one_hot(gidx, G, dtype=sc.dtype), axis=1)
        smask = jnp.repeat(gmask, E // G, axis=1)
        masked = jnp.where(smask > 0, sc, jnp.zeros_like(sc))
        tki = jax.lax.top_k(masked, TOPK)[1]
        tkw = jnp.take_along_axis(scores, tki, axis=1)
        tkw = tkw / (tkw.sum(-1, keepdims=True) + 1e-20)
        tkw = tkw * SCALE
        combine = (jax.nn.one_hot(tki, E, dtype=tkw.dtype) * tkw[..., None]).sum(1)
        g = jax.nn.silu(jnp.einsum('th,eih->tei', h, w_gate))
        u = jnp.einsum('th,eih->tei', h, w_up)
        routed = jnp.einsum('tei,ehi->th', g * u * combine[:, :, None], w_down)
        sg = jax.nn.silu(h @ sh_gate.T)
        shared = sg * (h @ sh_up.T) @ sh_down.T
        return (routed + shared).reshape(B, S, Hd)

    def _L2_xattn_ref(query, key, value, mask, Wq, bq, Wk, bk, Wv, bv, Wo, bo):
        import jax, jax.numpy as jnp
        import numpy as np
        import math
        B, S, D, H = (2, 512, 256, 16)
        DK = D // H

        def _split_heads(x):
            b, s, _ = x.shape
            return x.reshape(b, s, H, DK).transpose(0, 2, 1, 3)
        Q = _split_heads(query @ Wq.T + bq)
        K = _split_heads(key @ Wk.T + bk)
        V = _split_heads(value @ Wv.T + bv)
        scores = jnp.einsum('bhqd,bhkd->bhqk', Q, K) / math.sqrt(DK)
        scores = jnp.where(mask == 0, jnp.float32(-1000000000.0), scores)
        attn = jax.nn.softmax(scores, axis=-1)
        out = jnp.einsum('bhqk,bhkd->bhqd', attn, V)
        out = out.transpose(0, 2, 1, 3).reshape(query.shape[0], query.shape[1], D)
        return out @ Wo.T + bo

    def _L2_ffn_ref(x, Wr, br, W1, b1, W2, b2):
        import jax, jax.numpy as jnp
        import numpy as np
        E = 8
        K = 2
        CAPACITY_FACTOR = 1.25
        B, T, C = x.shape
        cap = max(1, int(T / E * CAPACITY_FACTOR))
        probs = jax.nn.softmax(x @ Wr + br, axis=-1)
        topk_p, topk_e = jax.lax.top_k(probs, K)
        e_flat = topk_e.reshape(B, T * K)
        p_flat = topk_p.reshape(B, T * K)
        oh = jax.nn.one_hot(e_flat, E, dtype=jnp.int32)
        pos_all = jnp.cumsum(oh, axis=1) - oh
        pos = jnp.take_along_axis(pos_all, e_flat[:, :, None], axis=2)[:, :, 0]
        keep = pos < cap
        b_idx = jnp.arange(B)[:, None]
        flat_idx = (e_flat * B + b_idx) * cap + jnp.minimum(pos, cap - 1)
        x_rep = jnp.broadcast_to(x[:, :, None, :], (B, T, K, C)).reshape(B, T * K, C)
        buf = jnp.zeros((E * B * cap, C), x.dtype).at[flat_idx.reshape(-1)].add((x_rep * keep[:, :, None].astype(x.dtype)).reshape(-1, C))
        buf = buf.reshape(E, B * cap, C)
        h = jax.nn.relu(jnp.einsum('enc,ech->enh', buf, W1) + b1[:, None, :])
        y = jnp.einsum('enh,ehc->enc', h, W2) + b2[:, None, :]
        y_tok = y.reshape(E * B * cap, C)[flat_idx.reshape(-1)].reshape(B, T * K, C)
        y_tok = y_tok * (p_flat * keep.astype(x.dtype))[:, :, None]
        return y_tok.reshape(B, T, K, C).sum(axis=2)

    def _L3_xattn_ref(q_in, k_in, v_in, phi_risk, phi_prio, phi_impl, Wq, bq, Wk, bk, Wv, bv, beta_risk, beta_prio, beta_impl):
        import jax, jax.numpy as jnp
        import numpy as np
        D = 256
        d = q_in.shape[-1]
        scale = jnp.asarray(d, q_in.dtype) ** (-0.5)
        Q = q_in @ Wq.T + bq
        K = k_in @ Wk.T + bk
        V = v_in @ Wv.T + bv
        att = jnp.einsum('bsd,btd->bst', Q, K) * scale
        att = att + beta_risk * phi_risk + beta_prio * phi_prio - beta_impl * phi_impl
        w = jax.nn.softmax(att, axis=-1)
        return jnp.einsum('bst,btd->bsd', w, V)

    def _L3_ffn_ref(x, w_g, c_fc, c_proj):
        import jax, jax.numpy as jnp
        import numpy as np
        N_EXP = 8
        TOP_K = 2
        CAP_FACTOR = 1.25
        NEG_INF = -1000000000.0

        def _moe_forward(x, w_g, c_fc, c_proj):
            B, T, D = x.shape
            N = B * T
            xf = x.reshape(N, D)
            logits = xf @ w_g
            topv, topi = jax.lax.top_k(logits, TOP_K)
            full = jnp.full_like(logits, NEG_INF)
            full = full.at[jnp.arange(N)[:, None], topi].set(topv)
            probs = jax.nn.softmax(full, axis=-1)
            capacity = int(TOP_K * CAP_FACTOR * N / N_EXP)
            capacity += capacity % 2
            mask = jax.nn.one_hot(jnp.swapaxes(topi, 0, 1), N_EXP, dtype=jnp.int32)
            rank = jnp.cumsum(mask.reshape(TOP_K * N, N_EXP), axis=0).reshape(TOP_K, N, N_EXP) - 1
            mask = mask * (rank < capacity)
            rank_sel = jnp.sum(mask * rank, axis=-1)
            wts = jnp.sum(mask * probs[None], axis=-1)
            cb = jnp.zeros((N, N_EXP, capacity), x.dtype)
            tok = jnp.arange(N)
            for k in range(TOP_K):
                cb = cb.at[tok, topi[:, k], rank_sel[k]].add(wts[k])
            sec_mask = (cb != 0).astype(x.dtype)
            exp_batches = jnp.einsum('nec,nd->ecd', sec_mask, xf)
            h = jax.nn.gelu(jnp.einsum('ecd,edh->ech', exp_batches, c_fc), approximate=False)
            exp_out = jnp.einsum('ech,ehd->ecd', h, c_proj)
            out = jnp.einsum('nec,ecd->nd', cb, exp_out)
            return out.reshape(B, T, D)
        return _moe_forward(x, w_g, c_fc, c_proj)
    x = x + _L0_xattn_ref(_layernorm(x, axis=-1), ctx_1024, ctx_1024, L0_xattn_Wq, L0_xattn_bq, L0_xattn_Wk, L0_xattn_bk, L0_xattn_Wv, L0_xattn_bv, L0_xattn_Wo, L0_xattn_bo)
    x = x + _L0_ffn_ref(_layernorm(x, axis=-1), L0_ffn_gate_w, L0_ffn_gate_b, L0_ffn_expert_bias, L0_ffn_w1, L0_ffn_b1, L0_ffn_w2, L0_ffn_b2)
    x = x + _L1_xattn_ref(_layernorm(x, axis=-1), ctx_1024, ctx_1024, L1_xattn_Wq, L1_xattn_bq, L1_xattn_Wk, L1_xattn_bk, L1_xattn_Wv, L1_xattn_bv, L1_xattn_Wo, L1_xattn_bo)
    x = x + _L1_ffn_ref(_layernorm(x, axis=-1), L1_ffn_gate_w, L1_ffn_gate_bias, L1_ffn_w_gate, L1_ffn_w_up, L1_ffn_w_down, L1_ffn_sh_gate, L1_ffn_sh_up, L1_ffn_sh_down)
    x = x + _L2_xattn_ref(_layernorm(x, axis=-1), ctx_1024, ctx_1024, mask_Bx1xSxS2_ik0, L2_xattn_Wq, L2_xattn_bq, L2_xattn_Wk, L2_xattn_bk, L2_xattn_Wv, L2_xattn_bv, L2_xattn_Wo, L2_xattn_bo)
    x = x + _L2_ffn_ref(_layernorm(x, axis=-1), L2_ffn_Wr, L2_ffn_br, L2_ffn_W1, L2_ffn_b1, L2_ffn_W2, L2_ffn_b2)
    x = x + _L3_xattn_ref(_layernorm(x, axis=-1), ctx_1024, ctx_1024, fside_BxSxS2_0, fside_BxSxS2_0, fside_BxSxS2_0, L3_xattn_Wq, L3_xattn_bq, L3_xattn_Wk, L3_xattn_bk, L3_xattn_Wv, L3_xattn_bv, L3_xattn_beta_risk, L3_xattn_beta_prio, L3_xattn_beta_impl)
    x = x + _L3_ffn_ref(_layernorm(x, axis=-1), L3_ffn_w_g, L3_ffn_c_fc, L3_ffn_c_proj)
    return x

_drawn_inputs = setup_inputs


def setup_inputs(seed=0):
    import zlib

    import numpy as np

    out = dict(_drawn_inputs(seed))
    spreads = {'L0_xattn_bq': (0.0, 0.274),
     'L0_xattn_bk': (0.0, 2.0),
     'L0_xattn_bv': (0.0, 0.1),
     'L0_xattn_bo': (0.0, 0.1),
     'L0_ffn_expert_bias': (0.0, 0.1),
     'L1_xattn_bq': (0.0, 0.721),
     'L1_xattn_bk': (0.0, 0.8),
     'L1_xattn_bv': (0.0, 0.1),
     'L1_xattn_bo': (0.0, 0.1),
     'L2_xattn_bq': (0.0, 1.66),
     'L2_xattn_bk': (0.0, 2.0),
     'L2_xattn_bv': (0.0, 0.336),
     'L2_xattn_bo': (0.0, 0.442),
     'L2_ffn_br': (0.0, 0.737),
     'L2_ffn_b1': (0.0, 0.8),
     'L2_ffn_b2': (0.0, 0.8)}
    factors = {'fside_BxSxS2_0': 64.0,
     'L0_ffn_b1': 6.682,
     'L0_ffn_b2': 5.375,
     'L1_ffn_gate_w': 8.0,
     'L1_ffn_gate_bias': 8.0,
     'L1_ffn_w_gate': 8.0,
     'L1_ffn_w_up': 8.0,
     'L1_ffn_w_down': 8.0,
     'L1_ffn_sh_gate': 6.066,
     'L1_ffn_sh_up': 5.917,
     'L1_ffn_sh_down': 5.981,
     'L2_ffn_Wr': 4.443,
     'L2_ffn_W1': 5.999,
     'L2_ffn_W2': 4.894,
     'L3_xattn_bq': 64.0,
     'L3_xattn_bk': 64.0,
     'L3_xattn_bv': 50.795,
     'L3_ffn_w_g': 7.634,
     'L3_ffn_c_fc': 6.772,
     'L3_ffn_c_proj': 6.624}
    for name, (base, spread) in spreads.items():
        noise = np.random.default_rng([zlib.crc32(name.encode()), seed]).standard_normal(out[name].shape)
        drawn = base * np.exp(spread * noise) if base else spread * noise
        out[name] = jnp.asarray(drawn.astype(out[name].dtype))
    for name, factor in factors.items():
        out[name] = (out[name] * factor).astype(out[name].dtype)
    return out
```

```python
from contextlib import ExitStack

import numpy as np

import concourse.bass as bass
from concourse import mybir
from concourse.alu_op_type import AluOpType as ALU

ACT = mybir.ActivationFunctionType
F32 = mybir.dt.float32
BF16 = mybir.dt.bfloat16
I32 = mybir.dt.int32
U32 = mybir.dt.uint32
AX = mybir.AxisListType

P = 128
B, S, D = 4, 512, 256
N = B * S
NT = N // P
KD = D // P
TPB = S // P
H, DH = 16, 16
GH = 4
NG = H // GH
HS = 32
NPROD = 6
SR = NPROD * DH
MR = 3
EPS = 1e-5
NEG = -float(2 ** 100)


class Phase:

    def __init__(self, nc, ctx, name):
        self.nc, self.ctx, self.name = nc, ctx, name

    def sb(self, name, shape, dt=F32):
        return self.ctx.enter_context(self.nc.sbuf_tensor(f"{self.name}_{name}", shape, dt))

    def ps(self, name, shape, dt=F32):
        return self.ctx.enter_context(self.nc.psum_tensor(f"{self.name}_{name}", shape, dt))

    def sem(self, name):
        return self.ctx.enter_context(self.nc.semaphore(f"{self.name}_{name}"))


def clear_semaphores(nc):
    free = sorted(nc.free_semaphores)
    runs = [[free[0], free[0] + 1]]
    for n in free[1:]:
        if n == runs[-1][1]:
            runs[-1][1] = n + 1
        else:
            runs.append([n, n + 1])
    for a, b in runs:
        nc.gpsimd.sem_clear(range(a, b))
    nc.all_engine_barrier()


class Steps:

    def __init__(self, eng, sem):
        self.eng, self.sem, self.n = eng, sem, 0

    def after(self, ins):
        ins.then_inc(self.sem, 1)
        self.n += 1
        self.eng.wait_ge(self.sem, self.n)



def setup_phase(nc, k, io):
    with ExitStack() as ctx:
        ph = Phase(nc, ctx, "setup")
        ctok = ph.sb("ctok", [P, NT, D])
        zero = ph.sb("zero", [P, 4 * D])
        before = ph.sb("before", [P, P])
        TP = ph.ps("tp", [P, 4, KD, 2 * P])
        x_loaded, ctx_loaded, consts = ph.sem("x_loaded"), ph.sem("ctx_loaded"), ph.sem("consts")
        turned, taken, zeroed, cleared = ph.sem("turned"), ph.sem("taken"), ph.sem("zeroed"), ph.sem("cleared")
        with nc.Block() as block:

            @block.sync
            def _(sp):
                sp.dma_start(k.identf[:], io["c_identf"]).then_inc(consts, 16)
                sp.dma_start(ctok[:], io["ctx_1024"].rearrange("b (t p) d -> p (b t) d", p=P)).then_inc(ctx_loaded, 16)
                sp.dma_start(k.x[:], io["x"].rearrange("b (t p) d -> p (b t) d", p=P)).then_inc(x_loaded, 16)
                sp.dma_start(before[:], io["c_before"]).then_inc(consts, 16)
                sp.dma_start(k.iota[:], io["c_iota"]).then_inc(consts, 16)
                sp.wait_ge(zeroed, 1)
                rows = k.xg.shape[0] // P
                src = zero[:].rearrange("p (r d) -> p r d", d=D)
                dst = k.xg.rearrange("(r p) d -> p r d", p=P)
                for r in range(0, rows, 4):
                    sp.dma_start(dst[:, r:r + 4, :], src).then_inc(cleared, 16)
                sp.wait_ge(consts, 16 * 3)
                sp.wait_ge(x_loaded, 16)
                sp.wait_ge(cleared, 16 * (rows // 4))

            @block.gpsimd
            def _(pool):
                nc.gpsimd.memset(zero[:], 0.0).then_inc(zeroed, 1)
                nc.gpsimd.memset(k.half[:], -0.5)
                nc.gpsimd.memset(k.onesb[:], 1.0)

            @block.tensor
            def _(pe):
                pe.wait_ge(consts, 16 * 3)
                pe.wait_ge(ctx_loaded, 16)
                for p in range(NT // 2):
                    if p >= 4:
                        pe.wait_ge(taken, p - 3)
                    for i in range(2):
                        for c in range(KD):
                            mm = nc.tensor.transpose(TP[:, p % 4, c, i * P:(i + 1) * P],
                                                     ctok[:, 2 * p + i, c * P:(c + 1) * P], k.identf[:])
                    mm.then_inc(turned, 1)

            @block.vector
            def _(dve):
                dve.wait_ge(consts, 16 * 3)
                nc.vector.tensor_copy(k.identb[:], k.identf[:])
                nc.vector.tensor_copy(k.before[:], before[:])

            @block.scalar
            def _(act):
                for p in range(NT // 2):
                    act.wait_ge(turned, p + 1)
                    nc.scalar.copy(k.ctxT[:, :, p * 2 * P:(p + 1) * 2 * P], TP[:, p % 4]).then_inc(taken, 1)



def layernorm_phase(nc, k, name):
    with ExitStack() as ctx:
        ph = Phase(nc, ctx, name)
        st = ph.sb("st", [P, NT, 6])
        mean, diff, var, rstd = (ph.sb(n, [P, NT]) for n in ("mean", "diff", "var", "rstd"))
        TP = ph.ps("tp", [P, 4, KD, 2 * P])
        dve_step, var_ready, rstd_ready = ph.sem("dve_step"), ph.sem("var_ready"), ph.sem("rstd_ready")
        xn_ready, turned, taken = ph.sem("xn_ready"), ph.sem("turned"), ph.sem("taken")
        with nc.Block() as block:

            @block.vector
            def _(dve):
                step = Steps(dve, dve_step)
                for t in range(NT):
                    ins = nc.vector.bn_stats(st[:, t, :], k.x[:, t, :])
                step.after(ins)
                me, se, mo, so = st[:, :, 1], st[:, :, 2], st[:, :, 4], st[:, :, 5]
                nc.vector.tensor_tensor(mean[:], me, mo, ALU.add)
                nc.vector.tensor_tensor(diff[:], me, mo, ALU.subtract)
                step.after(nc.vector.tensor_tensor(var[:], se, so, ALU.add))
                nc.vector.tensor_scalar(mean[:], mean[:], 0.5, None, ALU.mult)
                nc.vector.tensor_scalar(var[:], var[:], 1.0 / D, EPS, ALU.mult, ALU.add)
                step.after(nc.vector.tensor_tensor(diff[:], diff[:], diff[:], ALU.mult))
                nc.vector.scalar_tensor_tensor(out=var[:], in0=diff[:], scalar=0.25, in1=var[:],
                                               op0=ALU.mult, op1=ALU.add).then_inc(var_ready, 1)
                dve.wait_ge(rstd_ready, 1)
                for t in range(NT):
                    nc.vector.tensor_scalar(k.xn[:, t, :], k.x[:, t, :], mean[:, t:t + 1], rstd[:, t:t + 1],
                                            ALU.subtract, ALU.mult).then_inc(xn_ready, 1)

            @block.gpsimd
            def _(pool):
                pool.wait_ge(var_ready, 1)
                nc.gpsimd.tensor_tensor(rstd[:], var[:], k.half[:], ALU.pow).then_inc(rstd_ready, 1)

            @block.tensor
            def _(pe):
                for p in range(NT // 2):
                    pe.wait_ge(xn_ready, 2 * p + 2)
                    if p >= 4:
                        pe.wait_ge(taken, p - 3)
                    for i in range(2):
                        for c in range(KD):
                            mm = nc.tensor.transpose(TP[:, p % 4, c, i * P:(i + 1) * P],
                                                     k.xn[:, 2 * p + i, c * P:(c + 1) * P], k.identf[:])
                    mm.then_inc(turned, 1)

            @block.scalar
            def _(act):
                for p in range(NT // 2):
                    act.wait_ge(turned, p + 1)
                    nc.scalar.copy(k.xnT[:, :, p * 2 * P:(p + 1) * 2 * P], TP[:, p % 4]).then_inc(taken, 1)



Q_PARTS = (0, 1, 2, 0, 0, 1)
K_PARTS = (0, 0, 0, 1, 2, 1)


def heads_project_phase(nc, k, io, layer, rope):
    pre = f"L{layer}_xattn_"
    with ExitStack() as ctx:
        ph = Phase(nc, ctx, f"proj{layer}")
        names = ["Wq", "Wk", "Wv"] + (["Wq_turn", "Wk_turn"] if rope else [])
        W = {n: ph.sb(n, [P, KD, D]) for n in names}
        biases = ["bq", "bk"] + (["bq_turn", "bk_turn"] if rope else [])
        bias = {n: ph.sb(n, [P, KD]) for n in biases}
        tabs = {n: ph.sb(n, [P, S]) for n in (("cosq", "sinq", "cosk", "sink") if rope else ())}
        full = ph.sb("full", [P, 2, S])
        other = ph.sb("other", [P, 2, S])
        rest = ph.sb("rest", [P, 2, S])
        parts = ph.sb("parts", [P, 2, 3, N], BF16)
        QK = ph.ps("qk", [P, 2, S])
        QK2 = ph.ps("qk2", [P, 2, S])
        VP = ph.ps("vp", [P, 2, 2, D])
        w_loaded = ph.sem("w_loaded")
        qk_ready, qk_taken, v_ready, v_taken = (ph.sem(n) for n in ("qk_ready", "qk_taken", "v_ready", "v_taken"))
        high_ready, rest_ready, mid_ready, low_ready = (ph.sem(n) for n in ("high", "rest", "mid", "low"))
        dve_step = ph.sem("dve_step")
        stored = [ph.sem(f"stored{i}") for i in range(2)]
        units = [("q", m) for m in range(KD)] + [("k", m) for m in range(KD)]
        NC = N // S
        loads = 3 + 2 + (2 + 2 + 4 if rope else 0)
        with nc.Block() as block:

            @block.sync
            def _(sp):
                for n in names:
                    sp.dma_start(W[n][:], io[pre + n].rearrange("(c p) o -> p c o", p=P)).then_inc(w_loaded, 16)
                for n in biases:
                    sp.dma_start(bias[n][:], io[pre + n]).then_inc(w_loaded, 16)
                for n, t in tabs.items():
                    sp.dma_start(t[:], io["c_" + n]).then_inc(w_loaded, 16)
                for u, (what, m) in enumerate(units):
                    sp.wait_ge(low_ready, NC * (u + 1))
                    dst, order = (k.qstack, Q_PARTS) if what == "q" else (k.kstack, K_PARTS)
                    for r, part in enumerate(order):
                        sp.dma_start(dst[m * 8:(m + 1) * 8, r * DH:(r + 1) * DH, :],
                                     parts[:, u % 2, part, :]).then_inc(stored[u % 2], 16)
                for i in range(2):
                    sp.wait_ge(stored[i], 16 * NPROD * 2)

            @block.tensor
            def _(pe):
                pe.wait_ge(w_loaded, 16 * loads)
                s = 0
                for what, m in units:
                    src = k.xnT if what == "q" else k.ctxT
                    for c in range(NC):
                        if s >= 2:
                            pe.wait_ge(qk_taken, s - 1)
                        for n, ps in (("W" + what, QK), ("W" + what + "_turn", QK2))[:2 if rope else 1]:
                            for kd in range(KD):
                                mm = nc.tensor.matmul(ps[:, s % 2, :], W[n][:, kd, m * P:(m + 1) * P],
                                                      src[:, kd, c * S:(c + 1) * S],
                                                      start=(kd == 0), stop=(kd == KD - 1))
                        mm.then_inc(qk_ready, 1)
                        s += 1
                for t in range(NT // 2):
                    if t >= 2:
                        pe.wait_ge(v_taken, t - 1)
                    for i in range(2):
                        tok = (2 * t + i) * P
                        for kd in range(KD):
                            mm = nc.tensor.matmul(VP[:, t % 2, i, :], k.ctxT[:, kd, tok:tok + P], W["Wv"][:, kd, :],
                                                  start=(kd == 0), stop=(kd == KD - 1))
                    mm.then_inc(v_ready, 1)

            @block.vector
            def _(dve):
                step = Steps(dve, dve_step)
                dve.wait_ge(w_loaded, 16 * loads)
                s = 0
                for what, m in units:
                    for c in range(NC):
                        dve.wait_ge(qk_ready, s + 1)
                        if s >= 2:
                            dve.wait_ge(rest_ready, s - 1)
                        f = full[:, s % 2, :]
                        if rope:
                            nc.vector.scalar_tensor_tensor(out=f, in0=QK[:, s % 2, :], scalar=bias["b" + what][:, m:m + 1],
                                                           in1=tabs["cos" + what][:], op0=ALU.add, op1=ALU.mult)
                            step.after(nc.vector.scalar_tensor_tensor(
                                out=other[:, s % 2, :], in0=QK2[:, s % 2, :], scalar=bias["b" + what + "_turn"][:, m:m + 1],
                                in1=tabs["sin" + what][:], op0=ALU.add, op1=ALU.mult))
                            nc.vector.tensor_tensor(f, f, other[:, s % 2, :], ALU.add).then_inc(qk_taken, 1)
                        else:
                            scale = DH ** -0.5 if what == "q" else 1.0
                            nc.vector.tensor_scalar(f, QK[:, s % 2, :], bias["b" + what][:, m:m + 1], scale,
                                                    ALU.add, ALU.mult).then_inc(qk_taken, 1)
                        s += 1

            @block.scalar
            def _(act):
                s = 0
                for u in range(len(units)):
                    if u >= 2:
                        act.wait_ge(stored[u % 2], 16 * NPROD)
                    for c in range(NC):
                        act.wait_ge(qk_taken, s + 1)
                        nc.scalar.copy(parts[:, u % 2, 0, c * S:(c + 1) * S], full[:, s % 2, :]).then_inc(high_ready, 1)
                        act.wait_ge(rest_ready, s + 1)
                        nc.scalar.copy(parts[:, u % 2, 1, c * S:(c + 1) * S], rest[:, s % 2, :]).then_inc(mid_ready, 1)
                        s += 1
                for t in range(NT // 2):
                    act.wait_ge(v_ready, t + 1)
                    nc.scalar.copy(k.V[:, 2 * t:2 * t + 2, :], VP[:, t % 2]).then_inc(v_taken, 1)

            @block.gpsimd
            def _(pool):
                s = 0
                for u in range(len(units)):
                    for c in range(NC):
                        pool.wait_ge(high_ready, s + 1)
                        if s >= 2:
                            pool.wait_ge(low_ready, s - 1)
                        nc.gpsimd.tensor_tensor(rest[:, s % 2, :], full[:, s % 2, :], parts[:, u % 2, 0, c * S:(c + 1) * S],
                                                ALU.subtract).then_inc(rest_ready, 1)
                        pool.wait_ge(mid_ready, s + 1)
                        nc.gpsimd.tensor_tensor(parts[:, u % 2, 2, c * S:(c + 1) * S], rest[:, s % 2, :],
                                                parts[:, u % 2, 1, c * S:(c + 1) * S], ALU.subtract).then_inc(low_ready, 1)
                        s += 1


def mask_phase(nc, k, io):
    with ExitStack() as ctx:
        ph = Phase(nc, ctx, "mask")
        raw = ph.sb("raw", [P, 2, TPB, S], I32)
        TP = ph.ps("tp", [P, 4, 2 * S], BF16)
        loaded = [ph.sem(f"loaded{i}") for i in range(2)]
        pen_ready, turned, taken = ph.sem("pen_ready"), ph.sem("turned"), ph.sem("taken")
        with nc.Block() as block:

            @block.sync
            def _(sp):
                for b in range(B):
                    if b >= 2:
                        sp.wait_ge(pen_ready, b - 1)
                    sp.dma_start(raw[:, b % 2], io["mask_Bx1xSxS2_ik0"][b, 0].rearrange("(t p) s -> p t s", p=P)
                                 ).then_inc(loaded[b % 2], 16)

            @block.vector
            def _(dve):
                for b in range(B):
                    dve.wait_ge(loaded[b % 2], 16 * (b // 2 + 1))
                    nc.vector.tensor_scalar(k.pen[:, b * TPB:(b + 1) * TPB, :], raw[:, b % 2], 0.0, NEG,
                                            ALU.is_equal, ALU.mult).then_inc(pen_ready, 1)

            @block.tensor
            def _(pe):
                for b in range(B):
                    pe.wait_ge(pen_ready, b + 1)
                    for kt in range(TPB):
                        i = b * TPB + kt
                        if i >= 4:
                            pe.wait_ge(taken, i - 3)
                        for qt in range(TPB):
                            mm = nc.tensor.transpose(TP[:, i % 4, qt * P:(qt + 1) * P],
                                                     k.pen[:, b * TPB + qt, kt * P:(kt + 1) * P], k.identb[:])
                        mm.then_inc(turned, 1)

            @block.scalar
            def _(act):
                for i in range(NT):
                    act.wait_ge(turned, i + 1)
                    nc.scalar.copy(k.penT[:, i, :], TP[:, i % 4, 0:S]).then_inc(taken, 1)


def heads_attend_phase(nc, k, layer, masked):
    with ExitStack() as ctx:
        ph = Phase(nc, ctx, f"att{layer}")
        Qs = ph.sb("Qs", [P, NG, GH, S], BF16)
        Ks = ph.sb("Ks", [P, NG, GH, S], BF16)
        Vg = ph.sb("Vg", [P, NG, TPB, GH, HS])
        probs = ph.sb("probs", [P, 2, GH, S])
        M = ph.sb("M", [P, 2, GH * TPB])
        rest = ph.sb("rest", [P, GH * TPB])
        mparts = ph.sb("mparts", [P, 2, P], BF16)
        mT = ph.sb("mT", [MR * GH * TPB, 2, P], BF16)
        SA = ph.ps("SA", [P, 2, S])
        ST = ph.ps("ST", [P, 2, 2, S])
        O = ph.ps("O", [P, S])
        MT = ph.ps("MT", [P, 2 * S], BF16)
        qk_loaded = [ph.sem(f"qk_loaded{g}") for g in range(NG)]
        m_loaded = [ph.sem(f"m_loaded{g}") for g in range(NG)]
        v_copied = [ph.sem(f"v_copied{g}") for g in range(NG)]
        set_up = ph.sem("set_up")
        sa_ready, sa_free, split = ph.sem("sa_ready"), ph.sem("sa_free"), ph.sem("split")
        m_turned, m_copied = ph.sem("m_turned"), ph.sem("m_copied")
        st_ready, exp_done, pv_done, o_copied = (ph.sem(n) for n in ("st_ready", "exp_done", "pv_done", "o_copied"))
        SPLIT = 4
        UA = GH * TPB

        def later(b, g, d):
            return b + (g + d) // NG, (g + d) % NG

        with nc.Block() as block:

            @block.sync
            def _(sp):
                def load_stacks(b, g):
                    sp.dma_start(Qs[0:SR, g], k.qstack[g * GH:(g + 1) * GH, :, bass.ds(b * S, S)].rearrange("h r t -> r h t")
                                 ).then_inc(qk_loaded[g], 16)
                    sp.dma_start(Ks[0:SR, g], k.kstack[g * GH:(g + 1) * GH, :, bass.ds(b * S, S)].rearrange("h r t -> r h t")
                                 ).then_inc(qk_loaded[g], 16)

                def place_maxima(b, g):
                    sp.wait_ge(m_copied, b * NG + g + 2)
                    sp.dma_start(Qs[SR:SR + MR, g], mT[:, g % 2, :]).then_inc(m_loaded[g], 16)

                def group(b, g, last):
                    if not (last and g == NG - 1):
                        place_maxima(*later(b, g, 1))
                    if not last:
                        sp.wait_ge(st_ready, b * (8 * NG) + 8 * (g + 1))
                        load_stacks(b + 1, g)

                for g in range(NG):
                    load_stacks(0, g)
                place_maxima(0, 0)
                with sp.Fori(0, B - 1) as b:
                    for g in range(NG):
                        group(b, g, False)
                for g in range(NG):
                    group(B - 1, g, True)

            @block.tensor
            def _(pe):
                def maxima_scores(b, g, j, qt):
                    if j == 0 and qt == 0:
                        pe.wait_ge(qk_loaded[g], 32 * b + 32)
                    pe.wait_ge(sa_free, b * (NG * UA) + g * UA + j * TPB + qt + 1)
                    mm = nc.tensor.matmul(SA[:, qt % 2, :], Qs[0:SR, g, j, qt * P:(qt + 1) * P], Ks[0:SR, g, j, :],
                                          start=True, stop=not masked)
                    if masked:
                        mm = nc.tensor.matmul(SA[:, qt % 2, :], k.identb[:], k.pen[:, b * TPB + qt, :],
                                              start=False, stop=True)
                    mm.then_inc(sa_ready, 1)

                def turn_maxima(b, g):
                    pe.wait_ge(split, b * (NG * SPLIT) + SPLIT * (g + 1))
                    pe.wait_ge(m_copied, b * NG + g + 1)
                    nc.tensor.transpose(MT[:, 0:P], mparts[:, g % 2, :], k.identb[:]
                                        ).then_inc(m_turned, 1)

                def turned_scores(b, g, kt, pair):
                    if kt == 0 and pair == 0:
                        pe.wait_ge(m_loaded[g], 16 * b + 16)
                    pe.wait_ge(exp_done, b * (8 * NG) + 8 * g + 2 * kt + pair + 1)
                    for i in range(2):
                        j = 2 * pair + i
                        mm = nc.tensor.matmul(ST[:, pair, i, :], Ks[0:SR + MR, g, j, kt * P:(kt + 1) * P],
                                              Qs[0:SR + MR, g, j, :], start=True, stop=not masked)
                        if masked:
                            mm = nc.tensor.matmul(ST[:, pair, i, :], k.identb[:], k.penT[:, b * TPB + kt, :],
                                                  start=False, stop=True)
                    mm.then_inc(st_ready, 1)

                def weigh_values(b, g, kt, half):
                    if kt == 0 and half == 0:
                        pe.wait_ge(o_copied, b * NG + g + 1)
                        pe.wait_ge(v_copied[g], b + 1)
                    pe.wait_ge(exp_done, b * (8 * NG) + 8 * g + 2 * kt + half + 3)
                    for j in (2 * half, 2 * half + 1):
                        mm = nc.tensor.matmul(O[j * HS:(j + 1) * HS, :], Vg[:, g, kt, j, :], probs[:, kt % 2, j, :],
                                              start=(kt == 0), stop=(kt == TPB - 1))
                    if half:
                        mm.then_inc(pv_done, 1)

                def group(b, g, last):
                    for kt in range(TPB):
                        ahead = None if last and g >= NG - 2 else later(b, g, 2)
                        for i in range(2):
                            if ahead:
                                maxima_scores(*ahead, kt, i)
                            if kt < TPB - 1:
                                turned_scores(b, g, kt + 1, i)
                            elif not (last and g == NG - 1):
                                turned_scores(*later(b, g, 1), 0, i)
                        if ahead:
                            maxima_scores(*ahead, kt, 2)
                        weigh_values(b, g, kt, 0)
                        if ahead:
                            maxima_scores(*ahead, kt, 3)
                        weigh_values(b, g, kt, 1)
                        if kt == 0 and not (last and g == NG - 1):
                            turn_maxima(*later(b, g, 1))

                pe.sem_inc(pv_done, 2)
                pe.wait_ge(set_up, 2)
                for j in range(GH):
                    for qt in range(TPB):
                        maxima_scores(0, 0, j, qt)
                for j in range(GH):
                    for qt in range(TPB):
                        maxima_scores(0, 1, j, qt)
                    if j == 0:
                        turn_maxima(0, 0)
                for pair in range(2):
                    turned_scores(0, 0, 0, pair)
                with pe.Fori(0, B - 1) as b:
                    for g in range(NG):
                        group(b, g, False)
                for g in range(NG):
                    group(B - 1, g, True)

            @block.vector
            def _(dve):
                def maxima(b, g, j):
                    for qt in range(TPB):
                        dve.wait_ge(sa_ready, b * (NG * UA) + g * UA + j * TPB + qt + 1)
                        c = j * TPB + qt
                        nc.vector.tensor_reduce(M[:, g % 2, c:c + 1], SA[:, qt % 2, :], AX.X, ALU.max
                                                ).then_inc(sa_free, 1)

                def split_maxima(b, g):
                    m = M[:, g % 2, :]
                    parts = mparts[:, g % 2, 0:MR * UA].rearrange("p (a c) -> p a c", c=UA)
                    done = b * (NG * SPLIT) + SPLIT * g
                    dve.wait_ge(sa_free, b * (NG * UA) + (g + 1) * UA + 2)
                    nc.vector.tensor_scalar(parts[:, 0, :], m, -1.0, None, ALU.mult).then_inc(split, 1)
                    dve.wait_ge(split, done + 1)
                    nc.vector.scalar_tensor_tensor(out=rest[:], in0=m, scalar=-1.0, in1=parts[:, 0, :],
                                                   op0=ALU.mult, op1=ALU.subtract).then_inc(split, 1)
                    dve.wait_ge(split, done + 2)
                    nc.vector.tensor_copy(parts[:, 1, :], rest[:]).then_inc(split, 1)
                    dve.wait_ge(split, done + 3)
                    nc.vector.tensor_tensor(parts[:, 2, :], rest[:], parts[:, 1, :], ALU.subtract).then_inc(split, 1)

                def group(b, g):
                    for j in range(GH):
                        maxima(b, g, j)
                    split_maxima(b, g)

                dve.sem_inc(sa_free, 2)
                nc.vector.memset(Ks[SR:SR + MR], 1.0)
                nc.vector.memset(mparts[:], 0.0)
                nc.vector.memset(Vg[:], 0.0).then_inc(set_up, 1)
                dve.wait_ge(set_up, 1)
                nc.vector.memset(Vg[:, :, :, :, DH:DH + 1], 1.0).then_inc(set_up, 1)
                group(0, 0)
                group(0, 1)
                with dve.Fori(0, B - 1) as b:
                    for g in range(NG):
                        group(*later(b, g, 2))
                for g in range(NG - 2):
                    group(*later(B - 1, g, 2))

            @block.scalar
            def _(act):
                def exponentials(b, g, kt):
                    for pair in range(2):
                        act.wait_ge(st_ready, b * (8 * NG) + 8 * g + 2 * kt + pair + 1)
                        act.wait_ge(pv_done, b * (NG * TPB) + g * TPB + kt + 1)
                        nc.scalar.activation(probs[:, kt % 2, 2 * pair:2 * pair + 2, :], ST[:, pair], ACT.Exp
                                             ).then_inc(exp_done, 1)

                def copy_maxima(b, g):
                    act.wait_ge(m_turned, b * NG + g + 1)
                    nc.scalar.copy(mT[:, g % 2, :], MT[0:MR * UA, 0:P]).then_inc(m_copied, 1)

                def copy_out(b, g):
                    act.wait_ge(pv_done, b * (NG * TPB) + (g + 1) * TPB + 2)
                    nc.scalar.copy(k.AO[:, g, bass.ds(b * S, S)], O[:]).then_inc(o_copied, 1)

                def group(b, g, last):
                    for kt in range(TPB):
                        if kt < TPB - 1:
                            exponentials(b, g, kt + 1)
                        elif not (last and g == NG - 1):
                            exponentials(*later(b, g, 1), 0)
                        if kt == 1 and not (last and g == NG - 1):
                            copy_maxima(*later(b, g, 1))
                    copy_out(b, g)

                act.sem_inc(exp_done, 2)
                act.sem_inc(m_copied, 1)
                act.sem_inc(o_copied, 1)
                copy_maxima(0, 0)
                exponentials(0, 0, 0)
                with act.Fori(0, B - 1) as b:
                    for g in range(NG):
                        group(b, g, False)
                for g in range(NG):
                    group(B - 1, g, True)

            @block.gpsimd
            def _(pool):
                def copy_values(b, g):
                    src = k.V[:, bass.ds(b * TPB, TPB), g * GH * DH:(g + 1) * GH * DH]
                    nc.gpsimd.tensor_copy(Vg[:, g, :, :, 0:DH], src.rearrange("p t (j d) -> p t j d", d=DH)
                                          ).then_inc(v_copied[g], 1)

                pool.wait_ge(set_up, 2)
                for g in range(NG):
                    copy_values(0, g)
                with pool.Fori(0, B - 1) as b:
                    for g in range(NG):
                        pool.wait_ge(pv_done, b * (NG * TPB) + (g + 1) * TPB + 2)
                        copy_values(b + 1, g)


def heads_output_phase(nc, k, io, layer):
    pre = f"L{layer}_xattn_"
    A = P // H
    W = N // A
    with ExitStack() as ctx:
        ph = Phase(nc, ctx, f"out{layer}")
        Wo = ph.sb("Wo", [P, NG, D])
        bv = ph.sb("bv", [P, NG])
        spread = ph.sb("spread", [3 * H, NG, P])
        spreadb = ph.sb("spreadb", [3 * H, NG, P], BF16)
        sums = ph.sb("sums", [P, W])
        inv = ph.sb("inv", [P, W])
        parts = ph.sb("parts", [P, 3, W], BF16)
        rows = ph.sb("rows", [3 * H, N], BF16)
        R = ph.ps("R", [P, 2, S])
        Y = ph.ps("Y", [P, 4, S])
        loaded, spread_ready, r_ready, scaled, biased, y_ready, added, dve_step = (
            ph.sem(n) for n in ("loaded", "spread_ready", "r_ready", "scaled", "biased", "y_ready", "added", "dve_step"))
        sums_there, rows_there, part_ready = (ph.sem(n) for n in ("sums_there", "rows_there", "part_ready"))

        def move_sums(eng, heads):
            for h in heads:
                j, g = h // NG, h % NG
                row = j * HS + DH
                eng.dma_start(sums[h * A:(h + 1) * A, :], k.AO[row:row + 1, g, :]).then_inc(sums_there, 16)

        with nc.Block() as block:

            @block.sync
            def _(sp):
                move_sums(sp, range(0, H, 2))
                sp.dma_start(spread[:], io["c_spread"]).then_inc(loaded, 16)
                sp.dma_start(Wo[:], io[pre + "Wo"].rearrange("g p o -> p g o")).then_inc(loaded, 16)
                sp.dma_start(bv[:], io[pre + "bv"]).then_inc(loaded, 16)
                for part in range(3):
                    sp.wait_ge(part_ready, part + 1)
                    sp.dma_start(rows[part * H:(part + 1) * H, :], parts[:, part, :]).then_inc(rows_there, 16)
                sp.wait_ge(loaded, 48)

            @block.tensor
            def _(pe):
                def spread_inverses(c, g):
                    u = c * NG + g
                    if u >= 2:
                        pe.wait_ge(scaled, u - 1)
                    nc.tensor.matmul(R[:, u % 2, :], spreadb[:, g, :], rows[:, c * S:(c + 1) * S], start=True, stop=True
                                     ).then_inc(r_ready, 1)

                def project(c):
                    pe.wait_ge(biased, NG * (c + 1))
                    for i in range(TPB):
                        t = c * TPB + i
                        if t >= 4:
                            pe.wait_ge(added, t - 3)
                        for g in range(NG):
                            mm = nc.tensor.matmul(Y[:, t % 4, 0:D], k.AO[:, g, t * P:(t + 1) * P], Wo[:, g, :],
                                                  start=(g == 0), stop=(g == NG - 1))
                        mm.then_inc(y_ready, 1)

                pe.wait_ge(loaded, 48)
                pe.wait_ge(spread_ready, 1)
                pe.wait_ge(rows_there, 48)
                for c in range(B):
                    for g in range(NG):
                        spread_inverses(c, g)
                    if c >= 1:
                        project(c - 1)
                project(B - 1)

            @block.vector
            def _(dve):
                v = nc.vector
                step = Steps(dve, dve_step)

                def add_out(c):
                    for t in range(c * TPB, (c + 1) * TPB):
                        dve.wait_ge(y_ready, t + 1)
                        v.tensor_tensor(k.x[:, t, :], k.x[:, t, :], Y[:, t % 4, 0:D], ALU.add).then_inc(added, 1)

                dve.wait_ge(sums_there, 16 * H)
                step.after(v.reciprocal(inv[:], sums[:]))
                v.tensor_copy(parts[:, 0, :], inv[:]).then_inc(part_ready, 1)
                dve.wait_ge(part_ready, 1)
                step.after(v.tensor_tensor(inv[:], inv[:], parts[:, 0, :], ALU.subtract))
                v.tensor_copy(parts[:, 1, :], inv[:]).then_inc(part_ready, 1)
                dve.wait_ge(part_ready, 2)
                v.tensor_tensor(parts[:, 2, :], inv[:], parts[:, 1, :], ALU.subtract).then_inc(part_ready, 1)
                dve.wait_ge(loaded, 48)
                v.tensor_copy(spreadb[:], spread[:]).then_inc(spread_ready, 1)
                for c in range(B):
                    for g in range(NG):
                        u = c * NG + g
                        a = k.AO[:, g, c * S:(c + 1) * S]
                        dve.wait_ge(r_ready, u + 1)
                        v.tensor_tensor(a, a, R[:, u % 2, :], ALU.mult).then_inc(scaled, 1)
                    if c >= 1:
                        add_out(c - 1)
                add_out(B - 1)

            @block.scalar
            def _(act):
                move_sums(act, range(1, H, 2))
                act.wait_ge(loaded, 48)
                for u in range(B * NG):
                    c, g = u // NG, u % NG
                    a = k.AO[:, g, c * S:(c + 1) * S]
                    act.wait_ge(scaled, u + 1)
                    nc.scalar.activation(a, a, ACT.Identity, bias=bv[:, g:g + 1]).then_inc(biased, 1)


def heads_attention(nc, k, io, layer, rope=False, masked=False):
    with ExitStack() as ctx:
        ph = Phase(nc, ctx, f"heads{layer}")
        k.V = ph.sb("V", [P, NT, D])
        heads_project_phase(nc, k, io, layer, rope)
        k.AO = ph.sb("AO", [P, NG, N])
        if masked:
            k.pen = ph.sb("pen", [P, NT, S], BF16)
            k.penT = ph.sb("penT", [P, NT, S], BF16)
            mask_phase(nc, k, io)
        heads_attend_phase(nc, k, layer, masked)
        heads_output_phase(nc, k, io, layer)



def whole_attention(nc, k, io):
    pre = "L3_xattn_"
    with ExitStack() as ctx:
        ph = Phase(nc, ctx, "whole")
        W = {n: ph.sb(n, [P, KD, D]) for n in ("Wq", "Wk", "Wv")}
        bias = {n: ph.sb(n, [P, KD]) for n in ("bq", "bk")}
        bv = ph.sb("bv", [P, D])
        beta = ph.sb("beta", [P, 3])
        c01, c = ph.sb("c01", [P, 1]), ph.sb("c", [P, 1])
        qT, kT = ph.sb("qT", [P, KD, N]), ph.sb("kT", [P, KD, N])
        V = ph.sb("V", [P, NT, D])
        phi = ph.sb("phi", [P, NT, S])
        att = ph.sb("att", [P, 2, S])
        probs = ph.sb("probs", [P, 2, S])
        probsT = ph.sb("probsT", [P, 2, TPB, P])
        top, ntop = ph.sb("top", [P, NT]), ph.sb("ntop", [P, NT])
        total, inv = ph.sb("total", [P, NT]), ph.sb("inv", [P, NT])
        upd = ph.sb("upd", [P, 2, D])
        A = ph.ps("A", [P, 4, S])
        T = ph.ps("T", [P, 2, TPB, P])
        Y = ph.ps("Y", [P, 2, S])
        w_loaded, phi_loaded, dve_step = ph.sem("w_loaded"), ph.sem("phi_loaded"), ph.sem("dve_step")
        proj_ready, proj_taken = ph.sem("proj_ready"), ph.sem("proj_taken")
        s_ready, s_taken, top_ready, exp_done = (ph.sem(n) for n in ("s_ready", "s_taken", "top_ready", "exp_done"))
        turned, turn_taken, y_ready, y_taken = (ph.sem(n) for n in ("turned", "turn_taken", "y_ready", "y_taken"))
        NC = N // S
        projections = [(w, m, cc) for w in ("q", "k") for m in range(KD) for cc in range(NC)]
        NPJ = len(projections)
        with nc.Block() as block:

            @block.sync
            def _(sp):
                for n in W:
                    sp.dma_start(W[n][:], io[pre + n].rearrange("(c p) o -> p c o", p=P)).then_inc(w_loaded, 16)
                for n in bias:
                    sp.dma_start(bias[n][:], io[pre + n]).then_inc(w_loaded, 16)
                sp.dma_start(bv[:], io[pre + "bv"]).then_inc(w_loaded, 16)
                sp.dma_start(beta[:], io[pre + "beta"]).then_inc(w_loaded, 16)
                sp.dma_start(phi[:], io["fside_BxSxS2_0"].rearrange("b (t p) s -> p (b t) s", p=P)).then_inc(phi_loaded, 16)
                sp.wait_ge(phi_loaded, 16)

            @block.tensor
            def _(pe):
                pe.wait_ge(w_loaded, 16 * 7)
                for i, (w, m, cc) in enumerate(projections):
                    src = k.xnT if w == "q" else k.ctxT
                    if i >= 4:
                        pe.wait_ge(proj_taken, i - 3)
                    for kd in range(KD):
                        mm = nc.tensor.matmul(A[:, i % 4, :], W["W" + w][:, kd, m * P:(m + 1) * P],
                                              src[:, kd, cc * S:(cc + 1) * S], start=(kd == 0), stop=(kd == KD - 1))
                    mm.then_inc(proj_ready, 1)
                for t in range(NT):
                    i = NPJ + t
                    pe.wait_ge(proj_taken, i - 3)
                    for kd in range(KD):
                        mm = nc.tensor.matmul(A[:, i % 4, 0:D], k.ctxT[:, kd, t * P:(t + 1) * P], W["Wv"][:, kd, :],
                                              start=(kd == 0), stop=(kd == KD - 1))
                    mm.then_inc(proj_ready, 1)

                def scores(t):
                    if t < 4:
                        pe.wait_ge(proj_taken, NPJ + NT)
                    else:
                        pe.wait_ge(s_taken, t - 3)
                    for kd in range(KD):
                        mm = nc.tensor.matmul(A[:, t % 4, :], qT[:, kd, t * P:(t + 1) * P],
                                              kT[:, kd, (t // TPB) * S:(t // TPB + 1) * S],
                                              start=(kd == 0), stop=(kd == KD - 1))
                    mm.then_inc(s_ready, 1)

                def turn(t):
                    pe.wait_ge(exp_done, t + 1)
                    if t >= 2:
                        pe.wait_ge(turn_taken, t - 1)
                    for kt in range(TPB):
                        mm = nc.tensor.transpose(T[:, t % 2, kt, :], probs[:, t % 2, kt * P:(kt + 1) * P], k.identf[:])
                    mm.then_inc(turned, 1)

                def weigh(t):
                    pe.wait_ge(turn_taken, t + 1)
                    if t >= 2:
                        pe.wait_ge(y_taken, t - 1)
                    for kt in range(TPB):
                        mm = nc.tensor.matmul(Y[:, t % 2, 0:D], probsT[:, t % 2, kt, :], V[:, (t // TPB) * TPB + kt, :],
                                              start=(kt == 0), stop=(kt == TPB - 1))
                    mm.then_inc(y_ready, 1)

                for t in range(NT + 3):
                    if t < NT:
                        scores(t)
                    if 2 <= t < NT + 2:
                        turn(t - 2)
                    if t >= 3:
                        weigh(t - 3)

            @block.vector
            def _(dve):
                step = Steps(dve, dve_step)
                dve.wait_ge(w_loaded, 16 * 7)
                step.after(nc.vector.tensor_tensor(c01[:], beta[:, 0:1], beta[:, 1:2], ALU.add))
                step.after(nc.vector.tensor_tensor(c[:], c01[:], beta[:, 2:3], ALU.subtract))
                for i, (w, m, cc) in enumerate(projections):
                    dve.wait_ge(proj_ready, i + 1)
                    dst = (qT if w == "q" else kT)[:, m, cc * S:(cc + 1) * S]
                    nc.vector.tensor_scalar(dst, A[:, i % 4, :], bias["b" + w][:, m:m + 1], D ** -0.5 if w == "q" else 1.0,
                                            ALU.add, ALU.mult).then_inc(proj_taken, 1)
                for t in range(NT):
                    dve.wait_ge(proj_ready, NPJ + t + 1)
                    nc.vector.tensor_copy(V[:, t, :], A[:, (NPJ + t) % 4, 0:D]).then_inc(proj_taken, 1)
                dve.wait_ge(phi_loaded, 16)

                def add_out(t):
                    dve.wait_ge(exp_done, t + 1)
                    step.after(nc.vector.reciprocal(inv[:, t:t + 1], total[:, t:t + 1]))
                    dve.wait_ge(y_ready, t + 1)
                    ins = nc.vector.scalar_tensor_tensor(out=upd[:, t % 2, :], in0=Y[:, t % 2, 0:D], scalar=inv[:, t:t + 1],
                                                         in1=bv[:], op0=ALU.mult, op1=ALU.add)
                    ins.then_inc(y_taken, 1)
                    dve.wait_ge(y_taken, t + 1)
                    nc.vector.tensor_tensor(k.x[:, t, :], k.x[:, t, :], upd[:, t % 2, :], ALU.add)

                for t in range(NT):
                    dve.wait_ge(s_ready, t + 1)
                    if t >= 2:
                        dve.wait_ge(exp_done, t - 1)
                    nc.vector.scalar_tensor_tensor(out=att[:, t % 2, :], in0=phi[:, t, :], scalar=c[:, 0:1],
                                                   in1=A[:, t % 4, :], op0=ALU.mult, op1=ALU.add).then_inc(s_taken, 1)
                    dve.wait_ge(s_taken, t + 1)
                    step.after(nc.vector.tensor_reduce(top[:, t:t + 1], att[:, t % 2, :], AX.X, ALU.max))
                    nc.vector.tensor_scalar(ntop[:, t:t + 1], top[:, t:t + 1], -1.0, None, ALU.mult).then_inc(top_ready, 1)
                    if t >= 3:
                        add_out(t - 3)
                for t in range(NT - 3, NT):
                    add_out(t)

            @block.scalar
            def _(act):
                for t in range(NT):
                    act.wait_ge(top_ready, t + 1)
                    if t >= 2:
                        act.wait_ge(turned, t - 1)
                    nc.scalar.activation(probs[:, t % 2, :], att[:, t % 2, :], ACT.Exp, bias=ntop[:, t:t + 1],
                                         accum_out=total[:, t:t + 1]).then_inc(exp_done, 1)
                    if t >= 1:
                        act.wait_ge(turned, t)
                        nc.scalar.copy(probsT[:, (t - 1) % 2], T[:, (t - 1) % 2]).then_inc(turn_taken, 1)
                act.wait_ge(turned, NT)
                nc.scalar.copy(probsT[:, (NT - 1) % 2], T[:, (NT - 1) % 2]).then_inc(turn_taken, 1)



class Moe:

    def __init__(self, layer, gate, w1, w2, b1, b2, picks, units, size, chunk, func):
        self.layer, self.gate, self.w1, self.w2, self.b1, self.b2 = layer, gate, w1, w2, b1, b2
        self.picks, self.units, self.size, self.chunk, self.func = picks, units, size, chunk, func
        self.slots = units * size


E8 = 8
F = 1024
FT = F // P
CAP2 = int(S / E8 * 1.25)
CAP3 = int(2 * 1.25 * N / E8)
CAP3 += CAP3 % 2
SIZE0 = 2 * P
UNITS0 = (N + E8 * (SIZE0 - 1)) // SIZE0
UNITS0 += UNITS0 % 2
SIZE2 = -(-B * CAP2 // P) * P
MOES = {
    0: Moe(0, "L0_ffn_gate_w", "L0_ffn_w1", "L0_ffn_w2", "L0_ffn_b1", "L0_ffn_b2", 1, UNITS0, SIZE0, SIZE0, ACT.Relu),
    2: Moe(2, "L2_ffn_Wr", "L2_ffn_W1", "L2_ffn_W2", "L2_ffn_b1", "L2_ffn_b2", 2, E8, SIZE2, SIZE2, ACT.Relu),
    3: Moe(3, "L3_ffn_w_g", "L3_ffn_c_fc", "L3_ffn_c_proj", None, None, 2, E8, CAP3, CAP3 // 2, ACT.Gelu),
}
GATHERS = 4
FAR = float(1 << 20)


def logits_products(nc, k, pe, gate, L, E):
    for t in range(NT):
        for kd in range(KD):
            mm = nc.tensor.matmul(L[:, t, :], k.xnT[:, kd, t * P:(t + 1) * P], gate[:, kd, :],
                                  start=(kd == 0), stop=(kd == KD - 1))
    return mm


def route_phase(nc, k, io, moe, r):
    K = moe.picks
    with ExitStack() as ctx:
        ph = Phase(nc, ctx, f"route{moe.layer}")
        gate = ph.sb("gate", [P, KD, E8])
        gbias = ph.sb("gbias", [P, 2, NT, E8])
        lg = ph.sb("lg", [P, NT, E8])
        tmp = ph.sb("tmp", [P, NT, E8])
        best = ph.sb("best", [P, NT, 8])
        col = ph.sb("col", [P, NT])
        ix = ph.sb("ix", [P, NT, 8], U32)
        ixf = ph.sb("ixf", [P, NT, 8])
        hot = ph.sb("hot", [P, K, NT, E8])
        counted = 1 if moe.layer == 2 else K
        hotb = ph.sb("hotb", [P, counted, NT, E8], BF16)
        rank_in = ph.sb("rank_in", [P, counted, NT, E8])
        tot = ph.sb("tot", [P, counted * NT, E8])
        off = ph.sb("off", [P, counted * NT + 1, E8])
        rank = ph.sb("rank", [P, NT])
        base = ph.sb("base", [P, NT])
        keep = ph.sb("keep", [P, NT])
        slot = ph.sb("slot", [P, NT])
        slot2 = ph.sb("slot2", [P, NT])
        nunit = ph.sb("nunit", [P, E8, 8])
        cnt = ph.sb("cnt", [P, E8])
        uend = ph.sb("uend", [P, E8 + 1])
        utab = ph.sb("utab", [P, moe.units, E8])
        uexp = ph.sb("uexp", [P, moe.units])
        L = ph.ps("L", [P, NT, E8])
        C = ph.ps("C", [P, 512])
        Z = ph.ps("Z", [P, 512])
        loaded, l_ready, hot_ready, c_ready, dve_step, act_done, act_asked = (
            ph.sem(n) for n in ("loaded", "l_ready", "hot_ready", "c_ready", "dve_step", "act_done", "act_asked"))
        biases = {0: 2, 2: 1, 3: 0}[moe.layer]
        per = E8 * NT
        with nc.Block() as block:

            @block.sync
            def _(sp):
                sp.dma_start(gate[:], io[moe.gate].rearrange("(c p) e -> p c e", p=P)).then_inc(loaded, 16)
                if biases:
                    sp.dma_start(gbias[:, 0:biases], io[f"gbias{moe.layer}"]).then_inc(loaded, 16)
                sp.wait_ge(loaded, 16 * (1 + bool(biases)))

            @block.tensor
            def _(pe):
                pe.wait_ge(loaded, 16 * (1 + bool(biases)))
                logits_products(nc, k, pe, gate, L, E8).then_inc(l_ready, 1)
                pe.wait_ge(hot_ready, 1)
                flat = hotb[:].rearrange("p k t e -> p (k t e)")
                nc.tensor.matmul(C[:, 0:counted * per], k.before[:], flat, start=True, stop=True)
                nc.tensor.matmul(Z[:, 0:counted * per], k.onesb[:], flat, start=True, stop=True).then_inc(c_ready, 1)

            @block.scalar
            def _(act):
                if moe.layer == 2:
                    act.wait_ge(act_asked, 1)
                    nc.scalar.activation(lg[:], tmp[:], ACT.Exp).then_inc(act_done, 1)
                if moe.layer == 3:
                    act.wait_ge(act_asked, 1)
                    nc.scalar.activation(keep[:], col[:], ACT.Exp).then_inc(act_done, 1)

            @block.vector
            def _(dve):
                v = nc.vector
                step = Steps(dve, dve_step)
                wide = [P, NT, E8]

                def over(a):
                    return a.unsqueeze(2).to_broadcast(wide)

                dve.wait_ge(l_ready, 1)
                dve.wait_ge(loaded, 16 * (1 + bool(biases)))
                if biases:
                    step.after(v.tensor_tensor(lg[:], L[:], gbias[:, 0], ALU.add))
                    if biases == 2:
                        step.after(v.tensor_tensor(lg[:], lg[:], gbias[:, 1], ALU.add))
                else:
                    step.after(v.tensor_copy(lg[:], L[:]))
                if moe.layer == 2:
                    step.after(v.tensor_reduce(col[:], lg[:], AX.X, ALU.max))
                    v.tensor_tensor(tmp[:], lg[:], over(col[:]), ALU.subtract).then_inc(act_asked, 1)
                    dve.wait_ge(act_done, 1)
                    step.after(v.tensor_reduce(col[:], lg[:], AX.X, ALU.add))
                    step.after(v.reciprocal(col[:], col[:]))
                    step.after(v.tensor_tensor(lg[:], lg[:], over(col[:]), ALU.mult))
                for t in range(NT):
                    ins = v.max(best[:, t, :], lg[:, t, :])
                step.after(ins)
                for t in range(NT):
                    ins = v.max_index(ix[:, t, :], best[:, t, :], lg[:, t, :])
                step.after(ins)
                step.after(v.tensor_copy(ixf[:], ix[:]))
                if moe.layer == 2:
                    for p in range(K):
                        ins = v.tensor_copy(r.weight[:, p, :], best[:, :, p])
                elif moe.layer == 3:
                    v.tensor_tensor(col[:], best[:, :, 1], best[:, :, 0], ALU.subtract).then_inc(act_asked, 1)
                    dve.wait_ge(act_done, 1)
                    step.after(v.tensor_scalar(col[:], keep[:], 1.0, None, ALU.add))
                    step.after(v.reciprocal(r.weight[:, 0, :], col[:]))
                    ins = v.tensor_tensor(r.weight[:, 1, :], r.weight[:, 0, :], keep[:], ALU.mult)
                else:
                    ins = v.memset(r.weight[:], 1.0)
                step.after(ins)
                iota8 = k.iota[:, 0:E8].unsqueeze(1).to_broadcast(wide)
                for p in range(K):
                    ins = v.tensor_tensor(hot[:, p], iota8, ixf[:, :, p:p + 1].to_broadcast(wide), ALU.is_equal)
                step.after(ins)
                if moe.layer == 2:
                    ins = v.tensor_tensor(hotb[:, 0], hot[:, 0], hot[:, 1], ALU.add)
                else:
                    ins = v.tensor_copy(hotb[:], hot[:])
                ins.then_inc(hot_ready, 1)
                dve.wait_ge(c_ready, 1)
                v.tensor_copy(tot[:], Z[:, 0:counted * per].rearrange("p (t e) -> p t e", e=E8))
                step.after(v.memset(off[:], 0.0))
                for i in range(counted * NT):
                    if moe.layer == 2 and (i + 1) % TPB == 0:
                        continue
                    step.after(v.tensor_tensor(off[:, i + 1, :], off[:, i, :], tot[:, i, :], ALU.add))
                step.after(v.tensor_tensor(rank_in[:].rearrange("p k t e -> p (k t) e"), off[:, 0:counted * NT, :],
                                           C[:, 0:counted * per].rearrange("p (t e) -> p t e", e=E8), ALU.add))
                if moe.layer == 0:
                    step.after(v.tensor_scalar(cnt[:], off[:, NT, :], 1.0 / SIZE0, None, ALU.mult))
                    step.after(v.tensor_tensor(nunit[:], cnt[:].unsqueeze(2).to_broadcast([P, E8, 8]),
                                               k.iota[:, 0:8].unsqueeze(1).to_broadcast([P, E8, 8]), ALU.is_gt))
                    step.after(v.tensor_reduce(cnt[:], nunit[:], AX.X, ALU.add))
                    step.after(v.memset(uend[:], 0.0))
                    for e in range(E8):
                        step.after(v.tensor_tensor(uend[:, e + 1:e + 2], uend[:, e:e + 1], cnt[:, e:e + 1], ALU.add))
                    step.after(v.tensor_tensor(utab[:], k.iota[:, 0:moe.units].unsqueeze(2).to_broadcast([P, moe.units, E8]),
                                               uend[:, 1:].unsqueeze(1).to_broadcast([P, moe.units, E8]), ALU.is_ge))
                    step.after(v.tensor_reduce(uexp[:], utab[:], AX.X, ALU.add))
                    step.after(v.tensor_scalar(uexp[:], uexp[:], E8 - 1.0, None, ALU.min))
                    step.after(v.tensor_copy(r.unit_expert[:], uexp[:]))
                    step.after(v.tensor_tensor(tmp[:], hot[:, 0], uend[:, 0:E8].unsqueeze(1).to_broadcast(wide), ALU.mult))
                    step.after(v.tensor_reduce(base[:], tmp[:], AX.X, ALU.add))
                    step.after(v.tensor_scalar(base[:], base[:], float(SIZE0), None, ALU.mult))
                for p in range(K):
                    step.after(v.tensor_tensor(tmp[:], hot[:, p], rank_in[:, p % counted], ALU.mult))
                    step.after(v.tensor_reduce(rank[:], tmp[:], AX.X, ALU.add))
                    if moe.layer != 0:
                        step.after(v.tensor_scalar(base[:], ixf[:, :, p], float(moe.size), None, ALU.mult))
                    if moe.layer == 2:
                        for b in range(1, B):
                            sl = base[:, b * TPB:(b + 1) * TPB]
                            ins = v.tensor_scalar(sl, sl, float(b * CAP2), None, ALU.add)
                        step.after(ins)
                    cap = {0: float(N + 1), 2: float(CAP2), 3: float(CAP3)}[moe.layer]
                    v.tensor_tensor(slot[:], rank[:], base[:], ALU.add)
                    step.after(v.tensor_scalar(keep[:], rank[:], cap, None, ALU.is_lt))
                    v.tensor_tensor(r.weight[:, p, :], r.weight[:, p, :], keep[:], ALU.mult)
                    step.after(v.tensor_tensor(slot[:], slot[:], keep[:], ALU.mult))
                    v.tensor_copy(r.take[:, p, :], slot[:])
                    step.after(v.tensor_scalar(keep[:], keep[:], -FAR, FAR, ALU.mult, ALU.add))
                    step.after(v.tensor_tensor(slot2[:], slot[:], keep[:], ALU.add))
                    step.after(v.tensor_copy(r.put[:, p, :], slot2[:]))


def dispatch_phase(nc, k, moe, r):
    k.n_scattered += NT * moe.picks
    with nc.Block() as block:

        @block.gpsimd
        def _(pool):
            for t in range(NT):
                for p in range(moe.picks):
                    pool.indirect_dma_start(out=k.xg[0:moe.slots, :],
                                            out_offset=bass.IndirectOffsetOnAxis(ap=r.put[:, p, t:t + 1], axis=0),
                                            in_=k.xn[:, t, :], in_offset=None, bounds_check=moe.slots - 1,
                                            oob_is_err=False).then_inc(k.scattered, 16)
            pool.wait_ge(k.scattered, 16 * k.n_scattered)


def combine_phase(nc, k, moe, r):
    with ExitStack() as ctx:
        ph = Phase(nc, ctx, f"combine{moe.layer}")
        g = ph.sb("g", [P, GATHERS, D])
        added = ph.sem("added")
        todo = [(t, p) for t in range(NT) for p in range(moe.picks)]
        before = k.n_gathered
        k.n_gathered += len(todo) // GATHERS
        with nc.Block() as block:

            @block.gpsimd
            def _(pool):
                for i, (t, p) in enumerate(todo):
                    if i >= GATHERS:
                        pool.wait_ge(added, i - GATHERS + 1)
                    pool.indirect_dma_start(out=g[:, i % GATHERS, :], out_offset=None, in_=k.yg[0:moe.slots, :],
                                            in_offset=bass.IndirectOffsetOnAxis(ap=r.take[:, p, t:t + 1], axis=0),
                                            bounds_check=moe.slots - 1, oob_is_err=False
                                            ).then_inc(k.gathered[i % GATHERS], 16)

            @block.vector
            def _(dve):
                for i, (t, p) in enumerate(todo):
                    dve.wait_ge(k.gathered[i % GATHERS], 16 * (before + i // GATHERS + 1))
                    if p:
                        dve.wait_ge(added, i)
                    nc.vector.scalar_tensor_tensor(out=k.x[:, t, :], in0=g[:, i % GATHERS, :],
                                                   scalar=r.weight[:, p, t:t + 1], in1=k.x[:, t, :],
                                                   op0=ALU.mult, op1=ALU.add).then_inc(added, 1)


def experts_phase(nc, k, io, moe, r):
    n_t = moe.size // P
    CH = moe.chunk
    n_ch = moe.size // CH
    biased = moe.b1 is not None
    HR = 4
    with ExitStack() as ctx:
        ph = Phase(nc, ctx, f"experts{moe.layer}")
        W1 = ph.sb("W1", [P, 2, KD, F])
        W2 = ph.sb("W2", [P, 2, FT, D])
        b1 = ph.sb("b1", [P, 2, FT])
        b2 = ph.sb("b2", [P, 2, D])
        xg = ph.sb("xg", [P, 2, n_t, D])
        xgT = ph.sb("xgT", [P, 2, KD, moe.size])
        hT = ph.sb("hT", [P, FT, moe.size])
        y = ph.sb("y", [P, 2, n_t, D])
        T = ph.ps("T", [P, 2, KD, 2 * P])
        Hb = ph.ps("Hb", [P, HR, S])
        Y = ph.ps("Y", [P, 2, S])
        w_loaded = [ph.sem(f"w_loaded{i}") for i in range(2)]
        x_loaded = [ph.sem(f"x_loaded{i}") for i in range(2)]
        stored = [ph.sem(f"stored{i}") for i in range(2)]
        turned, turn_taken, h_ready, h_taken, y_ready, y_taken = (
            ph.sem(n) for n in ("turned", "turn_taken", "h_ready", "h_taken", "y_ready", "y_taken"))
        HU = FT * n_ch
        PAIRS = moe.units // 2
        wdma = 4 if biased else 2
        with nc.Block() as block:

            @block.sync
            def _(sp):
                def load(pair, i):
                    u = pair * 2 + i
                    if moe.layer == 0:
                        e = sp.value_load(r.unit_expert[0:1, bass.ds(u, 1)], min_val=0, max_val=E8 - 1)
                    else:
                        e = u
                    sp.dma_start(xg[:, i], k.xg[bass.ds(u * moe.size, moe.size), :].rearrange("(t p) d -> p t d", p=P)
                                 ).then_inc(x_loaded[i], 16)
                    sp.dma_start(W1[:, i], io[moe.w1][bass.ds(e, 1)].rearrange("e (c p) f -> p (e c) f", p=P)
                                 ).then_inc(w_loaded[i], 16)
                    sp.dma_start(W2[:, i], io[moe.w2][bass.ds(e, 1)].rearrange("e (f p) d -> p (e f) d", p=P)
                                 ).then_inc(w_loaded[i], 16)
                    if biased:
                        sp.dma_start(b1[:, i, :], io[moe.b1][bass.ds(e, 1)].rearrange("e p f -> p (e f)")
                                     ).then_inc(w_loaded[i], 16)
                        sp.dma_start(b2[:, i, :], io[moe.b2][bass.ds(e, 1)].rearrange("e p d -> p (e d)")
                                     ).then_inc(w_loaded[i], 16)

                def store(pair, i):
                    u = pair * 2 + i
                    sp.wait_ge(y_taken, pair * (2 * n_t) + (i + 1) * n_t + 2)
                    sp.dma_start(k.yg[bass.ds(u * moe.size, moe.size), :].rearrange("(t p) d -> p t d", p=P), y[:, i]
                                 ).then_inc(stored[i], 16)

                load(0, 0)
                load(0, 1)
                with sp.Fori(0, PAIRS - 1) as pair:
                    for i in range(2):
                        store(pair, i)
                        load(pair + 1, i)
                for i in range(2):
                    store(PAIRS - 1, i)
                for i in range(2):
                    sp.wait_ge(stored[i], 16 * PAIRS + 16)

            @block.tensor
            def _(pe):
                def turn(pair, i):
                    pe.wait_ge(x_loaded[i], pair * 16 + 16)
                    for t in range(n_t):
                        j = i * n_t + t
                        pe.wait_ge(turn_taken, pair * (2 * n_t) + j + 1)
                        for c in range(KD):
                            mm = nc.tensor.transpose(T[:, j % 2, c, 0:P], xg[:, i, t, c * P:(c + 1) * P], k.identf[:])
                        mm.then_inc(turned, 1)

                def first(pair, i):
                    pe.wait_ge(w_loaded[i], pair * (16 * wdma) + 16 * wdma)
                    pe.wait_ge(turn_taken, pair * (2 * n_t) + (i + 1) * n_t + 2)
                    for f in range(FT):
                        for ch in range(n_ch):
                            j = i * HU + f * n_ch + ch
                            pe.wait_ge(h_taken, pair * (2 * HU) + j + 1)
                            for kd in range(KD):
                                mm = nc.tensor.matmul(Hb[:, j % HR, 0:CH], W1[:, i, kd, f * P:(f + 1) * P],
                                                      xgT[:, i, kd, ch * CH:(ch + 1) * CH],
                                                      start=(kd == 0), stop=(kd == KD - 1))
                            mm.then_inc(h_ready, 1)

                def second(pair, i):
                    pe.wait_ge(h_taken, pair * (2 * HU) + (i + 1) * HU + HR)
                    for t in range(n_t):
                        j = i * n_t + t
                        pe.wait_ge(y_taken, pair * (2 * n_t) + j + 1)
                        for f in range(FT):
                            mm = nc.tensor.matmul(Y[:, j % 2, 0:D], hT[:, f, t * P:(t + 1) * P], W2[:, i, f, :],
                                                  start=(f == 0), stop=(f == FT - 1))
                        mm.then_inc(y_ready, 1)

                turn(0, 0)
                with pe.Fori(0, PAIRS - 1) as pair:
                    first(pair, 0)
                    turn(pair, 1)
                    second(pair, 0)
                    first(pair, 1)
                    turn(pair + 1, 0)
                    second(pair, 1)
                first(PAIRS - 1, 0)
                turn(PAIRS - 1, 1)
                second(PAIRS - 1, 0)
                first(PAIRS - 1, 1)
                second(PAIRS - 1, 1)

            @block.scalar
            def _(act):
                def hidden(pair, i):
                    act.wait_ge(w_loaded[i], pair * (16 * wdma) + 16 * wdma)
                    for f in range(FT):
                        for ch in range(n_ch):
                            j = i * HU + f * n_ch + ch
                            act.wait_ge(h_ready, pair * (2 * HU) + j + 1)
                            nc.scalar.activation(hT[:, f, ch * CH:(ch + 1) * CH], Hb[:, j % HR, 0:CH], moe.func,
                                                 bias=b1[:, i, f:f + 1] if biased else 0.0).then_inc(h_taken, 1)

                act.sem_inc(h_taken, HR)
                with act.Fori(0, PAIRS) as pair:
                    for i in range(2):
                        hidden(pair, i)

            @block.vector
            def _(dve):
                def take_turned(pair, i):
                    for t in range(n_t):
                        j = i * n_t + t
                        dve.wait_ge(turned, pair * (2 * n_t) + j + 1)
                        nc.vector.tensor_copy(xgT[:, i, :, t * P:(t + 1) * P], T[:, j % 2, :, 0:P]).then_inc(turn_taken, 1)

                def take_out(pair, i):
                    dve.wait_ge(stored[i], pair * 16 + 16)
                    if biased:
                        dve.wait_ge(w_loaded[i], pair * (16 * wdma) + 16 * wdma)
                    for t in range(n_t):
                        j = i * n_t + t
                        dve.wait_ge(y_ready, pair * (2 * n_t) + j + 1)
                        if biased:
                            ins = nc.vector.tensor_tensor(y[:, i, t, :], Y[:, j % 2, 0:D], b2[:, i, :], ALU.add)
                        else:
                            ins = nc.vector.tensor_copy(y[:, i, t, :], Y[:, j % 2, 0:D])
                        ins.then_inc(y_taken, 1)

                for i in range(2):
                    dve.sem_inc(stored[i], 16)
                dve.sem_inc(turn_taken, 2)
                dve.sem_inc(y_taken, 2)
                take_turned(0, 0)
                with dve.Fori(0, PAIRS - 1) as pair:
                    take_turned(pair, 1)
                    take_out(pair, 0)
                    take_turned(pair + 1, 0)
                    take_out(pair, 1)
                take_turned(PAIRS - 1, 1)
                take_out(PAIRS - 1, 0)
                take_out(PAIRS - 1, 1)


class Routes:
    pass


def slot_moe(nc, k, io, moe):
    with ExitStack() as ctx:
        ph = Phase(nc, ctx, f"moe{moe.layer}")
        r = Routes()
        r.weight = ph.sb("weight", [P, moe.picks, NT])
        r.take = ph.sb("take", [P, moe.picks, NT], U32)
        r.put = ph.sb("put", [P, moe.picks, NT], U32)
        r.unit_expert = ph.sb("unit_expert", [P, moe.units], I32)
        route_phase(nc, k, io, moe, r)
        dispatch_phase(nc, k, moe, r)
        experts_phase(nc, k, io, moe, r)
        combine_phase(nc, k, moe, r)


E32, GRP, PICKS1, GRPS = 32, 8, 8, 4
ESZ = E32 // GRP
SCALE1 = 2.5
SHARED = 2


def group_route_phase(nc, k, io, r):
    with ExitStack() as ctx:
        ph = Phase(nc, ctx, "route1")
        gate = ph.sb("gate", [P, KD, E32])
        gbias = ph.sb("gbias", [P, NT, E32])
        sc = ph.sb("sc", [P, NT, E32])
        sb = ph.sb("sb", [P, NT, E32])
        ab = [ph.sb(f"ab{i}", [P, NT, GRP]) for i in range(6)]
        grp = ph.sb("grp", [P, NT, GRP])
        best = ph.sb("best", [P, NT, 8])
        ix = ph.sb("ix", [P, NT, 8], U32)
        ixf = ph.sb("ixf", [P, NT, 8])
        gm = ph.sb("gm", [P, NT, GRP])
        one = ph.sb("one", [P, NT, E32])
        comb = ph.sb("comb", [P, NT, E32])
        sums = ph.sb("sums", [P, NT])
        parts = ph.sb("parts", [P, NT, 3, E32], BF16)
        L = ph.ps("L", [P, NT, E32])
        T = ph.ps("T", [3 * E32, 2, 2 * S], BF16)
        loaded, l_ready, sig_done, dve_step, parts_ready, turned, taken = (
            ph.sem(n) for n in ("loaded", "l_ready", "sig_done", "dve_step", "parts_ready", "turned", "taken"))
        with nc.Block() as block:

            @block.sync
            def _(sp):
                sp.dma_start(gate[:], io["L1_ffn_gate_w"].rearrange("(c p) e -> p c e", p=P)).then_inc(loaded, 16)
                sp.dma_start(gbias[:], io["gbias1"]).then_inc(loaded, 16)
                sp.wait_ge(loaded, 32)

            @block.tensor
            def _(pe):
                pe.wait_ge(loaded, 32)
                logits_products(nc, k, pe, gate, L, E32).then_inc(l_ready, 1)
                pe.wait_ge(parts_ready, 1)
                for q in range(NT // TPB):
                    if q >= 2:
                        pe.wait_ge(taken, q - 1)
                    for i in range(TPB):
                        t = q * TPB + i
                        mm = nc.tensor.transpose(T[:, q % 2, i * P:(i + 1) * P], parts[:, t].rearrange("p a e -> p (a e)"),
                                                 k.identb[:])
                    mm.then_inc(turned, 1)

            @block.scalar
            def _(act):
                act.wait_ge(l_ready, 1)
                nc.scalar.activation(sc[:], L[:], ACT.Sigmoid).then_inc(sig_done, 1)
                for q in range(NT // TPB):
                    act.wait_ge(turned, q + 1)
                    nc.scalar.copy(r.combT[:, q * S:(q + 1) * S], T[:, q % 2, 0:S]).then_inc(taken, 1)

            @block.vector
            def _(dve):
                v = nc.vector
                step = Steps(dve, dve_step)
                dve.wait_ge(sig_done, 1)
                dve.wait_ge(loaded, 32)
                step.after(v.tensor_tensor(sb[:], sc[:], gbias[:], ALU.add))
                s4 = sb[:].rearrange("p t (g m) -> p t g m", m=ESZ)
                v.tensor_tensor(ab[0][:], s4[:, :, :, 0], s4[:, :, :, 1], ALU.max)
                v.tensor_tensor(ab[1][:], s4[:, :, :, 0], s4[:, :, :, 1], ALU.min)
                v.tensor_tensor(ab[2][:], s4[:, :, :, 2], s4[:, :, :, 3], ALU.max)
                step.after(v.tensor_tensor(ab[3][:], s4[:, :, :, 2], s4[:, :, :, 3], ALU.min))
                v.tensor_tensor(ab[4][:], ab[0][:], ab[2][:], ALU.max)
                v.tensor_tensor(ab[5][:], ab[0][:], ab[2][:], ALU.min)
                step.after(v.tensor_tensor(ab[1][:], ab[1][:], ab[3][:], ALU.max))
                step.after(v.tensor_tensor(ab[5][:], ab[5][:], ab[1][:], ALU.max))
                step.after(v.tensor_tensor(grp[:], ab[4][:], ab[5][:], ALU.add))
                for t in range(NT):
                    ins = v.max(best[:, t, :], grp[:, t, :])
                step.after(ins)
                for t in range(NT):
                    ins = v.max_index(ix[:, t, :], best[:, t, :], grp[:, t, :])
                step.after(ins)
                step.after(v.tensor_copy(ixf[:], ix[:]))
                step.after(v.memset(gm[:], 0.0))
                wide = [P, NT, GRP]
                iota8 = k.iota[:, 0:GRP].unsqueeze(1).to_broadcast(wide)
                for p in range(GRPS):
                    step.after(v.tensor_tensor(grp[:], iota8, ixf[:, :, p:p + 1].to_broadcast(wide), ALU.is_equal))
                    step.after(v.tensor_tensor(gm[:], gm[:], grp[:], ALU.add))
                for m in range(ESZ):
                    ins = v.tensor_tensor(s4[:, :, :, m], s4[:, :, :, m], gm[:], ALU.mult)
                step.after(ins)
                for t in range(NT):
                    ins = v.max(best[:, t, :], sb[:, t, :])
                step.after(ins)
                for t in range(NT):
                    ins = v.max_index(ix[:, t, :], best[:, t, :], sb[:, t, :])
                step.after(ins)
                step.after(v.tensor_copy(ixf[:], ix[:]))
                step.after(v.memset(comb[:], 0.0))
                wide = [P, NT, E32]
                iota32 = k.iota[:, 0:E32].unsqueeze(1).to_broadcast(wide)
                for p in range(PICKS1):
                    step.after(v.tensor_tensor(one[:], iota32, ixf[:, :, p:p + 1].to_broadcast(wide), ALU.is_equal))
                    step.after(v.tensor_tensor(comb[:], comb[:], one[:], ALU.add))
                step.after(v.tensor_tensor(comb[:], comb[:], sc[:], ALU.mult))
                step.after(v.tensor_reduce(sums[:], comb[:], AX.X, ALU.add))
                step.after(v.tensor_scalar(sums[:], sums[:], 1e-20, None, ALU.add))
                step.after(v.reciprocal(sums[:], sums[:]))
                step.after(v.tensor_tensor(comb[:], comb[:], sums[:].unsqueeze(2).to_broadcast(wide), ALU.mult))
                step.after(v.tensor_scalar(comb[:], comb[:], SCALE1, None, ALU.mult))
                step.after(v.tensor_copy(parts[:, :, 0, :], comb[:]))
                step.after(v.tensor_tensor(comb[:], comb[:], parts[:, :, 0, :], ALU.subtract))
                step.after(v.tensor_copy(parts[:, :, 1, :], comb[:]))
                v.tensor_tensor(parts[:, :, 2, :], comb[:], parts[:, :, 1, :], ALU.subtract).then_inc(parts_ready, 1)


def gated_experts_phase(nc, k, io, r):
    RING = 4
    NE = E32 + SHARED
    WID = 2 * KD * P + D
    with ExitStack() as ctx:
        ph = Phase(nc, ctx, "experts1")
        W = ph.sb("W", [P, RING, WID])
        sil = ph.sb("sil", [P, 2, S])
        prod = ph.sb("prod", [P, 2, S])
        hid = ph.sb("hid", [P, 2, S])
        picks = ph.sb("picks", [3 * E32, E32, P])
        pick = ph.sb("pick", [3 * E32, E32, P], BF16)
        G, U = ph.ps("G", [P, 2, S]), ph.ps("U", [P, 2, S])
        CB = ph.ps("CB", [P, 2, S])
        Y = ph.ps("Y", [P, 2, 2, D])
        p_loaded, p_ready = ph.sem("p_loaded"), ph.sem("p_ready")
        w_loaded = [ph.sem(f"w_loaded{i}") for i in range(RING)]
        gu_ready, sil_done, prod_done, hid_done, y_done, y_added, cb_ready, down_done = (
            ph.sem(n) for n in ("gu_ready", "sil_done", "prod_done", "hid_done", "y_done", "y_added", "cb_ready", "down_done"))
        NC = N // S

        def weights(i):
            w = W[:, i]
            return (w[:, 0:KD * P].rearrange("p (c f) -> p c f", c=KD),
                    w[:, KD * P:2 * KD * P].rearrange("p (c f) -> p c f", c=KD), w[:, 2 * KD * P:])

        with nc.Block() as block:

            @block.sync
            def _(sp):
                sp.dma_start(picks[:], io["c_pick"]).then_inc(p_loaded, 16)
                for n in range(NC * NE):
                    if n >= RING:
                        sp.wait_ge(down_done, n - RING + 1)
                    sp.dma_start(W[:, n % RING], io["w_gated"][n % NE]).then_inc(w_loaded[n % RING], 16)
                sp.wait_ge(p_loaded, 16)

            @block.tensor
            def _(pe):
                def up(n):
                    c, e = n // NE, n % NE
                    wg, wu, _ = weights(n % RING)
                    pe.wait_ge(w_loaded[n % RING], 16 * (n // RING + 1))
                    if n >= 2:
                        pe.wait_ge(hid_done, n - 1)
                    for w, ps in ((wg, G), (wu, U)):
                        for kd in range(KD):
                            nc.tensor.matmul(ps[:, n % 2, :], w[:, kd, :], k.xnT[:, kd, c * S:(c + 1) * S],
                                             start=(kd == 0), stop=(kd == KD - 1))
                    mm = nc.tensor.matmul(CB[:, n % 2, :], pick[:, e % E32, :], r.combT[:, c * S:(c + 1) * S],
                                          start=True, stop=True)
                    mm.then_inc(gu_ready, 1)

                def down(n):
                    c, e = n // NE, n % NE
                    wd = weights(n % RING)[2]
                    pe.wait_ge(hid_done, n + 1)
                    if e == 0 and c:
                        pe.wait_ge(y_added, TPB * c)
                    for i in range(TPB):
                        mm = nc.tensor.matmul(Y[:, i // 2, i % 2, :], hid[:, n % 2, i * P:(i + 1) * P], wd,
                                              start=(e == 0 and i % 2 == 0), stop=(e == NE - 1), skip_group_check=True)
                    mm.then_inc(down_done, 1)

                pe.wait_ge(p_ready, 1)
                for n in range(NC * NE + 1):
                    if n < NC * NE:
                        up(n)
                    if n >= 1:
                        down(n - 1)

            @block.scalar
            def _(act):
                for n in range(NC * NE):
                    act.wait_ge(gu_ready, n + 1)
                    if n >= 2:
                        act.wait_ge(prod_done, n - 1)
                    nc.scalar.activation(sil[:, n % 2, :], G[:, n % 2, :], ACT.Silu).then_inc(sil_done, 1)

            @block.vector
            def _(dve):
                def add_out(c):
                    dve.wait_ge(down_done, NE * (c + 1))
                    for i in range(TPB):
                        t = c * TPB + i
                        nc.vector.tensor_tensor(k.x[:, t, :], k.x[:, t, :], Y[:, i // 2, i % 2, :], ALU.add).then_inc(y_added, 1)

                dve.wait_ge(p_loaded, 16)
                nc.vector.tensor_copy(pick[:], picks[:]).then_inc(p_ready, 1)
                for n in range(NC * NE):
                    c, e = n // NE, n % NE
                    dve.wait_ge(sil_done, n + 1)
                    if n >= 2:
                        dve.wait_ge(down_done, n - 1)
                    if e < E32:
                        nc.vector.tensor_tensor(prod[:, n % 2, :], sil[:, n % 2, :], U[:, n % 2, :], ALU.mult
                                                ).then_inc(prod_done, 1)
                        dve.wait_ge(prod_done, n + 1)
                        nc.vector.tensor_tensor(hid[:, n % 2, :], prod[:, n % 2, :], CB[:, n % 2, :], ALU.mult
                                                ).then_inc(hid_done, 1)
                    else:
                        nc.vector.tensor_tensor(prod[:, n % 2, :], sil[:, n % 2, :], U[:, n % 2, :], ALU.mult
                                                ).then_inc(prod_done, 1)
                        dve.wait_ge(prod_done, n + 1)
                        nc.vector.tensor_copy(hid[:, n % 2, :], prod[:, n % 2, :]).then_inc(hid_done, 1)
                    if e == NE - 1:
                        add_out(c)


def gated_moe(nc, k, io):
    with ExitStack() as ctx:
        ph = Phase(nc, ctx, "moe1")
        r = Routes()
        r.combT = ph.sb("combT", [3 * E32, N], BF16)
        group_route_phase(nc, k, io, r)
        gated_experts_phase(nc, k, io, r)


def moe(nc, k, io, layer):
    if layer == 1:
        gated_moe(nc, k, io)
    else:
        slot_moe(nc, k, io, MOES[layer])


def ffn_layout(f):
    io = {}

    def each_token(a, *shape):
        return np.ascontiguousarray(np.broadcast_to(a, shape))

    io["L0_ffn_gate_w"] = np.ascontiguousarray(f["L0_ffn_gate_w"].T)
    io["L2_ffn_Wr"], io["L3_ffn_w_g"] = f["L2_ffn_Wr"], f["L3_ffn_w_g"]
    io["gbias0"] = each_token(np.stack([f["L0_ffn_gate_b"], f["L0_ffn_expert_bias"]])[None, :, None, :], P, 2, NT, E8)
    io["gbias2"] = each_token(f["L2_ffn_br"][None, None, None, :], P, 1, NT, E8)
    for m in MOES.values():
        io[m.w1], io[m.w2] = f[m.w1], f[m.w2]
        if m.b1:
            io[m.b1] = np.ascontiguousarray(f[m.b1].reshape(E8, FT, P).transpose(0, 2, 1))
            io[m.b2] = each_token(f[m.b2][:, None, :], E8, P, D)
    io["L1_ffn_gate_w"] = np.ascontiguousarray(f["L1_ffn_gate_w"].T)
    io["gbias1"] = each_token(f["L1_ffn_gate_bias"][None, None, :], P, NT, E32)
    wg = np.concatenate([f["L1_ffn_w_gate"], f["L1_ffn_sh_gate"].reshape(SHARED, P, D)])
    wu = np.concatenate([f["L1_ffn_w_up"], f["L1_ffn_sh_up"].reshape(SHARED, P, D)])
    wd = np.concatenate([f["L1_ffn_w_down"].transpose(0, 2, 1), f["L1_ffn_sh_down"].T.reshape(SHARED, P, D)])
    turned = [w.transpose(0, 2, 1).reshape(-1, KD, P, P).transpose(0, 2, 1, 3).reshape(-1, P, KD * P) for w in (wg, wu)]
    io["w_gated"] = np.ascontiguousarray(np.concatenate(turned + [wd], axis=2))
    pre = "L3_xattn_"
    for w in ("Wq", "Wk", "Wv"):
        io[pre + w] = np.ascontiguousarray(f[pre + w].T)
    for b in ("bq", "bk"):
        io[pre + b] = np.ascontiguousarray(f[pre + b].reshape(KD, P).T)
    io[pre + "bv"] = each_token(f[pre + "bv"][None, :], P, D)
    io[pre + "beta"] = each_token(np.stack([f[pre + "beta_" + n].reshape(()) for n in ("risk", "prio", "impl")])[None, :], P, 3)
    return io



class Kept:
    pass


def program(nc, io, out, stages=99, start=0):
    with ExitStack() as ctx:
        ph = Phase(nc, ctx, "kept")
        k = Kept()
        k.x = ph.sb("x", [P, NT, D])
        k.xn = ph.sb("xn", [P, NT, D])
        k.xnT = ph.sb("xnT", [P, KD, N])
        k.ctxT = ph.sb("ctxT", [P, KD, N])
        k.identf = ph.sb("identf", [P, P])
        k.identb = ph.sb("identb", [P, P], BF16)
        k.before = ph.sb("before", [P, P], BF16)
        k.onesb = ph.sb("onesb", [P, P], BF16)
        k.iota = ph.sb("iota", [P, 32])
        k.half = ph.sb("half", [P, NT])
        k.qstack = nc.dram_tensor("qstack", (H, SR, N), BF16, kind="Internal").ap()
        k.kstack = nc.dram_tensor("kstack", (H, SR, N), BF16, kind="Internal").ap()
        k.xg = nc.dram_tensor("xg", (8 * 640, D), F32, kind="Internal").ap()
        k.yg = nc.dram_tensor("yg", (8 * 640, D), F32, kind="Internal").ap()
        k.scattered = ph.sem("scattered")
        k.gathered = [ph.sem(f"gathered{i}") for i in range(GATHERS)]
        k.n_scattered = k.n_gathered = 0
        setup_phase(nc, k, io)
        clear_semaphores(nc)
        stage_list = [
            lambda: heads_attention(nc, k, io, 0),
            lambda: moe(nc, k, io, 0),
            lambda: heads_attention(nc, k, io, 1, rope=True),
            lambda: moe(nc, k, io, 1),
            lambda: heads_attention(nc, k, io, 2, masked=True),
            lambda: moe(nc, k, io, 2),
            lambda: whole_attention(nc, k, io),
            lambda: moe(nc, k, io, 3),
        ]
        for s, stage in enumerate(stage_list[:stages]):
            if s < start:
                continue
            layernorm_phase(nc, k, f"ln{s}")
            stage()
            clear_semaphores(nc)
        store_phase(nc, k, out)


def store_phase(nc, k, out):
    with nc.semaphore("stored") as stored, nc.Block() as block:

        @block.sync
        def _(sp):
            sp.dma_start(out.rearrange("b (t p) d -> p (b t) d", p=P), k.x[:]).then_inc(stored, 16)
            sp.wait_ge(stored, 16)



def laid_out(inputs):
    f = {n: np.ascontiguousarray(a) for n, a in inputs.items()}
    io = {n: f[n] for n in ("x", "ctx_1024", "fside_BxSxS2_0", "mask_Bx1xSxS2_ik0")}

    def column(a, n=KD):
        return np.ascontiguousarray(a.reshape(n, P).T)

    def beside(a, axis):
        return np.concatenate([a, np.zeros_like(a)], axis=axis)

    turn = np.arange(D).reshape(H, 2, DH // 2)[:, ::-1].reshape(D)
    for layer in range(3):
        pre = f"L{layer}_xattn_"
        for w in ("Wq", "Wk", "Wv"):
            io[pre + w] = np.ascontiguousarray(f[pre + w].T)
        for b in ("bq", "bk"):
            io[pre + b] = column(f[pre + b])
        if layer == 1:
            for w in ("Wq", "Wk"):
                io[pre + w + "_turn"] = np.ascontiguousarray(f[pre + w][turn].T)
            for b in ("bq", "bk"):
                io[pre + b + "_turn"] = column(f[pre + b][turn])
        wo = beside(f[pre + "Wo"].T.reshape(NG, GH, DH, D), 2)
        wo[0, 0, DH] = f[pre + "bo"]
        io[pre + "Wo"] = np.ascontiguousarray(wo.reshape(NG, P, D))
        io[pre + "bv"] = column(beside(f[pre + "bv"].reshape(NG, GH, DH), 2).reshape(-1), NG)
    io.update(ffn_layout(f))
    io.update(constants())
    return io


def constants():
    c = {}
    c["c_identf"] = np.eye(P, dtype=np.float32)
    p = np.arange(P)
    row = np.arange(3 * H) % H
    c["c_spread"] = np.ascontiguousarray(((row[:, None, None] // NG == p[None, None, :] // HS)
                                          & (row[:, None, None] % NG == np.arange(NG)[None, :, None])).astype(np.float32))
    c["c_before"] = (p[:, None] < p[None, :]).astype(np.float32)
    c["c_iota"] = np.broadcast_to(np.arange(32, dtype=np.float32), (P, 32)).copy()
    c["c_pick"] = np.ascontiguousarray(np.broadcast_to((np.arange(3 * E32)[:, None] % E32 == np.arange(E32)[None, :])[:, :, None],
                                                       (3 * E32, E32, P))).astype(np.float32)
    inv_freq = (1.0 / np.float32(10000.0) ** (np.arange(0, DH, 2, dtype=np.float32) / np.float32(DH))).astype(np.float32)
    pos = (np.float32(10.0) * (np.arange(S, dtype=np.float32) / np.float32(S))).astype(np.float32)
    freqs = np.outer(pos, inv_freq).astype(np.float32)
    cos, sin = np.cos(freqs).T, np.sin(freqs).T
    cos = np.tile(np.concatenate([cos, cos]), (P // DH, 1)).astype(np.float32)
    sin = np.tile(np.concatenate([-sin, sin]), (P // DH, 1)).astype(np.float32)
    c["c_cosk"], c["c_sink"] = cos, sin
    c["c_cosq"], c["c_sinq"] = cos * np.float32(DH ** -0.5), sin * np.float32(DH ** -0.5)
    return c


def kernel(**inputs):
    import concourse.bacc as bacc
    from concourse.bass_utils import run_bass_kernel_spmd

    nc = bacc.Bacc("TRN2", target_bir_lowering=False, num_devices=1)
    arrays = {f"in_{n}": a for n, a in laid_out(inputs).items()}
    io = {n[3:]: nc.dram_tensor(n, a.shape, mybir.dt.from_np(a.dtype), kind="ExternalInput").ap() for n, a in arrays.items()}
    out = nc.dram_tensor("out_x", (B, S, D), F32, kind="ExternalOutput").ap()
    program(nc, io, out)
    r = run_bass_kernel_spmd(nc, [arrays], core_ids=[0])
    return r.results[0]["out_x"]
```

```python
from contextlib import ExitStack

import numpy as np

import concourse.bass as bass
from concourse import mybir
from concourse.alu_op_type import AluOpType as ALU

ACT = mybir.ActivationFunctionType
F32 = mybir.dt.float32
BF16 = mybir.dt.bfloat16
F32R = mybir.dt.float32r
I32 = mybir.dt.int32
U32 = mybir.dt.uint32
AX = mybir.AxisListType

P = 128
B, S, D = 4, 512, 256
N = B * S
NT = N // P
KD = D // P
TPB = S // P
H, DH = 16, 16
GH = 4
NG = H // GH
HS = 32
NPROD = 6
SR = NPROD * DH
MR = 3
EPS = 1e-5
NEG = -float(2 ** 100)


class Phase:

    def __init__(self, nc, ctx, name):
        self.nc, self.ctx, self.name = nc, ctx, name

    def sb(self, name, shape, dt=F32):
        return self.ctx.enter_context(self.nc.sbuf_tensor(f"{self.name}_{name}", shape, dt))

    def ps(self, name, shape, dt=F32):
        return self.ctx.enter_context(self.nc.psum_tensor(f"{self.name}_{name}", shape, dt))

    def sem(self, name):
        return self.ctx.enter_context(self.nc.semaphore(f"{self.name}_{name}"))


class Pair:

    def __init__(self, high, low):
        self.high, self.low = high, low

    def __getitem__(self, key):
        return Pair(self.high[key], self.low[key])

    @classmethod
    def of(cls, ph, name, shape):
        return cls(ph.sb(name + "_high", shape, F32R), ph.sb(name + "_low", shape, F32R))


def low_part(vector, pair, full):
    return vector.tensor_tensor(pair.low, full, pair.high.bitcast(F32), ALU.subtract)


def product(nc, out, lhsT, rhs, start, stop):
    nc.tensor.matmul(out, lhsT.high, rhs.high, start=start, stop=False, skip_group_check=True)
    nc.tensor.matmul(out, lhsT.high, rhs.low, start=False, stop=False, skip_group_check=True)
    return nc.tensor.matmul(out, lhsT.low, rhs.high, start=False, stop=stop, skip_group_check=True)


def clear_semaphores(nc):
    free = sorted(nc.free_semaphores)
    runs = [[free[0], free[0] + 1]]
    for n in free[1:]:
        if n == runs[-1][1]:
            runs[-1][1] = n + 1
        else:
            runs.append([n, n + 1])
    for a, b in runs:
        nc.gpsimd.sem_clear(range(a, b))
    nc.all_engine_barrier()


class Steps:

    def __init__(self, eng, sem):
        self.eng, self.sem, self.n = eng, sem, 0

    def after(self, ins):
        ins.then_inc(self.sem, 1)
        self.n += 1
        self.eng.wait_ge(self.sem, self.n)



def setup_phase(nc, k, io):
    with ExitStack() as ctx:
        ph = Phase(nc, ctx, "setup")
        ctok = ph.sb("ctok", [P, NT, D])
        zero = ph.sb("zero", [P, 4 * D])
        before = ph.sb("before", [P, P])
        TP = ph.ps("tp", [P, 4, KD, 2 * P])
        x_loaded, ctx_loaded, consts = ph.sem("x_loaded"), ph.sem("ctx_loaded"), ph.sem("consts")
        turned, taken, zeroed, cleared = ph.sem("turned"), ph.sem("taken"), ph.sem("zeroed"), ph.sem("cleared")
        high = ph.sem("high")
        with nc.Block() as block:

            @block.sync
            def _(sp):
                sp.dma_start(k.identf[:], io["c_identf"]).then_inc(consts, 16)
                sp.dma_start(ctok[:], io["ctx_1024"].rearrange("b (t p) d -> p (b t) d", p=P)).then_inc(ctx_loaded, 16)
                sp.dma_start(k.x[:], io["x"].rearrange("b (t p) d -> p (b t) d", p=P)).then_inc(x_loaded, 16)
                sp.dma_start(before[:], io["c_before"]).then_inc(consts, 16)
                sp.dma_start(k.iota[:], io["c_iota"]).then_inc(consts, 16)
                sp.wait_ge(zeroed, 1)
                rows = k.xg.shape[0] // P
                src = zero[:].rearrange("p (r d) -> p r d", d=D)
                dst = k.xg.rearrange("(r p) d -> p r d", p=P)
                for r in range(0, rows, 4):
                    sp.dma_start(dst[:, r:r + 4, :], src).then_inc(cleared, 16)
                sp.wait_ge(consts, 16 * 3)
                sp.wait_ge(x_loaded, 16)
                sp.wait_ge(cleared, 16 * (rows // 4))

            @block.gpsimd
            def _(pool):
                nc.gpsimd.memset(zero[:], 0.0).then_inc(zeroed, 1)
                nc.gpsimd.memset(k.half[:], -0.5)
                nc.gpsimd.memset(k.onesb[:], 1.0)

            @block.tensor
            def _(pe):
                pe.wait_ge(consts, 16 * 3)
                pe.wait_ge(ctx_loaded, 16)
                for p in range(NT // 2):
                    if p >= 4:
                        pe.wait_ge(taken, p - 3)
                    for i in range(2):
                        for c in range(KD):
                            mm = nc.tensor.transpose(TP[:, p % 4, c, i * P:(i + 1) * P],
                                                     ctok[:, 2 * p + i, c * P:(c + 1) * P], k.identf[:])
                    mm.then_inc(turned, 1)

            @block.vector
            def _(dve):
                dve.wait_ge(consts, 16 * 3)
                nc.vector.tensor_copy(k.identb[:], k.identf[:])
                nc.vector.tensor_copy(k.before[:], before[:])
                for p in range(NT // 2):
                    dve.wait_ge(high, p + 1)
                    low_part(nc.vector, k.ctxT[:, :, p * 2 * P:(p + 1) * 2 * P], TP[:, p % 4]).then_inc(taken, 1)

            @block.scalar
            def _(act):
                for p in range(NT // 2):
                    act.wait_ge(turned, p + 1)
                    nc.scalar.copy(k.ctxT.high[:, :, p * 2 * P:(p + 1) * 2 * P], TP[:, p % 4]).then_inc(high, 1)



def layernorm_phase(nc, k, name):
    with ExitStack() as ctx:
        ph = Phase(nc, ctx, name)
        st = ph.sb("st", [P, NT, 6])
        mean, diff, var, rstd = (ph.sb(n, [P, NT]) for n in ("mean", "diff", "var", "rstd"))
        TP = ph.ps("tp", [P, 4, KD, 2 * P])
        dve_step, var_ready, rstd_ready = ph.sem("dve_step"), ph.sem("var_ready"), ph.sem("rstd_ready")
        xn_ready, turned, high, taken = ph.sem("xn_ready"), ph.sem("turned"), ph.sem("high"), ph.sem("taken")
        with nc.Block() as block:

            @block.vector
            def _(dve):
                def take_low(p):
                    dve.wait_ge(high, p + 1)
                    low_part(nc.vector, k.xnT[:, :, p * 2 * P:(p + 1) * 2 * P], TP[:, p % 4]).then_inc(taken, 1)

                step = Steps(dve, dve_step)
                for t in range(NT):
                    ins = nc.vector.bn_stats(st[:, t, :], k.x[:, t, :])
                step.after(ins)
                me, se, mo, so = st[:, :, 1], st[:, :, 2], st[:, :, 4], st[:, :, 5]
                nc.vector.tensor_tensor(mean[:], me, mo, ALU.add)
                nc.vector.tensor_tensor(diff[:], me, mo, ALU.subtract)
                step.after(nc.vector.tensor_tensor(var[:], se, so, ALU.add))
                nc.vector.tensor_scalar(mean[:], mean[:], 0.5, None, ALU.mult)
                nc.vector.tensor_scalar(var[:], var[:], 1.0 / D, EPS, ALU.mult, ALU.add)
                step.after(nc.vector.tensor_tensor(diff[:], diff[:], diff[:], ALU.mult))
                nc.vector.scalar_tensor_tensor(out=var[:], in0=diff[:], scalar=0.25, in1=var[:],
                                               op0=ALU.mult, op1=ALU.add).then_inc(var_ready, 1)
                dve.wait_ge(rstd_ready, 1)
                for t in range(NT):
                    nc.vector.tensor_scalar(k.xn[:, t, :], k.x[:, t, :], mean[:, t:t + 1], rstd[:, t:t + 1],
                                            ALU.subtract, ALU.mult).then_inc(xn_ready, 1)
                    if t % 2 and t > 2:
                        take_low(t // 2 - 1)
                take_low(NT // 2 - 1)

            @block.gpsimd
            def _(pool):
                pool.wait_ge(var_ready, 1)
                nc.gpsimd.tensor_tensor(rstd[:], var[:], k.half[:], ALU.pow).then_inc(rstd_ready, 1)

            @block.tensor
            def _(pe):
                for p in range(NT // 2):
                    pe.wait_ge(xn_ready, 2 * p + 2)
                    if p >= 4:
                        pe.wait_ge(taken, p - 3)
                    for i in range(2):
                        for c in range(KD):
                            mm = nc.tensor.transpose(TP[:, p % 4, c, i * P:(i + 1) * P],
                                                     k.xn[:, 2 * p + i, c * P:(c + 1) * P], k.identf[:])
                    mm.then_inc(turned, 1)

            @block.scalar
            def _(act):
                for p in range(NT // 2):
                    act.wait_ge(turned, p + 1)
                    nc.scalar.copy(k.xnT.high[:, :, p * 2 * P:(p + 1) * 2 * P], TP[:, p % 4]).then_inc(high, 1)



Q_PARTS = (0, 1, 2, 0, 0, 1)
K_PARTS = (0, 0, 0, 1, 2, 1)


def heads_project_phase(nc, k, io, layer, rope):
    pre = f"L{layer}_xattn_"
    with ExitStack() as ctx:
        ph = Phase(nc, ctx, f"proj{layer}")
        names = ["Wq", "Wk", "Wv"] + (["Wq_turn", "Wk_turn"] if rope else [])
        raw = {n: ph.sb(n, [P, KD, D]) for n in names}
        W = {n: Pair.of(ph, n + "p", [P, KD, D]) for n in names}
        biases = ["bq", "bk"] + (["bq_turn", "bk_turn"] if rope else [])
        bias = {n: ph.sb(n, [P, KD]) for n in biases}
        tabs = {n: ph.sb(n, [P, S]) for n in (("cosq", "sinq", "cosk", "sink") if rope else ())}
        full = ph.sb("full", [P, 2, S])
        other = ph.sb("other", [P, 2, S])
        rest = ph.sb("rest", [P, 2, S])
        parts = ph.sb("parts", [P, 2, 3, N], BF16)
        QK = ph.ps("qk", [P, 2, S])
        QK2 = ph.ps("qk2", [P, 2, S])
        VP = ph.ps("vp", [P, 2, 2, D])
        w_loaded, w_high, w_split = ph.sem("w_loaded"), ph.sem("w_high"), ph.sem("w_split")
        qk_ready, qk_taken, v_ready, v_taken = (ph.sem(n) for n in ("qk_ready", "qk_taken", "v_ready", "v_taken"))
        high_ready, rest_ready, mid_ready, low_ready = (ph.sem(n) for n in ("high", "rest", "mid", "low"))
        dve_step = ph.sem("dve_step")
        stored = [ph.sem(f"stored{i}") for i in range(2)]
        units = [("q", m) for m in range(KD)] + [("k", m) for m in range(KD)]
        NC = N // S
        loads = 3 + 2 + (2 + 2 + 4 if rope else 0)
        with nc.Block() as block:

            @block.sync
            def _(sp):
                for n in names:
                    sp.dma_start(raw[n][:], io[pre + n].rearrange("(c p) o -> p c o", p=P)).then_inc(w_loaded, 16)
                for n in biases:
                    sp.dma_start(bias[n][:], io[pre + n]).then_inc(w_loaded, 16)
                for n, t in tabs.items():
                    sp.dma_start(t[:], io["c_" + n]).then_inc(w_loaded, 16)
                for u, (what, m) in enumerate(units):
                    sp.wait_ge(low_ready, NC * (u + 1))
                    dst, order = (k.qstack, Q_PARTS) if what == "q" else (k.kstack, K_PARTS)
                    for r, part in enumerate(order):
                        sp.dma_start(dst[m * 8:(m + 1) * 8, r * DH:(r + 1) * DH, :],
                                     parts[:, u % 2, part, :]).then_inc(stored[u % 2], 16)
                for i in range(2):
                    sp.wait_ge(stored[i], 16 * NPROD * 2)

            @block.tensor
            def _(pe):
                pe.wait_ge(w_split, len(names))
                s = 0
                for what, m in units:
                    src = k.xnT if what == "q" else k.ctxT
                    for c in range(NC):
                        if s >= 2:
                            pe.wait_ge(qk_taken, s - 1)
                        for n, ps in (("W" + what, QK), ("W" + what + "_turn", QK2))[:2 if rope else 1]:
                            for kd in range(KD):
                                mm = product(nc, ps[:, s % 2, :], W[n][:, kd, m * P:(m + 1) * P],
                                             src[:, kd, c * S:(c + 1) * S], kd == 0, kd == KD - 1)
                        mm.then_inc(qk_ready, 1)
                        s += 1
                for t in range(NT // 2):
                    if t >= 2:
                        pe.wait_ge(v_taken, t - 1)
                    for i in range(2):
                        tok = (2 * t + i) * P
                        for kd in range(KD):
                            mm = product(nc, VP[:, t % 2, i, :], k.ctxT[:, kd, tok:tok + P], W["Wv"][:, kd, :],
                                         kd == 0, kd == KD - 1)
                    mm.then_inc(v_ready, 1)

            @block.vector
            def _(dve):
                step = Steps(dve, dve_step)
                for i, n in enumerate(names):
                    dve.wait_ge(w_high, i + 1)
                    low_part(nc.vector, W[n][:], raw[n][:]).then_inc(w_split, 1)
                s = 0
                for what, m in units:
                    for c in range(NC):
                        dve.wait_ge(qk_ready, s + 1)
                        if s >= 2:
                            dve.wait_ge(rest_ready, s - 1)
                        f = full[:, s % 2, :]
                        if rope:
                            nc.vector.scalar_tensor_tensor(out=f, in0=QK[:, s % 2, :], scalar=bias["b" + what][:, m:m + 1],
                                                           in1=tabs["cos" + what][:], op0=ALU.add, op1=ALU.mult)
                            step.after(nc.vector.scalar_tensor_tensor(
                                out=other[:, s % 2, :], in0=QK2[:, s % 2, :], scalar=bias["b" + what + "_turn"][:, m:m + 1],
                                in1=tabs["sin" + what][:], op0=ALU.add, op1=ALU.mult))
                            nc.vector.tensor_tensor(f, f, other[:, s % 2, :], ALU.add).then_inc(qk_taken, 1)
                        else:
                            scale = DH ** -0.5 if what == "q" else 1.0
                            nc.vector.tensor_scalar(f, QK[:, s % 2, :], bias["b" + what][:, m:m + 1], scale,
                                                    ALU.add, ALU.mult).then_inc(qk_taken, 1)
                        s += 1

            @block.scalar
            def _(act):
                act.wait_ge(w_loaded, 16 * loads)
                for n in names:
                    nc.scalar.copy(W[n].high[:], raw[n][:]).then_inc(w_high, 1)
                s = 0
                for u in range(len(units)):
                    if u >= 2:
                        act.wait_ge(stored[u % 2], 16 * NPROD)
                    for c in range(NC):
                        act.wait_ge(qk_taken, s + 1)
                        nc.scalar.copy(parts[:, u % 2, 0, c * S:(c + 1) * S], full[:, s % 2, :]).then_inc(high_ready, 1)
                        act.wait_ge(rest_ready, s + 1)
                        nc.scalar.copy(parts[:, u % 2, 1, c * S:(c + 1) * S], rest[:, s % 2, :]).then_inc(mid_ready, 1)
                        s += 1
                for t in range(NT // 2):
                    act.wait_ge(v_ready, t + 1)
                    nc.scalar.copy(k.V[:, 2 * t:2 * t + 2, :], VP[:, t % 2]).then_inc(v_taken, 1)

            @block.gpsimd
            def _(pool):
                s = 0
                for u in range(len(units)):
                    for c in range(NC):
                        pool.wait_ge(high_ready, s + 1)
                        if s >= 2:
                            pool.wait_ge(low_ready, s - 1)
                        nc.gpsimd.tensor_tensor(rest[:, s % 2, :], full[:, s % 2, :], parts[:, u % 2, 0, c * S:(c + 1) * S],
                                                ALU.subtract).then_inc(rest_ready, 1)
                        pool.wait_ge(mid_ready, s + 1)
                        nc.gpsimd.tensor_tensor(parts[:, u % 2, 2, c * S:(c + 1) * S], rest[:, s % 2, :],
                                                parts[:, u % 2, 1, c * S:(c + 1) * S], ALU.subtract).then_inc(low_ready, 1)
                        s += 1


def mask_phase(nc, k, io):
    with ExitStack() as ctx:
        ph = Phase(nc, ctx, "mask")
        raw = ph.sb("raw", [P, 2, TPB, S], I32)
        TP = ph.ps("tp", [P, 4, 2 * S], BF16)
        loaded = [ph.sem(f"loaded{i}") for i in range(2)]
        pen_ready, turned, taken = ph.sem("pen_ready"), ph.sem("turned"), ph.sem("taken")
        with nc.Block() as block:

            @block.sync
            def _(sp):
                for b in range(B):
                    if b >= 2:
                        sp.wait_ge(pen_ready, b - 1)
                    sp.dma_start(raw[:, b % 2], io["mask_Bx1xSxS2_ik0"][b, 0].rearrange("(t p) s -> p t s", p=P)
                                 ).then_inc(loaded[b % 2], 16)

            @block.vector
            def _(dve):
                for b in range(B):
                    dve.wait_ge(loaded[b % 2], 16 * (b // 2 + 1))
                    nc.vector.tensor_scalar(k.pen[:, b * TPB:(b + 1) * TPB, :], raw[:, b % 2], 0.0, NEG,
                                            ALU.is_equal, ALU.mult).then_inc(pen_ready, 1)

            @block.tensor
            def _(pe):
                for b in range(B):
                    pe.wait_ge(pen_ready, b + 1)
                    for kt in range(TPB):
                        i = b * TPB + kt
                        if i >= 4:
                            pe.wait_ge(taken, i - 3)
                        for qt in range(TPB):
                            mm = nc.tensor.transpose(TP[:, i % 4, qt * P:(qt + 1) * P],
                                                     k.pen[:, b * TPB + qt, kt * P:(kt + 1) * P], k.identb[:])
                        mm.then_inc(turned, 1)

            @block.scalar
            def _(act):
                for i in range(NT):
                    act.wait_ge(turned, i + 1)
                    nc.scalar.copy(k.penT[:, i, :], TP[:, i % 4, 0:S]).then_inc(taken, 1)


def heads_attend_phase(nc, k, layer, masked):
    with ExitStack() as ctx:
        ph = Phase(nc, ctx, f"att{layer}")
        Qs = ph.sb("Qs", [P, NG, GH, S], BF16)
        Ks = ph.sb("Ks", [P, NG, GH, S], BF16)
        Vg = ph.sb("Vg", [P, NG, TPB, GH, HS])
        probs = ph.sb("probs", [P, 2, GH, S])
        M = ph.sb("M", [P, 2, GH * TPB])
        pen = ph.sb("pen", [P, 2, TPB, S], BF16) if masked else None
        masked_scores = ph.sb("masked_scores", [P, 2, S]) if masked else None
        waiter = ph.sb("waiter", [P, GH * TPB])
        pen_copied = [ph.sem(f"pen_copied{i}") for i in range(2)]
        rest = ph.sb("rest", [P, GH * TPB])
        mparts = ph.sb("mparts", [P, 2, P], BF16)
        mT = ph.sb("mT", [MR * GH * TPB, 2, P], BF16)
        SA = ph.ps("SA", [P, 2, S])
        ST = ph.ps("ST", [P, 2, 2, S])
        O = ph.ps("O", [P, S])
        MT = ph.ps("MT", [P, 2 * S], BF16)
        qk_loaded = [ph.sem(f"qk_loaded{g}") for g in range(NG)]
        m_loaded = [ph.sem(f"m_loaded{g}") for g in range(NG)]
        v_copied = [ph.sem(f"v_copied{g}") for g in range(NG)]
        set_up = ph.sem("set_up")
        sa_ready, sa_free, split = ph.sem("sa_ready"), ph.sem("sa_free"), ph.sem("split")
        m_turned, m_copied = ph.sem("m_turned"), ph.sem("m_copied")
        st_ready, exp_done, pv_done, o_copied = (ph.sem(n) for n in ("st_ready", "exp_done", "pv_done", "o_copied"))
        SPLIT = 4
        UA = GH * TPB

        def later(b, g, d):
            return b + (g + d) // NG, (g + d) % NG

        with nc.Block() as block:

            @block.sync
            def _(sp):
                def load_stacks(b, g):
                    sp.dma_start(Qs[0:SR, g], k.qstack[g * GH:(g + 1) * GH, :, bass.ds(b * S, S)].rearrange("h r t -> r h t")
                                 ).then_inc(qk_loaded[g], 16)
                    sp.dma_start(Ks[0:SR, g], k.kstack[g * GH:(g + 1) * GH, :, bass.ds(b * S, S)].rearrange("h r t -> r h t")
                                 ).then_inc(qk_loaded[g], 16)

                def place_maxima(b, g):
                    sp.wait_ge(m_copied, b * NG + g + 2)
                    sp.dma_start(Qs[SR:SR + MR, g], mT[:, g % 2, :]).then_inc(m_loaded[g], 16)

                def copy_pen(b, half):
                    sp.dma_start(pen[:, half], k.pen[:, bass.ds(b * TPB, TPB), :]).then_inc(pen_copied[half], 16)

                def group(b, g, last):
                    if masked and not last and g in (0, 2):
                        sp.wait_ge(sa_free, b * (NG * UA) + (g + 2) * UA + 2)
                        copy_pen(b + 1, g // 2)
                    if not (last and g == NG - 1):
                        place_maxima(*later(b, g, 1))
                    if not last:
                        sp.wait_ge(st_ready, b * (8 * NG) + 8 * (g + 1))
                        load_stacks(b + 1, g)

                for g in range(NG):
                    load_stacks(0, g)
                if masked:
                    for half in range(2):
                        copy_pen(0, half)
                place_maxima(0, 0)
                with sp.Fori(0, B - 1) as b:
                    for g in range(NG):
                        group(b, g, False)
                for g in range(NG):
                    group(B - 1, g, True)

            @block.tensor
            def _(pe):
                def maxima_scores(b, g, j, qt):
                    if j == 0 and qt == 0:
                        pe.wait_ge(qk_loaded[g], 32 * b + 32)
                    pe.wait_ge(sa_free, b * (NG * UA) + g * UA + j * TPB + qt + 1)
                    mm = nc.tensor.matmul(SA[:, qt % 2, :], Qs[0:SR, g, j, qt * P:(qt + 1) * P], Ks[0:SR, g, j, :],
                                          start=True, stop=True)
                    mm.then_inc(sa_ready, 1)

                def turn_maxima(b, g):
                    pe.wait_ge(split, b * (NG * SPLIT) + SPLIT * (g + 1))
                    pe.wait_ge(m_copied, b * NG + g + 1)
                    nc.tensor.transpose(MT[:, 0:P], mparts[:, g % 2, :], k.identb[:]
                                        ).then_inc(m_turned, 1)

                def turned_scores(b, g, kt, pair):
                    if kt == 0 and pair == 0:
                        pe.wait_ge(m_loaded[g], 16 * b + 16)
                    pe.wait_ge(exp_done, b * (8 * NG) + 8 * g + 2 * kt + pair + 1)
                    for i in range(2):
                        j = 2 * pair + i
                        mm = nc.tensor.matmul(ST[:, pair, i, :], Ks[0:SR + MR, g, j, kt * P:(kt + 1) * P],
                                              Qs[0:SR + MR, g, j, :], start=True, stop=not masked)
                        if masked:
                            mm = nc.tensor.matmul(ST[:, pair, i, :], k.identb[:], k.penT[:, b * TPB + kt, :],
                                                  start=False, stop=True)
                    mm.then_inc(st_ready, 1)

                def weigh_values(b, g, kt, heads):
                    for j in heads:
                        if kt == 0 and j == 0:
                            pe.wait_ge(o_copied, b * NG + g + 1)
                            pe.wait_ge(v_copied[g], b + 1)
                        if j % 2 == 0:
                            pe.wait_ge(exp_done, b * (8 * NG) + 8 * g + 2 * kt + j // 2 + 3)
                        mm = nc.tensor.matmul(O[j * HS:(j + 1) * HS, :], Vg[:, g, kt, j, :], probs[:, kt % 2, j, :],
                                              start=(kt == 0), stop=(kt == TPB - 1))
                    if heads[-1] == GH - 1:
                        mm.then_inc(pv_done, 1)

                def group(b, g, last):
                    for kt in range(TPB):
                        ahead = None if last and g >= NG - 2 else later(b, g, 2)
                        for i in range(2):
                            if ahead:
                                maxima_scores(*ahead, kt, i)
                            if kt < TPB - 1:
                                turned_scores(b, g, kt + 1, i)
                            elif not (last and g == NG - 1):
                                turned_scores(*later(b, g, 1), 0, i)
                        if ahead:
                            maxima_scores(*ahead, kt, 2)
                        weigh_values(b, g, kt, (0,))
                        if ahead:
                            maxima_scores(*ahead, kt, 3)
                        weigh_values(b, g, kt, (1, 2, 3))
                        if kt == 0 and not (last and g == NG - 1):
                            turn_maxima(*later(b, g, 1))

                pe.sem_inc(pv_done, 2)
                pe.wait_ge(set_up, 2)
                for j in range(GH):
                    for qt in range(TPB):
                        maxima_scores(0, 0, j, qt)
                for j in range(GH):
                    for qt in range(TPB):
                        maxima_scores(0, 1, j, qt)
                    if j == 0:
                        turn_maxima(0, 0)
                for pair in range(2):
                    turned_scores(0, 0, 0, pair)
                with pe.Fori(0, B - 1) as b:
                    for g in range(NG):
                        group(b, g, False)
                for g in range(NG):
                    group(B - 1, g, True)

            @block.vector
            def _(dve):
                def maxima(b, g, j):
                    if masked and j == 0:
                        dve.wait_ge(pen_copied[g // 2], b * 16 + 16)
                    for qt in range(TPB):
                        dve.wait_ge(sa_ready, b * (NG * UA) + g * UA + j * TPB + qt + 1)
                        c = j * TPB + qt
                        if masked:
                            nc.vector.memset(waiter[:, c:c + 1], 0.0)
                            ins = nc.vector.tensor_tensor_reduce(masked_scores[:, qt % 2, :], SA[:, qt % 2, :],
                                                                 pen[:, g // 2, qt, :], 1.0, 2 * NEG, ALU.add, ALU.max,
                                                                 M[:, g % 2, c:c + 1])
                        else:
                            ins = nc.vector.tensor_reduce(M[:, g % 2, c:c + 1], SA[:, qt % 2, :], AX.X, ALU.max)
                        ins.then_inc(sa_free, 1)

                def split_maxima(b, g):
                    m = M[:, g % 2, :]
                    parts = mparts[:, g % 2, 0:MR * UA].rearrange("p (a c) -> p a c", c=UA)
                    done = b * (NG * SPLIT) + SPLIT * g
                    dve.wait_ge(sa_free, b * (NG * UA) + (g + 1) * UA + 2)
                    nc.vector.tensor_scalar(parts[:, 0, :], m, -1.0, None, ALU.mult).then_inc(split, 1)
                    dve.wait_ge(split, done + 1)
                    nc.vector.scalar_tensor_tensor(out=rest[:], in0=m, scalar=-1.0, in1=parts[:, 0, :],
                                                   op0=ALU.mult, op1=ALU.subtract).then_inc(split, 1)
                    dve.wait_ge(split, done + 2)
                    nc.vector.tensor_copy(parts[:, 1, :], rest[:]).then_inc(split, 1)
                    dve.wait_ge(split, done + 3)
                    nc.vector.tensor_tensor(parts[:, 2, :], rest[:], parts[:, 1, :], ALU.subtract).then_inc(split, 1)

                def group(b, g):
                    for j in range(GH):
                        maxima(b, g, j)
                    split_maxima(b, g)

                dve.sem_inc(sa_free, 2)
                nc.vector.memset(Ks[SR:SR + MR], 1.0)
                nc.vector.memset(mparts[:], 0.0)
                nc.vector.memset(Vg[:], 0.0).then_inc(set_up, 1)
                dve.wait_ge(set_up, 1)
                nc.vector.memset(Vg[:, :, :, :, DH:DH + 1], 1.0).then_inc(set_up, 1)
                group(0, 0)
                group(0, 1)
                with dve.Fori(0, B - 1) as b:
                    for g in range(NG):
                        group(*later(b, g, 2))
                for g in range(NG - 2):
                    group(*later(B - 1, g, 2))

            @block.scalar
            def _(act):
                def exponentials(b, g, kt):
                    for pair in range(2):
                        act.wait_ge(st_ready, b * (8 * NG) + 8 * g + 2 * kt + pair + 1)
                        act.wait_ge(pv_done, b * (NG * TPB) + g * TPB + kt + 1)
                        nc.scalar.activation(probs[:, kt % 2, 2 * pair:2 * pair + 2, :], ST[:, pair], ACT.Exp
                                             ).then_inc(exp_done, 1)

                def copy_maxima(b, g):
                    act.wait_ge(m_turned, b * NG + g + 1)
                    nc.scalar.copy(mT[:, g % 2, :], MT[0:MR * UA, 0:P]).then_inc(m_copied, 1)

                def copy_out(b, g):
                    act.wait_ge(pv_done, b * (NG * TPB) + (g + 1) * TPB + 2)
                    nc.scalar.copy(k.AO[:, g, bass.ds(b * S, S)], O[:]).then_inc(o_copied, 1)

                def group(b, g, last):
                    for kt in range(TPB):
                        if kt < TPB - 1:
                            exponentials(b, g, kt + 1)
                        elif not (last and g == NG - 1):
                            exponentials(*later(b, g, 1), 0)
                        if kt == 1 and not (last and g == NG - 1):
                            copy_maxima(*later(b, g, 1))
                    copy_out(b, g)

                act.sem_inc(exp_done, 2)
                act.sem_inc(m_copied, 1)
                act.sem_inc(o_copied, 1)
                copy_maxima(0, 0)
                exponentials(0, 0, 0)
                with act.Fori(0, B - 1) as b:
                    for g in range(NG):
                        group(b, g, False)
                for g in range(NG):
                    group(B - 1, g, True)

            @block.gpsimd
            def _(pool):
                def copy_values(b, g):
                    src = k.V[:, bass.ds(b * TPB, TPB), g * GH * DH:(g + 1) * GH * DH]
                    nc.gpsimd.tensor_copy(Vg[:, g, :, :, 0:DH], src.rearrange("p t (j d) -> p t j d", d=DH)
                                          ).then_inc(v_copied[g], 1)

                pool.wait_ge(set_up, 2)
                for g in range(NG):
                    copy_values(0, g)
                with pool.Fori(0, B - 1) as b:
                    for g in range(NG):
                        pool.wait_ge(pv_done, b * (NG * TPB) + (g + 1) * TPB + 2)
                        copy_values(b + 1, g)


def heads_output_phase(nc, k, io, layer):
    pre = f"L{layer}_xattn_"
    A = P // H
    W = N // A
    with ExitStack() as ctx:
        ph = Phase(nc, ctx, f"out{layer}")
        raw = ph.sb("raw", [P, NG, D])
        Wo = Pair.of(ph, "Wo", [P, NG, D])
        out = Pair.of(ph, "out", [P, 2, NG, S])
        bv = ph.sb("bv", [P, NG])
        spread = ph.sb("spread", [3 * H, NG, P])
        spreadb = ph.sb("spreadb", [3 * H, NG, P], BF16)
        sums = ph.sb("sums", [P, W])
        inv = ph.sb("inv", [P, W])
        parts = ph.sb("parts", [P, 3, W], BF16)
        rows = ph.sb("rows", [3 * H, N], BF16)
        R = ph.ps("R", [P, 2, S])
        Y = ph.ps("Y", [P, 4, S])
        loaded, spread_ready, r_ready, scaled, high, split, y_ready, added, dve_step, w_high = (
            ph.sem(n) for n in ("loaded", "spread_ready", "r_ready", "scaled", "high", "split", "y_ready", "added",
                                "dve_step", "w_high"))
        sums_there, rows_there, part_ready = (ph.sem(n) for n in ("sums_there", "rows_there", "part_ready"))

        def move_sums(eng, heads):
            for h in heads:
                j, g = h // NG, h % NG
                row = j * HS + DH
                eng.dma_start(sums[h * A:(h + 1) * A, :], k.AO[row:row + 1, g, :]).then_inc(sums_there, 16)

        with nc.Block() as block:

            @block.sync
            def _(sp):
                move_sums(sp, range(0, H, 2))
                sp.dma_start(spread[:], io["c_spread"]).then_inc(loaded, 16)
                sp.dma_start(raw[:], io[pre + "Wo"].rearrange("g p o -> p g o")).then_inc(loaded, 16)
                sp.dma_start(bv[:], io[pre + "bv"]).then_inc(loaded, 16)
                for part in range(3):
                    sp.wait_ge(part_ready, part + 1)
                    sp.dma_start(rows[part * H:(part + 1) * H, :], parts[:, part, :]).then_inc(rows_there, 16)
                sp.wait_ge(loaded, 48)

            @block.tensor
            def _(pe):
                def spread_inverses(c, g):
                    u = c * NG + g
                    if u >= 2:
                        pe.wait_ge(scaled, u - 1)
                    nc.tensor.matmul(R[:, u % 2, :], spreadb[:, g, :], rows[:, c * S:(c + 1) * S], start=True, stop=True
                                     ).then_inc(r_ready, 1)

                def project(c):
                    pe.wait_ge(split, NG * (c + 1))
                    for i in range(TPB):
                        t = c * TPB + i
                        if t >= 4:
                            pe.wait_ge(added, t - 3)
                        for g in range(NG):
                            mm = product(nc, Y[:, t % 4, 0:D], out[:, c % 2, g, i * P:(i + 1) * P], Wo[:, g, :],
                                         g == 0, g == NG - 1)
                        mm.then_inc(y_ready, 1)

                pe.wait_ge(loaded, 48)
                pe.wait_ge(spread_ready, 1)
                pe.wait_ge(rows_there, 48)
                for c in range(B):
                    for g in range(NG):
                        spread_inverses(c, g)
                    if c >= 1:
                        project(c - 1)
                project(B - 1)

            @block.vector
            def _(dve):
                v = nc.vector
                step = Steps(dve, dve_step)

                def add_out(c):
                    for t in range(c * TPB, (c + 1) * TPB):
                        dve.wait_ge(y_ready, t + 1)
                        v.tensor_tensor(k.x[:, t, :], k.x[:, t, :], Y[:, t % 4, 0:D], ALU.add).then_inc(added, 1)

                dve.wait_ge(sums_there, 16 * H)
                step.after(v.reciprocal(inv[:], sums[:]))
                v.tensor_copy(parts[:, 0, :], inv[:]).then_inc(part_ready, 1)
                dve.wait_ge(part_ready, 1)
                step.after(v.tensor_tensor(inv[:], inv[:], parts[:, 0, :], ALU.subtract))
                v.tensor_copy(parts[:, 1, :], inv[:]).then_inc(part_ready, 1)
                dve.wait_ge(part_ready, 2)
                v.tensor_tensor(parts[:, 2, :], inv[:], parts[:, 1, :], ALU.subtract).then_inc(part_ready, 1)
                dve.wait_ge(loaded, 48)
                v.tensor_copy(spreadb[:], spread[:])
                dve.wait_ge(w_high, 1)
                low_part(v, Wo[:], raw[:]).then_inc(spread_ready, 1)

                def take_low(u):
                    c, g = u // NG, u % NG
                    o = out[:, c % 2, g, :]
                    dve.wait_ge(high, u + 1)
                    v.scalar_tensor_tensor(out=o.low, in0=k.AO[:, g, c * S:(c + 1) * S], scalar=bv[:, g:g + 1],
                                           in1=o.high.bitcast(F32), op0=ALU.add, op1=ALU.subtract).then_inc(split, 1)

                for c in range(B):
                    for g in range(NG):
                        u = c * NG + g
                        a = k.AO[:, g, c * S:(c + 1) * S]
                        dve.wait_ge(r_ready, u + 1)
                        v.tensor_tensor(a, a, R[:, u % 2, :], ALU.mult).then_inc(scaled, 1)
                        if g:
                            take_low(u - 1)
                    take_low(u)
                    if c >= 1:
                        add_out(c - 1)
                add_out(B - 1)

            @block.scalar
            def _(act):
                move_sums(act, range(1, H, 2))
                act.wait_ge(loaded, 48)
                nc.scalar.copy(Wo.high[:], raw[:]).then_inc(w_high, 1)
                for u in range(B * NG):
                    c, g = u // NG, u % NG
                    act.wait_ge(scaled, u + 1)
                    if g == 0 and c >= 2:
                        act.wait_ge(y_ready, TPB * (c - 1))
                    nc.scalar.activation(out.high[:, c % 2, g, :], k.AO[:, g, c * S:(c + 1) * S], ACT.Identity,
                                         bias=bv[:, g:g + 1]).then_inc(high, 1)


def normalised(nc, k, ctx, name, keep_rows=False):
    ph = Phase(nc, ctx, name + "_kept")
    k.xnT = Pair.of(ph, "xnT", [P, KD, N])
    with ExitStack() as rows:
        k.xn = Phase(nc, ctx if keep_rows else rows, name + "_rows").sb("xn", [P, NT, D])
        layernorm_phase(nc, k, name)


def heads_attention(nc, k, io, layer, rope=False, masked=False):
    with ExitStack() as ctx:
        ph = Phase(nc, ctx, f"heads{layer}")
        k.V = ph.sb("V", [P, NT, D])
        with ExitStack() as inner:
            normalised(nc, k, inner, f"ln_att{layer}")
            heads_project_phase(nc, k, io, layer, rope)
        k.AO = ph.sb("AO", [P, NG, N])
        if masked:
            k.pen = ph.sb("pen", [P, NT, S], BF16)
            k.penT = ph.sb("penT", [P, NT, S], BF16)
            mask_phase(nc, k, io)
        heads_attend_phase(nc, k, layer, masked)
        heads_output_phase(nc, k, io, layer)



def whole_attention(nc, k, io):
    with ExitStack() as ctx:
        ph = Phase(nc, ctx, "whole")
        k.phi = ph.sb("phi", [P, 2, TPB, S])
        k.phi_loaded = [ph.sem(f"phi_loaded{i}") for i in range(2)]
        k.qT, k.kT = (Pair.of(ph, n, [P, KD, N]) for n in ("qT", "kT"))
        k.V = ph.sb("V", [P, NT, D])
        with ExitStack() as inner:
            normalised(nc, k, inner, "ln_whole")
            whole_project_phase(nc, k, io)
        whole_attend_phase(nc, k, io)


def load_phi(sp, k, io, b):
    sp.dma_start(k.phi[:, b % 2], io["fside_BxSxS2_0"][b].rearrange("(t p) s -> p t s", p=P)
                 ).then_inc(k.phi_loaded[b % 2], 16)


def whole_project_phase(nc, k, io):
    pre = "L3_xattn_"
    with ExitStack() as ctx:
        ph = Phase(nc, ctx, "whole_project")
        raw = {n: ph.sb(n, [P, KD, D]) for n in ("Wq", "Wk", "Wv")}
        W = {n: Pair.of(ph, n + "p", [P, KD, D]) for n in raw}
        bias = {n: ph.sb(n, [P, KD]) for n in ("bq", "bk")}
        full = ph.sb("full", [P, 2, S])
        A = ph.ps("A", [P, 4, S])
        loaded = {n: ph.sem(n + "_loaded") for n in raw}
        b_loaded, high, split = ph.sem("b_loaded"), ph.sem("high"), ph.sem("split")
        proj_ready, proj_taken, part_high, part_low = (ph.sem(n) for n in ("proj_ready", "proj_taken", "part_high", "part_low"))
        projections = [(w, m, cc) for w in ("q", "k") for m in range(KD) for cc in range(N // S)]
        NPJ = len(projections)
        with nc.Block() as block:

            @block.sync
            def _(sp):
                for n in raw:
                    sp.dma_start(raw[n][:], io[pre + n].rearrange("(c p) o -> p c o", p=P)).then_inc(loaded[n], 16)
                for n in bias:
                    sp.dma_start(bias[n][:], io[pre + n]).then_inc(b_loaded, 16)
                for b in range(2):
                    load_phi(sp, k, io, b)
                sp.wait_ge(b_loaded, 32)

            @block.tensor
            def _(pe):
                for i, (w, m, cc) in enumerate(projections):
                    src = k.xnT if w == "q" else k.ctxT
                    pe.wait_ge(split, 1 if w == "q" else 2)
                    if i >= 4:
                        pe.wait_ge(proj_taken, i - 3)
                    for kd in range(KD):
                        mm = product(nc, A[:, i % 4, :], W["W" + w][:, kd, m * P:(m + 1) * P],
                                     src[:, kd, cc * S:(cc + 1) * S], kd == 0, kd == KD - 1)
                    mm.then_inc(proj_ready, 1)
                pe.wait_ge(split, 3)
                for t in range(NT):
                    i = NPJ + t
                    pe.wait_ge(proj_taken, i - 3)
                    for kd in range(KD):
                        mm = product(nc, A[:, i % 4, 0:D], k.ctxT[:, kd, t * P:(t + 1) * P], W["Wv"][:, kd, :],
                                     kd == 0, kd == KD - 1)
                    mm.then_inc(proj_ready, 1)

            @block.vector
            def _(dve):
                for i, n in enumerate(raw):
                    dve.wait_ge(high, i + 1)
                    low_part(nc.vector, W[n][:], raw[n][:]).then_inc(split, 1)
                dve.wait_ge(b_loaded, 32)
                for i, (w, m, cc) in enumerate(projections):
                    dve.wait_ge(proj_ready, i + 1)
                    if i >= 2:
                        dve.wait_ge(part_low, i - 1)
                    nc.vector.tensor_scalar(full[:, i % 2, :], A[:, i % 4, :], bias["b" + w][:, m:m + 1],
                                            D ** -0.5 if w == "q" else 1.0, ALU.add, ALU.mult).then_inc(proj_taken, 1)
                for t in range(NT):
                    dve.wait_ge(proj_ready, NPJ + t + 1)
                    nc.vector.tensor_copy(k.V[:, t, :], A[:, (NPJ + t) % 4, 0:D]).then_inc(proj_taken, 1)

            @block.scalar
            def _(act):
                for n in raw:
                    act.wait_ge(loaded[n], 16)
                    nc.scalar.copy(W[n].high[:], raw[n][:]).then_inc(high, 1)
                for i, (w, m, cc) in enumerate(projections):
                    act.wait_ge(proj_taken, i + 1)
                    dst = (k.qT if w == "q" else k.kT)[:, m, cc * S:(cc + 1) * S]
                    nc.scalar.copy(dst.high, full[:, i % 2, :]).then_inc(part_high, 1)

            @block.gpsimd
            def _(pool):
                for i, (w, m, cc) in enumerate(projections):
                    pool.wait_ge(part_high, i + 1)
                    dst = (k.qT if w == "q" else k.kT)[:, m, cc * S:(cc + 1) * S]
                    low_part(nc.gpsimd, dst, full[:, i % 2, :]).then_inc(part_low, 1)


def whole_attend_phase(nc, k, io):
    pre = "L3_xattn_"
    with ExitStack() as ctx:
        ph = Phase(nc, ctx, "whole_attend")
        bv = ph.sb("bv", [P, D])
        beta = ph.sb("beta", [P, 3])
        c01, c = ph.sb("c01", [P, 1]), ph.sb("c", [P, 1])
        att = ph.sb("att", [P, 2, S])
        probs = ph.sb("probs", [P, 2, S])
        probsT = ph.sb("probsT", [P, 2, TPB, P])
        top, ntop = ph.sb("top", [P, NT]), ph.sb("ntop", [P, NT])
        total, inv = ph.sb("total", [P, NT]), ph.sb("inv", [P, NT])
        upd = ph.sb("upd", [P, 2, D])
        A = ph.ps("A", [P, 4, S])
        T = ph.ps("T", [P, 2, TPB, P])
        Y = ph.ps("Y", [P, 2, S])
        loaded, dve_step = ph.sem("loaded"), ph.sem("dve_step")
        s_ready, s_taken, top_ready, exp_done = (ph.sem(n) for n in ("s_ready", "s_taken", "top_ready", "exp_done"))
        turned, turn_taken, y_ready, y_taken = (ph.sem(n) for n in ("turned", "turn_taken", "y_ready", "y_taken"))
        with nc.Block() as block:

            @block.sync
            def _(sp):
                sp.dma_start(beta[:], io[pre + "beta"]).then_inc(loaded, 16)
                sp.dma_start(bv[:], io[pre + "bv"]).then_inc(loaded, 16)
                for b in range(2, B):
                    sp.wait_ge(s_taken, (b - 1) * TPB)
                    load_phi(sp, k, io, b)

            @block.tensor
            def _(pe):
                def scores(t):
                    if t >= 4:
                        pe.wait_ge(s_taken, t - 3)
                    for kd in range(KD):
                        mm = product(nc, A[:, t % 4, :], k.qT[:, kd, t * P:(t + 1) * P],
                                     k.kT[:, kd, (t // TPB) * S:(t // TPB + 1) * S], kd == 0, kd == KD - 1)
                    mm.then_inc(s_ready, 1)

                def turn(t):
                    pe.wait_ge(exp_done, t + 1)
                    if t >= 2:
                        pe.wait_ge(turn_taken, t - 1)
                    for kt in range(TPB):
                        mm = nc.tensor.transpose(T[:, t % 2, kt, :], probs[:, t % 2, kt * P:(kt + 1) * P], k.identf[:])
                    mm.then_inc(turned, 1)

                def weigh(t):
                    pe.wait_ge(turn_taken, t + 1)
                    if t >= 2:
                        pe.wait_ge(y_taken, t - 1)
                    for kt in range(TPB):
                        mm = nc.tensor.matmul(Y[:, t % 2, 0:D], probsT[:, t % 2, kt, :], k.V[:, (t // TPB) * TPB + kt, :],
                                              start=(kt == 0), stop=(kt == TPB - 1))
                    mm.then_inc(y_ready, 1)

                for t in range(NT + 3):
                    if t < NT:
                        scores(t)
                    if 2 <= t < NT + 2:
                        turn(t - 2)
                    if t >= 3:
                        weigh(t - 3)

            @block.vector
            def _(dve):
                step = Steps(dve, dve_step)
                dve.wait_ge(loaded, 32)
                step.after(nc.vector.tensor_tensor(c01[:], beta[:, 0:1], beta[:, 1:2], ALU.add))
                step.after(nc.vector.tensor_tensor(c[:], c01[:], beta[:, 2:3], ALU.subtract))

                def add_out(t):
                    dve.wait_ge(exp_done, t + 1)
                    step.after(nc.vector.reciprocal(inv[:, t:t + 1], total[:, t:t + 1]))
                    dve.wait_ge(y_ready, t + 1)
                    ins = nc.vector.scalar_tensor_tensor(out=upd[:, t % 2, :], in0=Y[:, t % 2, 0:D], scalar=inv[:, t:t + 1],
                                                         in1=bv[:], op0=ALU.mult, op1=ALU.add)
                    ins.then_inc(y_taken, 1)
                    dve.wait_ge(y_taken, t + 1)
                    nc.vector.tensor_tensor(k.x[:, t, :], k.x[:, t, :], upd[:, t % 2, :], ALU.add)

                for t in range(NT):
                    b, i = divmod(t, TPB)
                    if i == 0:
                        dve.wait_ge(k.phi_loaded[b % 2], 16 * (b // 2 + 1))
                    dve.wait_ge(s_ready, t + 1)
                    if t >= 2:
                        dve.wait_ge(exp_done, t - 1)
                    nc.vector.scalar_tensor_tensor(out=att[:, t % 2, :], in0=k.phi[:, b % 2, i, :], scalar=c[:, 0:1],
                                                   in1=A[:, t % 4, :], op0=ALU.mult, op1=ALU.add).then_inc(s_taken, 1)
                    dve.wait_ge(s_taken, t + 1)
                    step.after(nc.vector.tensor_reduce(top[:, t:t + 1], att[:, t % 2, :], AX.X, ALU.max))
                    nc.vector.tensor_scalar(ntop[:, t:t + 1], top[:, t:t + 1], -1.0, None, ALU.mult).then_inc(top_ready, 1)
                    if t >= 3:
                        add_out(t - 3)
                for t in range(NT - 3, NT):
                    add_out(t)

            @block.scalar
            def _(act):
                for t in range(NT):
                    act.wait_ge(top_ready, t + 1)
                    if t >= 2:
                        act.wait_ge(turned, t - 1)
                    nc.scalar.activation(probs[:, t % 2, :], att[:, t % 2, :], ACT.Exp, bias=ntop[:, t:t + 1],
                                         accum_out=total[:, t:t + 1]).then_inc(exp_done, 1)
                    if t >= 1:
                        act.wait_ge(turned, t)
                        nc.scalar.copy(probsT[:, (t - 1) % 2], T[:, (t - 1) % 2]).then_inc(turn_taken, 1)
                act.wait_ge(turned, NT)
                nc.scalar.copy(probsT[:, (NT - 1) % 2], T[:, (NT - 1) % 2]).then_inc(turn_taken, 1)



class Moe:

    def __init__(self, layer, gate, w1, w2, b1, b2, picks, units, size, chunk, func):
        self.layer, self.gate, self.w1, self.w2, self.b1, self.b2 = layer, gate, w1, w2, b1, b2
        self.picks, self.units, self.size, self.chunk, self.func = picks, units, size, chunk, func
        self.slots = units * size


E8 = 8
F = 1024
FT = F // P
CAP2 = int(S / E8 * 1.25)
CAP3 = int(2 * 1.25 * N / E8)
CAP3 += CAP3 % 2
SIZE0 = 2 * P
UNITS0 = (N + E8 * (SIZE0 - 1)) // SIZE0
UNITS0 += UNITS0 % 2
SIZE2 = -(-B * CAP2 // P) * P
MOES = {
    0: Moe(0, "L0_ffn_gate_w", "L0_ffn_w1", "L0_ffn_w2", "L0_ffn_b1", "L0_ffn_b2", 1, UNITS0, SIZE0, SIZE0, ACT.Relu),
    2: Moe(2, "L2_ffn_Wr", "L2_ffn_W1", "L2_ffn_W2", "L2_ffn_b1", "L2_ffn_b2", 2, E8, SIZE2, SIZE2, ACT.Relu),
    3: Moe(3, "L3_ffn_w_g", "L3_ffn_c_fc", "L3_ffn_c_proj", None, None, 2, E8, CAP3, CAP3 // 2, ACT.Gelu),
}
GATHERS = 4
FAR = float(1 << 20)


def logits_products(nc, k, pe, gate, L, E):
    for t in range(NT):
        for kd in range(KD):
            mm = product(nc, L[:, t, :], k.xnT[:, kd, t * P:(t + 1) * P], gate[:, kd, :], kd == 0, kd == KD - 1)
    return mm


def route_phase(nc, k, io, moe, r):
    K = moe.picks
    with ExitStack() as ctx:
        ph = Phase(nc, ctx, f"route{moe.layer}")
        raw = ph.sb("raw", [P, KD, E8])
        gate = Pair.of(ph, "gate", [P, KD, E8])
        gbias = ph.sb("gbias", [P, 2, NT, E8])
        lg = ph.sb("lg", [P, NT, E8])
        tmp = ph.sb("tmp", [P, NT, E8])
        best = ph.sb("best", [P, NT, 8])
        col = ph.sb("col", [P, NT])
        ix = ph.sb("ix", [P, NT, 8], U32)
        ixf = ph.sb("ixf", [P, NT, 8])
        hot = ph.sb("hot", [P, K, NT, E8])
        counted = 1 if moe.layer == 2 else K
        hotb = ph.sb("hotb", [P, counted, NT, E8], BF16)
        rank_in = ph.sb("rank_in", [P, counted, NT, E8])
        tot = ph.sb("tot", [P, counted * NT, E8])
        off = ph.sb("off", [P, counted * NT + 1, E8])
        rank = ph.sb("rank", [P, NT])
        base = ph.sb("base", [P, NT])
        keep = ph.sb("keep", [P, NT])
        slot = ph.sb("slot", [P, NT])
        slot2 = ph.sb("slot2", [P, NT])
        nunit = ph.sb("nunit", [P, E8, 8])
        cnt = ph.sb("cnt", [P, E8])
        uend = ph.sb("uend", [P, E8 + 1])
        utab = ph.sb("utab", [P, moe.units, E8])
        uexp = ph.sb("uexp", [P, moe.units])
        L = ph.ps("L", [P, NT, E8])
        C = ph.ps("C", [P, 512])
        Z = ph.ps("Z", [P, 512])
        gate_split = ph.sem("gate_split")
        loaded, l_ready, hot_ready, c_ready, dve_step, act_done, act_asked = (
            ph.sem(n) for n in ("loaded", "l_ready", "hot_ready", "c_ready", "dve_step", "act_done", "act_asked"))
        biases = {0: 2, 2: 1, 3: 0}[moe.layer]
        per = E8 * NT
        with nc.Block() as block:

            @block.sync
            def _(sp):
                sp.dma_start(raw[:], io[moe.gate].rearrange("(c p) e -> p c e", p=P)).then_inc(loaded, 16)
                if biases:
                    sp.dma_start(gbias[:, 0:biases], io[f"gbias{moe.layer}"]).then_inc(loaded, 16)
                sp.wait_ge(loaded, 16 * (1 + bool(biases)))

            @block.tensor
            def _(pe):
                pe.wait_ge(gate_split, 2)
                logits_products(nc, k, pe, gate, L, E8).then_inc(l_ready, 1)
                pe.wait_ge(hot_ready, 1)
                flat = hotb[:].rearrange("p k t e -> p (k t e)")
                nc.tensor.matmul(C[:, 0:counted * per], k.before[:], flat, start=True, stop=True)
                nc.tensor.matmul(Z[:, 0:counted * per], k.onesb[:], flat, start=True, stop=True).then_inc(c_ready, 1)

            @block.scalar
            def _(act):
                if moe.layer == 2:
                    act.wait_ge(act_asked, 1)
                    nc.scalar.activation(lg[:], tmp[:], ACT.Exp).then_inc(act_done, 1)
                if moe.layer == 3:
                    act.wait_ge(act_asked, 1)
                    nc.scalar.activation(keep[:], col[:], ACT.Exp).then_inc(act_done, 1)

            @block.vector
            def _(dve):
                v = nc.vector
                step = Steps(dve, dve_step)
                wide = [P, NT, E8]

                def over(a):
                    return a.unsqueeze(2).to_broadcast(wide)

                dve.wait_ge(loaded, 16 * (1 + bool(biases)))
                nc.vector.tensor_copy(gate.high[:], raw[:]).then_inc(gate_split, 1)
                dve.wait_ge(gate_split, 1)
                low_part(nc.vector, gate[:], raw[:]).then_inc(gate_split, 1)
                dve.wait_ge(l_ready, 1)
                if biases:
                    step.after(v.tensor_tensor(lg[:], L[:], gbias[:, 0], ALU.add))
                    if biases == 2:
                        step.after(v.tensor_tensor(lg[:], lg[:], gbias[:, 1], ALU.add))
                else:
                    step.after(v.tensor_copy(lg[:], L[:]))
                if moe.layer == 2:
                    step.after(v.tensor_reduce(col[:], lg[:], AX.X, ALU.max))
                    v.tensor_tensor(tmp[:], lg[:], over(col[:]), ALU.subtract).then_inc(act_asked, 1)
                    dve.wait_ge(act_done, 1)
                    step.after(v.tensor_reduce(col[:], lg[:], AX.X, ALU.add))
                    step.after(v.reciprocal(col[:], col[:]))
                    step.after(v.tensor_tensor(lg[:], lg[:], over(col[:]), ALU.mult))
                for t in range(NT):
                    ins = v.max(best[:, t, :], lg[:, t, :])
                step.after(ins)
                for t in range(NT):
                    ins = v.max_index(ix[:, t, :], best[:, t, :], lg[:, t, :])
                step.after(ins)
                step.after(v.tensor_copy(ixf[:], ix[:]))
                if moe.layer == 2:
                    for p in range(K):
                        ins = v.tensor_copy(r.weight[:, p, :], best[:, :, p])
                elif moe.layer == 3:
                    v.tensor_tensor(col[:], best[:, :, 1], best[:, :, 0], ALU.subtract).then_inc(act_asked, 1)
                    dve.wait_ge(act_done, 1)
                    step.after(v.tensor_scalar(col[:], keep[:], 1.0, None, ALU.add))
                    step.after(v.reciprocal(r.weight[:, 0, :], col[:]))
                    ins = v.tensor_tensor(r.weight[:, 1, :], r.weight[:, 0, :], keep[:], ALU.mult)
                else:
                    ins = v.memset(r.weight[:], 1.0)
                step.after(ins)
                iota8 = k.iota[:, 0:E8].unsqueeze(1).to_broadcast(wide)
                for p in range(K):
                    ins = v.tensor_tensor(hot[:, p], iota8, ixf[:, :, p:p + 1].to_broadcast(wide), ALU.is_equal)
                step.after(ins)
                if moe.layer == 2:
                    ins = v.tensor_tensor(hotb[:, 0], hot[:, 0], hot[:, 1], ALU.add)
                else:
                    ins = v.tensor_copy(hotb[:], hot[:])
                ins.then_inc(hot_ready, 1)
                dve.wait_ge(c_ready, 1)
                v.tensor_copy(tot[:], Z[:, 0:counted * per].rearrange("p (t e) -> p t e", e=E8))
                step.after(v.memset(off[:], 0.0))
                for i in range(counted * NT):
                    if moe.layer == 2 and (i + 1) % TPB == 0:
                        continue
                    step.after(v.tensor_tensor(off[:, i + 1, :], off[:, i, :], tot[:, i, :], ALU.add))
                step.after(v.tensor_tensor(rank_in[:].rearrange("p k t e -> p (k t) e"), off[:, 0:counted * NT, :],
                                           C[:, 0:counted * per].rearrange("p (t e) -> p t e", e=E8), ALU.add))
                if moe.layer == 0:
                    step.after(v.tensor_scalar(cnt[:], off[:, NT, :], 1.0 / SIZE0, None, ALU.mult))
                    step.after(v.tensor_tensor(nunit[:], cnt[:].unsqueeze(2).to_broadcast([P, E8, 8]),
                                               k.iota[:, 0:8].unsqueeze(1).to_broadcast([P, E8, 8]), ALU.is_gt))
                    step.after(v.tensor_reduce(cnt[:], nunit[:], AX.X, ALU.add))
                    step.after(v.memset(uend[:], 0.0))
                    for e in range(E8):
                        step.after(v.tensor_tensor(uend[:, e + 1:e + 2], uend[:, e:e + 1], cnt[:, e:e + 1], ALU.add))
                    step.after(v.tensor_tensor(utab[:], k.iota[:, 0:moe.units].unsqueeze(2).to_broadcast([P, moe.units, E8]),
                                               uend[:, 1:].unsqueeze(1).to_broadcast([P, moe.units, E8]), ALU.is_ge))
                    step.after(v.tensor_reduce(uexp[:], utab[:], AX.X, ALU.add))
                    step.after(v.tensor_scalar(uexp[:], uexp[:], E8 - 1.0, None, ALU.min))
                    step.after(v.tensor_copy(r.unit_expert[:], uexp[:]))
                    step.after(v.tensor_tensor(tmp[:], hot[:, 0], uend[:, 0:E8].unsqueeze(1).to_broadcast(wide), ALU.mult))
                    step.after(v.tensor_reduce(base[:], tmp[:], AX.X, ALU.add))
                    step.after(v.tensor_scalar(base[:], base[:], float(SIZE0), None, ALU.mult))
                for p in range(K):
                    step.after(v.tensor_tensor(tmp[:], hot[:, p], rank_in[:, p % counted], ALU.mult))
                    step.after(v.tensor_reduce(rank[:], tmp[:], AX.X, ALU.add))
                    if moe.layer != 0:
                        step.after(v.tensor_scalar(base[:], ixf[:, :, p], float(moe.size), None, ALU.mult))
                    if moe.layer == 2:
                        for b in range(1, B):
                            sl = base[:, b * TPB:(b + 1) * TPB]
                            ins = v.tensor_scalar(sl, sl, float(b * CAP2), None, ALU.add)
                        step.after(ins)
                    cap = {0: float(N + 1), 2: float(CAP2), 3: float(CAP3)}[moe.layer]
                    v.tensor_tensor(slot[:], rank[:], base[:], ALU.add)
                    step.after(v.tensor_scalar(keep[:], rank[:], cap, None, ALU.is_lt))
                    v.tensor_tensor(r.weight[:, p, :], r.weight[:, p, :], keep[:], ALU.mult)
                    step.after(v.tensor_tensor(slot[:], slot[:], keep[:], ALU.mult))
                    v.tensor_copy(r.take[:, p, :], slot[:])
                    step.after(v.tensor_scalar(keep[:], keep[:], -FAR, FAR, ALU.mult, ALU.add))
                    step.after(v.tensor_tensor(slot2[:], slot[:], keep[:], ALU.add))
                    step.after(v.tensor_copy(r.put[:, p, :], slot2[:]))


class Matrices:

    def __init__(self, ph):
        self.raw1, self.raw2 = ph.sb("raw1", [P, 2, KD, F]), ph.sb("raw2", [P, 2, FT, D])
        self.W1, self.W2 = Pair.of(ph, "W1", [P, 2, KD, F]), Pair.of(ph, "W2", [P, 2, FT, D])


def unit_expert(sp, moe, r, u):
    if moe.layer == 0:
        return sp.value_load(r.unit_expert[0:1, bass.ds(u, 1)], min_val=0, max_val=E8 - 1)
    return u


def first_matrix(io, moe, e):
    return io[moe.w1][bass.ds(e, 1)].rearrange("e (c p) f -> p (e c) f", p=P)


def second_matrix(io, moe, e):
    return io[moe.w2][bass.ds(e, 1)].rearrange("e (f p) d -> p (e f) d", p=P)


def dispatch_phase(nc, k, io, moe, r, m):
    k.n_scattered += NT * moe.picks
    with ExitStack() as ctx:
        ph = Phase(nc, ctx, f"dispatch{moe.layer}")
        loaded = [ph.sem(f"loaded{w}") for w in (1, 2)]
        high, split = ph.sem("high"), ph.sem("split")
        matrices = ((m.raw1, m.W1), (m.raw2, m.W2))
        block = ctx.enter_context(nc.Block())

        @block.sync
        def _(sp):
            e = unit_expert(sp, moe, r, 0)
            sp.dma_start(m.raw1[:, 0], first_matrix(io, moe, e)).then_inc(loaded[0], 16)
            sp.dma_start(m.raw2[:, 0], second_matrix(io, moe, e)).then_inc(loaded[1], 16)

        @block.scalar
        def _(act):
            for w, (raw, W) in enumerate(matrices):
                act.wait_ge(loaded[w], 16)
                nc.scalar.copy(W.high[:, 0], raw[:, 0]).then_inc(high, 1)

        @block.vector
        def _(dve):
            for w, (raw, W) in enumerate(matrices):
                dve.wait_ge(high, w + 1)
                low_part(nc.vector, W[:, 0], raw[:, 0]).then_inc(split, 1)
            dve.wait_ge(split, 2)

        @block.gpsimd
        def _(pool):
            for t in range(NT):
                for p in range(moe.picks):
                    pool.indirect_dma_start(out=k.xg[0:moe.slots, :],
                                            out_offset=bass.IndirectOffsetOnAxis(ap=r.put[:, p, t:t + 1], axis=0),
                                            in_=k.xn[:, t, :], in_offset=None, bounds_check=moe.slots - 1,
                                            oob_is_err=False).then_inc(k.scattered, 16)
            pool.wait_ge(k.scattered, 16 * k.n_scattered)


def combine_phase(nc, k, moe, r):
    with ExitStack() as ctx:
        ph = Phase(nc, ctx, f"combine{moe.layer}")
        g = ph.sb("g", [P, GATHERS, D])
        added = ph.sem("added")
        todo = [(t, p) for t in range(NT) for p in range(moe.picks)]
        before = k.n_gathered
        k.n_gathered += len(todo) // GATHERS
        with nc.Block() as block:

            @block.gpsimd
            def _(pool):
                for i, (t, p) in enumerate(todo):
                    if i >= GATHERS:
                        pool.wait_ge(added, i - GATHERS + 1)
                    pool.indirect_dma_start(out=g[:, i % GATHERS, :], out_offset=None, in_=k.yg[0:moe.slots, :],
                                            in_offset=bass.IndirectOffsetOnAxis(ap=r.take[:, p, t:t + 1], axis=0),
                                            bounds_check=moe.slots - 1, oob_is_err=False
                                            ).then_inc(k.gathered[i % GATHERS], 16)

            @block.vector
            def _(dve):
                for i, (t, p) in enumerate(todo):
                    dve.wait_ge(k.gathered[i % GATHERS], 16 * (before + i // GATHERS + 1))
                    if p:
                        dve.wait_ge(added, i)
                    nc.vector.scalar_tensor_tensor(out=k.x[:, t, :], in0=g[:, i % GATHERS, :],
                                                   scalar=r.weight[:, p, t:t + 1], in1=k.x[:, t, :],
                                                   op0=ALU.mult, op1=ALU.add).then_inc(added, 1)


def experts_phase(nc, k, io, moe, r, m):
    n_t = moe.size // P
    CH = moe.chunk
    n_ch = moe.size // CH
    biased = moe.b1 is not None
    HR = 4
    with ExitStack() as ctx:
        ph = Phase(nc, ctx, f"experts{moe.layer}")
        raw1, raw2, W1, W2 = m.raw1, m.raw2, m.W1, m.W2
        b1 = ph.sb("b1", [P, 2, FT])
        b2 = ph.sb("b2", [P, 2, D])
        xg = ph.sb("xg", [P, 2, n_t, D])
        xgT = Pair.of(ph, "xgT", [P, 2, KD, moe.size])
        h = ph.sb("h", [P, HR, CH])
        hT = Pair.of(ph, "hT", [P, FT, moe.size])
        y = ph.sb("y", [P, 2, n_t, D])
        T = ph.ps("T", [P, 2, KD, 2 * P])
        Hb = ph.ps("Hb", [P, HR, S])
        Y = ph.ps("Y", [P, 2, S])
        w1_loaded, w2_loaded = ([ph.sem(f"w{w}_loaded{i}") for i in range(2)] for w in (1, 2))
        w1_high, w2_high, w1_split, w2_split = (ph.sem(n) for n in ("w1_high", "w2_high", "w1_split", "w2_split"))
        x_loaded = [ph.sem(f"x_loaded{i}") for i in range(2)]
        b_loaded = [ph.sem(f"b_loaded{i}") for i in range(2)]
        stored = [ph.sem(f"stored{i}") for i in range(2)]
        turned, turn_high, turn_taken, h_ready, h_taken, h_high, h_split, y_ready, y_taken = (
            ph.sem(n) for n in ("turned", "turn_high", "turn_taken", "h_ready", "h_taken", "h_high", "h_split",
                                "y_ready", "y_taken"))
        HU = FT * n_ch
        PAIRS = moe.units // 2

        def unit_pairs(eng, unit):
            with eng.Fori(0, PAIRS - 1) as pair:
                for i in range(2):
                    unit(pair, i, False)
            for i in range(2):
                unit(PAIRS - 1, i, i == 1)

        with nc.Block() as block:

            @block.sync
            def _(sp):
                def load_matrices(pair, i):
                    e = unit_expert(sp, moe, r, pair * 2 + i)
                    reused = not isinstance(pair, int) or pair > 0
                    if reused:
                        sp.wait_ge(w1_split, pair * 2 + i - 1)
                    sp.dma_start(raw1[:, i], first_matrix(io, moe, e)).then_inc(w1_loaded[i], 16)
                    if reused:
                        sp.wait_ge(w2_split, pair * 2 + i - 1)
                    sp.dma_start(raw2[:, i], second_matrix(io, moe, e)).then_inc(w2_loaded[i], 16)

                def load_tokens(pair, i):
                    if not isinstance(pair, int) or pair > 0:
                        sp.wait_ge(turned, (pair * 2 + i - 1) * n_t)
                    sp.dma_start(xg[:, i], k.xg[bass.ds((pair * 2 + i) * moe.size, moe.size), :]
                                 .rearrange("(t p) d -> p t d", p=P)).then_inc(x_loaded[i], 16)

                def load_biases(pair, i):
                    if biased:
                        e = unit_expert(sp, moe, r, pair * 2 + i)
                        sp.dma_start(b1[:, i, :], io[moe.b1][bass.ds(e, 1)].rearrange("e p f -> p (e f)")
                                     ).then_inc(b_loaded[i], 16)
                        sp.dma_start(b2[:, i, :], io[moe.b2][bass.ds(e, 1)].rearrange("e p d -> p (e d)")
                                     ).then_inc(b_loaded[i], 16)

                def store(pair, i):
                    sp.wait_ge(y_taken, pair * (2 * n_t) + (i + 1) * n_t + 2)
                    sp.dma_start(k.yg[bass.ds((pair * 2 + i) * moe.size, moe.size), :].rearrange("(t p) d -> p t d", p=P),
                                 y[:, i]).then_inc(stored[i], 16)

                def around(pair, i, first=False, last=False):
                    if not last:
                        load_matrices(pair + 1, i)
                        load_tokens(pair + 1, i)
                    if not (first and i == 0):
                        store(pair - 1 + i, 1 - i)
                    if not (last and i == 1):
                        load_biases(pair + i, 1 - i)

                for i in range(2):
                    sp.sem_inc((w1_loaded, w2_loaded)[i][0], 16)
                load_tokens(0, 0)
                load_biases(0, 0)
                load_matrices(0, 1)
                load_tokens(0, 1)
                for i in range(2):
                    around(0, i, first=True)
                with sp.Fori(1, PAIRS - 1) as pair:
                    for i in range(2):
                        around(pair, i)
                for i in range(2):
                    around(PAIRS - 1, i, last=True)
                store(PAIRS - 1, 1)
                for i in range(2):
                    sp.wait_ge(stored[i], 16 * PAIRS + 16)

            @block.tensor
            def _(pe):
                def turn(pair, i, t):
                    j = i * n_t + t
                    if t == 0:
                        pe.wait_ge(x_loaded[i], pair * 16 + 16)
                    pe.wait_ge(turn_taken, pair * (2 * n_t) + j + 1)
                    for c in range(KD):
                        mm = nc.tensor.transpose(T[:, j % 2, c, 0:P], xg[:, i, t, c * P:(c + 1) * P], k.identf[:])
                    mm.then_inc(turned, 1)

                def first(pair, i):
                    pe.wait_ge(w1_split, pair * 2 + i + 1)
                    pe.wait_ge(turn_taken, pair * (2 * n_t) + (i + 1) * n_t + 2)
                    for f in range(FT):
                        for ch in range(n_ch):
                            j = i * HU + f * n_ch + ch
                            pe.wait_ge(h_taken, pair * (2 * HU) + j + 1)
                            for kd in range(KD):
                                mm = product(nc, Hb[:, j % HR, 0:CH], W1[:, i, kd, f * P:(f + 1) * P],
                                             xgT[:, i, kd, ch * CH:(ch + 1) * CH], kd == 0, kd == KD - 1)
                            mm.then_inc(h_ready, 1)

                def second(pair, i, last):
                    pe.wait_ge(w2_split, pair * 2 + i + 1)
                    for t in range(n_t):
                        if not last:
                            turn(pair + i, 1 - i, t)
                        j = i * n_t + t
                        pe.wait_ge(y_taken, pair * (2 * n_t) + j + 1)
                        for f in range(FT):
                            if t == 0:
                                pe.wait_ge(h_split, pair * (2 * HU) + i * HU + (f + 1) * n_ch + HR)
                            mm = product(nc, Y[:, j % 2, 0:D], hT[:, f, t * P:(t + 1) * P], W2[:, i, f, :],
                                         f == 0, f == FT - 1)
                        mm.then_inc(y_ready, 1)

                def unit(pair, i, last):
                    first(pair, i)
                    second(pair, i, last)

                for t in range(n_t):
                    turn(0, 0, t)
                unit_pairs(pe, unit)

            @block.scalar
            def _(act):
                def matrix_high(pair, i, which):
                    raw, W, loaded, high = ((raw1, W1, w1_loaded, w1_high), (raw2, W2, w2_loaded, w2_high))[which]
                    act.wait_ge(loaded[i], pair * 16 + 16)
                    nc.scalar.copy(W.high[:, i], raw[:, i]).then_inc(high, 1)

                def hidden(pair, i):
                    if biased:
                        act.wait_ge(b_loaded[i], pair * 32 + 32)
                    for f in range(FT):
                        for ch in range(n_ch):
                            j = i * HU + f * n_ch + ch
                            act.wait_ge(h_ready, pair * (2 * HU) + j + 1)
                            act.wait_ge(h_split, pair * (2 * HU) + j + 1)
                            nc.scalar.activation(h[:, j % HR, :], Hb[:, j % HR, 0:CH], moe.func,
                                                 bias=b1[:, i, f:f + 1] if biased else 0.0).then_inc(h_taken, 1)

                def turned_high(pair, i, tiles):
                    for t in tiles:
                        j = i * n_t + t
                        act.wait_ge(turned, pair * (2 * n_t) + j + 1)
                        nc.scalar.copy(xgT.high[:, i, :, t * P:(t + 1) * P], T[:, j % 2, :, 0:P]).then_inc(turn_high, 1)

                def unit(pair, i, last):
                    if not last:
                        matrix_high(pair + i, 1 - i, 0)
                    hidden(pair, i)
                    if not last:
                        turned_high(pair + i, 1 - i, range(n_t - 1))
                        matrix_high(pair + i, 1 - i, 1)
                        turned_high(pair + i, 1 - i, [n_t - 1])

                act.sem_inc(h_taken, HR)
                act.sem_inc(w1_high, 1)
                act.sem_inc(w2_high, 1)
                turned_high(0, 0, range(n_t))
                unit_pairs(act, unit)

            @block.gpsimd
            def _(pool):
                def unit(pair, i, last):
                    if not last:
                        pool.wait_ge(w1_high, (pair + i) * 2 + (1 - i) + 1)
                        low_part(nc.gpsimd, W1[:, 1 - i], raw1[:, 1 - i]).then_inc(w1_split, 1)

                pool.sem_inc(w1_split, 1)
                unit_pairs(pool, unit)

            @block.vector
            def _(dve):
                def cut_hidden(pair, i):
                    def part(n):
                        f, ch = divmod(n, n_ch)
                        return hT[:, f, ch * CH:(ch + 1) * CH]

                    for n in range(HU + 1):
                        j = i * HU + n
                        if n < HU:
                            dve.wait_ge(h_taken, pair * (2 * HU) + j + 1 + HR)
                            nc.vector.tensor_copy(part(n).high, h[:, j % HR, :]).then_inc(h_high, 1)
                        if n:
                            dve.wait_ge(h_high, pair * (2 * HU) + j)
                            low_part(nc.vector, part(n - 1), h[:, (j - 1) % HR, :]).then_inc(h_split, 1)

                def take_turned(pair, i, t):
                    j = i * n_t + t
                    dve.wait_ge(turn_high, pair * (2 * n_t) + j + 1)
                    low_part(nc.vector, xgT[:, i, :, t * P:(t + 1) * P], T[:, j % 2, :, 0:P]).then_inc(turn_taken, 1)

                def take_out(pair, i, t):
                    j = i * n_t + t
                    if t == 0:
                        dve.wait_ge(stored[i], pair * 16 + 16)
                        if biased:
                            dve.wait_ge(b_loaded[i], pair * 32 + 32)
                    dve.wait_ge(y_ready, pair * (2 * n_t) + j + 1)
                    if biased:
                        ins = nc.vector.tensor_tensor(y[:, i, t, :], Y[:, j % 2, 0:D], b2[:, i, :], ALU.add)
                    else:
                        ins = nc.vector.tensor_copy(y[:, i, t, :], Y[:, j % 2, 0:D])
                    ins.then_inc(y_taken, 1)

                def matrix_low(pair, i):
                    dve.wait_ge(w2_high, pair * 2 + i + 1)
                    low_part(nc.vector, W2[:, i], raw2[:, i]).then_inc(w2_split, 1)

                def unit(pair, i, last):
                    cut_hidden(pair, i)
                    out = 0
                    if not last:
                        for t in range(n_t - 1):
                            take_turned(pair + i, 1 - i, t)
                            if t:
                                take_out(pair, i, out)
                                out += 1
                        matrix_low(pair + i, 1 - i)
                        take_turned(pair + i, 1 - i, n_t - 1)
                    for t in range(out, n_t):
                        take_out(pair, i, t)

                for i in range(2):
                    dve.sem_inc(stored[i], 16)
                dve.sem_inc(turn_taken, 2)
                dve.sem_inc(y_taken, 2)
                dve.sem_inc(h_split, HR)
                dve.sem_inc(w2_split, 1)
                for t in range(n_t):
                    take_turned(0, 0, t)
                unit_pairs(dve, unit)


class Routes:
    pass


def slot_moe(nc, k, io, moe):
    with ExitStack() as ctx:
        ph = Phase(nc, ctx, f"moe{moe.layer}")
        r = Routes()
        r.weight = ph.sb("weight", [P, moe.picks, NT])
        r.take = ph.sb("take", [P, moe.picks, NT], U32)
        r.put = ph.sb("put", [P, moe.picks, NT], U32)
        r.unit_expert = ph.sb("unit_expert", [P, moe.units], I32)
        with ExitStack() as matrices_kept:
            m = Matrices(Phase(nc, matrices_kept, f"matrices{moe.layer}"))
            with ExitStack() as inner:
                normalised(nc, k, inner, f"ln_moe{moe.layer}", keep_rows=True)
                route_phase(nc, k, io, moe, r)
                dispatch_phase(nc, k, io, moe, r, m)
            experts_phase(nc, k, io, moe, r, m)
        combine_phase(nc, k, moe, r)


E32, GRP, PICKS1, GRPS = 32, 8, 8, 4
ESZ = E32 // GRP
SCALE1 = 2.5
SHARED = 2


def group_route_phase(nc, k, io, r):
    with ExitStack() as ctx:
        ph = Phase(nc, ctx, "route1")
        raw = ph.sb("raw", [P, KD, E32])
        gate = Pair.of(ph, "gate", [P, KD, E32])
        gbias = ph.sb("gbias", [P, NT, E32])
        sc = ph.sb("sc", [P, NT, E32])
        sb = ph.sb("sb", [P, NT, E32])
        ab = [ph.sb(f"ab{i}", [P, NT, GRP]) for i in range(6)]
        grp = ph.sb("grp", [P, NT, GRP])
        best = ph.sb("best", [P, NT, 8])
        ix = ph.sb("ix", [P, NT, 8], U32)
        ixf = ph.sb("ixf", [P, NT, 8])
        gm = ph.sb("gm", [P, NT, GRP])
        one = ph.sb("one", [P, NT, E32])
        comb = ph.sb("comb", [P, NT, E32])
        sums = ph.sb("sums", [P, NT])
        parts = ph.sb("parts", [P, NT, 3, E32], BF16)
        L = ph.ps("L", [P, NT, E32])
        T = ph.ps("T", [3 * E32, 2, 2 * S], BF16)
        gate_split = ph.sem("gate_split")
        loaded, l_ready, sig_done, dve_step, parts_ready, turned, taken = (
            ph.sem(n) for n in ("loaded", "l_ready", "sig_done", "dve_step", "parts_ready", "turned", "taken"))
        with nc.Block() as block:

            @block.sync
            def _(sp):
                sp.dma_start(raw[:], io["L1_ffn_gate_w"].rearrange("(c p) e -> p c e", p=P)).then_inc(loaded, 16)
                sp.dma_start(gbias[:], io["gbias1"]).then_inc(loaded, 16)
                sp.wait_ge(loaded, 32)

            @block.tensor
            def _(pe):
                pe.wait_ge(gate_split, 2)
                logits_products(nc, k, pe, gate, L, E32).then_inc(l_ready, 1)
                pe.wait_ge(parts_ready, 1)
                for q in range(NT // TPB):
                    if q >= 2:
                        pe.wait_ge(taken, q - 1)
                    for i in range(TPB):
                        t = q * TPB + i
                        mm = nc.tensor.transpose(T[:, q % 2, i * P:(i + 1) * P], parts[:, t].rearrange("p a e -> p (a e)"),
                                                 k.identb[:])
                    mm.then_inc(turned, 1)

            @block.scalar
            def _(act):
                act.wait_ge(l_ready, 1)
                nc.scalar.activation(sc[:], L[:], ACT.Sigmoid).then_inc(sig_done, 1)
                for q in range(NT // TPB):
                    act.wait_ge(turned, q + 1)
                    nc.scalar.copy(r.combT[:, q * S:(q + 1) * S], T[:, q % 2, 0:S]).then_inc(taken, 1)

            @block.vector
            def _(dve):
                v = nc.vector
                step = Steps(dve, dve_step)
                dve.wait_ge(loaded, 32)
                nc.vector.tensor_copy(gate.high[:], raw[:]).then_inc(gate_split, 1)
                dve.wait_ge(gate_split, 1)
                low_part(nc.vector, gate[:], raw[:]).then_inc(gate_split, 1)
                dve.wait_ge(sig_done, 1)
                step.after(v.tensor_tensor(sb[:], sc[:], gbias[:], ALU.add))
                s4 = sb[:].rearrange("p t (g m) -> p t g m", m=ESZ)
                v.tensor_tensor(ab[0][:], s4[:, :, :, 0], s4[:, :, :, 1], ALU.max)
                v.tensor_tensor(ab[1][:], s4[:, :, :, 0], s4[:, :, :, 1], ALU.min)
                v.tensor_tensor(ab[2][:], s4[:, :, :, 2], s4[:, :, :, 3], ALU.max)
                step.after(v.tensor_tensor(ab[3][:], s4[:, :, :, 2], s4[:, :, :, 3], ALU.min))
                v.tensor_tensor(ab[4][:], ab[0][:], ab[2][:], ALU.max)
                v.tensor_tensor(ab[5][:], ab[0][:], ab[2][:], ALU.min)
                step.after(v.tensor_tensor(ab[1][:], ab[1][:], ab[3][:], ALU.max))
                step.after(v.tensor_tensor(ab[5][:], ab[5][:], ab[1][:], ALU.max))
                step.after(v.tensor_tensor(grp[:], ab[4][:], ab[5][:], ALU.add))
                for t in range(NT):
                    ins = v.max(best[:, t, :], grp[:, t, :])
                step.after(ins)
                for t in range(NT):
                    ins = v.max_index(ix[:, t, :], best[:, t, :], grp[:, t, :])
                step.after(ins)
                step.after(v.tensor_copy(ixf[:], ix[:]))
                step.after(v.memset(gm[:], 0.0))
                wide = [P, NT, GRP]
                iota8 = k.iota[:, 0:GRP].unsqueeze(1).to_broadcast(wide)
                for p in range(GRPS):
                    step.after(v.tensor_tensor(grp[:], iota8, ixf[:, :, p:p + 1].to_broadcast(wide), ALU.is_equal))
                    step.after(v.tensor_tensor(gm[:], gm[:], grp[:], ALU.add))
                for m in range(ESZ):
                    ins = v.tensor_tensor(s4[:, :, :, m], s4[:, :, :, m], gm[:], ALU.mult)
                step.after(ins)
                for t in range(NT):
                    ins = v.max(best[:, t, :], sb[:, t, :])
                step.after(ins)
                for t in range(NT):
                    ins = v.max_index(ix[:, t, :], best[:, t, :], sb[:, t, :])
                step.after(ins)
                step.after(v.tensor_copy(ixf[:], ix[:]))
                step.after(v.memset(comb[:], 0.0))
                wide = [P, NT, E32]
                iota32 = k.iota[:, 0:E32].unsqueeze(1).to_broadcast(wide)
                for p in range(PICKS1):
                    step.after(v.tensor_tensor(one[:], iota32, ixf[:, :, p:p + 1].to_broadcast(wide), ALU.is_equal))
                    step.after(v.tensor_tensor(comb[:], comb[:], one[:], ALU.add))
                step.after(v.tensor_tensor(comb[:], comb[:], sc[:], ALU.mult))
                step.after(v.tensor_reduce(sums[:], comb[:], AX.X, ALU.add))
                step.after(v.tensor_scalar(sums[:], sums[:], 1e-20, None, ALU.add))
                step.after(v.reciprocal(sums[:], sums[:]))
                step.after(v.tensor_tensor(comb[:], comb[:], sums[:].unsqueeze(2).to_broadcast(wide), ALU.mult))
                step.after(v.tensor_scalar(comb[:], comb[:], SCALE1, None, ALU.mult))
                step.after(v.tensor_copy(parts[:, :, 0, :], comb[:]))
                step.after(v.tensor_tensor(comb[:], comb[:], parts[:, :, 0, :], ALU.subtract))
                step.after(v.tensor_copy(parts[:, :, 1, :], comb[:]))
                v.tensor_tensor(parts[:, :, 2, :], comb[:], parts[:, :, 1, :], ALU.subtract).then_inc(parts_ready, 1)


def gated_experts_phase(nc, k, io, r):
    NE = E32 + SHARED
    NW = 4

    NHID = 3

    def slot_before(e, slots=NW):
        return e - slots if e >= slots else max(f for f in range(NE) if f % slots == e) - NE

    WID = 2 * KD * P + D
    with ExitStack() as ctx:
        ph = Phase(nc, ctx, "experts1")
        raw = ph.sb("raw", [P, NW, WID])
        W = Pair.of(ph, "W", [P, NW, WID])
        sil = ph.sb("sil", [P, 2, S])
        prod = ph.sb("prod", [P, 2, S])
        full = ph.sb("full", [P, 2, S])
        hid = Pair.of(ph, "hid", [P, NHID, S])
        picks = ph.sb("picks", [3 * E32, E32, P])
        pick = ph.sb("pick", [3 * E32, E32, P], BF16)
        G, U = ph.ps("G", [P, 2, S]), ph.ps("U", [P, 2, S])
        CB = ph.ps("CB", [P, 2, S])
        Y = ph.ps("Y", [P, 2, 2, D])
        p_loaded, p_ready = ph.sem("p_loaded"), ph.sem("p_ready")
        w_loaded = [ph.sem(f"w_loaded{i}") for i in range(NW)]
        w_high, w_split, gu_ready, sil_done, prod_done, full_done, hid_high, hid_done, down_done = (
            ph.sem(n) for n in ("w_high", "w_split", "gu_ready", "sil_done", "prod_done", "full_done", "hid_high",
                                "hid_done", "down_done"))
        y_added = ph.sem("y_added")
        NC = N // S

        def matrices(i):
            gate, up = (Pair(*(a[:, i, o * KD * P:(o + 1) * KD * P].rearrange("p (c f) -> p c f", c=KD)
                               for a in (W.high, W.low))) for o in range(2))
            return gate, up, W[:, i, 2 * KD * P:]

        with nc.Block() as block:

            @block.sync
            def _(sp):
                sp.dma_start(picks[:], io["c_pick"]).then_inc(p_loaded, 16)
                with sp.Fori(0, NC) as c:
                    for e in range(NE):
                        sp.wait_ge(w_split, c * NE + slot_before(e) + NW + 1)
                        sp.dma_start(raw[:, e % NW], io["w_gated"][e]).then_inc(w_loaded[e % NW], 16)
                sp.wait_ge(p_loaded, 16)

            @block.tensor
            def _(pe):
                def up(c, e):
                    wg, wu, _ = matrices(e % NW)
                    pe.wait_ge(w_split, c * NE + e + NW + 1)
                    pe.wait_ge(full_done, c * NE + e + 1)
                    for w, ps in ((wg, G), (wu, U)):
                        for kd in range(KD):
                            product(nc, ps[:, e % 2, :], w[:, kd, :], k.xnT[:, kd, bass.ds(c * S, S)], kd == 0, kd == KD - 1)
                    mm = nc.tensor.matmul(CB[:, e % 2, :], pick[:, e % E32, :], r.combT[:, bass.ds(c * S, S)],
                                          start=True, stop=True)
                    mm.then_inc(gu_ready, 1)

                def down(c, e):
                    wd = matrices(e % NW)[2]
                    pe.wait_ge(hid_done, c * NE + e + 1)
                    if e == 0:
                        pe.wait_ge(y_added, c * TPB + TPB)
                    for i in range(TPB):
                        mm = product(nc, Y[:, i // 2, i % 2, :], hid[:, e % NHID, i * P:(i + 1) * P], wd,
                                     e == 0 and i % 2 == 0, e == NE - 1)
                    mm.then_inc(down_done, 1)

                pe.wait_ge(p_ready, 1)
                with pe.Fori(0, NC) as c:
                    for e in range(NE):
                        up(c, e)
                        if e >= 2:
                            down(c, e - 2)
                    down(c, NE - 2)
                    down(c, NE - 1)

            @block.scalar
            def _(act):
                def matrices_high(c, e):
                    uses = len(range(e % NW, NE, NW))
                    act.wait_ge(w_loaded[e % NW], c * (16 * uses) + (e // NW) * 16 + 16)
                    act.wait_ge(down_done, c * NE + slot_before(e) + NW + 1)
                    nc.scalar.copy(W.high[:, e % NW], raw[:, e % NW]).then_inc(w_high, 1)

                def hidden_high(c, e):
                    act.wait_ge(full_done, c * NE + e + 3)
                    act.wait_ge(down_done, c * NE + slot_before(e, NHID) + NW + 1)
                    nc.scalar.copy(hid.high[:, e % NHID, :], full[:, e % 2, :]).then_inc(hid_high, 1)

                act.sem_inc(down_done, NW)
                with act.Fori(0, NC) as c:
                    matrices_high(c, 0)
                    matrices_high(c, 1)
                    for e in range(NE):
                        act.wait_ge(gu_ready, c * NE + e + 1)
                        act.wait_ge(prod_done, c * NE + e + 1)
                        nc.scalar.activation(sil[:, e % 2, :], G[:, e % 2, :], ACT.Silu).then_inc(sil_done, 1)
                        if e + 2 < NE:
                            matrices_high(c, e + 2)
                        hidden_high(c, e)

            @block.gpsimd
            def _(pool):
                with pool.Fori(0, NC) as c:
                    for e in range(NE):
                        pool.wait_ge(w_high, c * NE + e + 1)
                        low_part(nc.gpsimd, W[:, e % NW], raw[:, e % NW]).then_inc(w_split, 1)

            @block.vector
            def _(dve):
                def hidden(c, e):
                    i = e % 2
                    dve.wait_ge(sil_done, c * NE + e + 1)
                    last = full if e >= E32 else prod
                    nc.vector.tensor_tensor(last[:, i, :], sil[:, i, :], U[:, i, :], ALU.mult).then_inc(prod_done, 1)
                    dve.wait_ge(prod_done, c * NE + e + 3)
                    if e >= E32:
                        dve.sem_inc(full_done, 1)
                    else:
                        nc.vector.tensor_tensor(full[:, i, :], prod[:, i, :], CB[:, i, :], ALU.mult).then_inc(full_done, 1)

                def hidden_low(c, e):
                    dve.wait_ge(hid_high, c * NE + e + 1)
                    low_part(nc.vector, hid[:, e % NHID, :], full[:, e % 2, :]).then_inc(hid_done, 1)

                dve.sem_inc(full_done, 2)
                dve.sem_inc(prod_done, 2)
                dve.sem_inc(w_split, NW)
                dve.sem_inc(y_added, TPB)
                dve.wait_ge(p_loaded, 16)
                nc.vector.tensor_copy(pick[:], picks[:]).then_inc(p_ready, 1)
                with dve.Fori(0, NC) as c:
                    for e in range(NE):
                        hidden(c, e)
                        hidden_low(c, e)
                    dve.wait_ge(down_done, c * NE + NE + NW)
                    for i in range(TPB):
                        xt = k.x[:, bass.ds(c * TPB + i, 1), :].rearrange("p t d -> p (t d)")
                        nc.vector.tensor_tensor(xt, xt, Y[:, i // 2, i % 2, :], ALU.add).then_inc(y_added, 1)


def gated_moe(nc, k, io):
    with ExitStack() as ctx:
        ph = Phase(nc, ctx, "moe1")
        r = Routes()
        r.combT = ph.sb("combT", [3 * E32, N], BF16)
        normalised(nc, k, ctx, "ln_moe1")
        group_route_phase(nc, k, io, r)
        gated_experts_phase(nc, k, io, r)


def moe(nc, k, io, layer):
    if layer == 1:
        gated_moe(nc, k, io)
    else:
        slot_moe(nc, k, io, MOES[layer])


def ffn_layout(f):
    io = {}

    def each_token(a, *shape):
        return np.ascontiguousarray(np.broadcast_to(a, shape))

    io["L0_ffn_gate_w"] = np.ascontiguousarray(f["L0_ffn_gate_w"].T)
    io["L2_ffn_Wr"], io["L3_ffn_w_g"] = f["L2_ffn_Wr"], f["L3_ffn_w_g"]
    io["gbias0"] = each_token(np.stack([f["L0_ffn_gate_b"], f["L0_ffn_expert_bias"]])[None, :, None, :], P, 2, NT, E8)
    io["gbias2"] = each_token(f["L2_ffn_br"][None, None, None, :], P, 1, NT, E8)
    for m in MOES.values():
        io[m.w1], io[m.w2] = f[m.w1], f[m.w2]
        if m.b1:
            io[m.b1] = np.ascontiguousarray(f[m.b1].reshape(E8, FT, P).transpose(0, 2, 1))
            io[m.b2] = each_token(f[m.b2][:, None, :], E8, P, D)
    io["L1_ffn_gate_w"] = np.ascontiguousarray(f["L1_ffn_gate_w"].T)
    io["gbias1"] = each_token(f["L1_ffn_gate_bias"][None, None, :], P, NT, E32)
    wg = np.concatenate([f["L1_ffn_w_gate"], f["L1_ffn_sh_gate"].reshape(SHARED, P, D)])
    wu = np.concatenate([f["L1_ffn_w_up"], f["L1_ffn_sh_up"].reshape(SHARED, P, D)])
    wd = np.concatenate([f["L1_ffn_w_down"].transpose(0, 2, 1), f["L1_ffn_sh_down"].T.reshape(SHARED, P, D)])
    turned = [w.transpose(0, 2, 1).reshape(-1, KD, P, P).transpose(0, 2, 1, 3).reshape(-1, P, KD * P) for w in (wg, wu)]
    io["w_gated"] = np.ascontiguousarray(np.concatenate(turned + [wd], axis=2))
    pre = "L3_xattn_"
    for w in ("Wq", "Wk", "Wv"):
        io[pre + w] = np.ascontiguousarray(f[pre + w].T)
    for b in ("bq", "bk"):
        io[pre + b] = np.ascontiguousarray(f[pre + b].reshape(KD, P).T)
    io[pre + "bv"] = each_token(f[pre + "bv"][None, :], P, D)
    io[pre + "beta"] = each_token(np.stack([f[pre + "beta_" + n].reshape(()) for n in ("risk", "prio", "impl")])[None, :], P, 3)
    return io



class Kept:
    pass


def program(nc, io, out, stages=99, start=0):
    with ExitStack() as ctx:
        ph = Phase(nc, ctx, "kept")
        k = Kept()
        k.x = ph.sb("x", [P, NT, D])
        k.identf = ph.sb("identf", [P, P])
        k.identb = ph.sb("identb", [P, P], BF16)
        k.before = ph.sb("before", [P, P], BF16)
        k.onesb = ph.sb("onesb", [P, P], BF16)
        k.iota = ph.sb("iota", [P, 32])
        k.half = ph.sb("half", [P, NT])
        k.qstack = nc.dram_tensor("qstack", (H, SR, N), BF16, kind="Internal").ap()
        k.kstack = nc.dram_tensor("kstack", (H, SR, N), BF16, kind="Internal").ap()
        k.xg = nc.dram_tensor("xg", (8 * 640, D), F32, kind="Internal").ap()
        k.yg = nc.dram_tensor("yg", (8 * 640, D), F32, kind="Internal").ap()
        k.scattered = ph.sem("scattered")
        k.gathered = [ph.sem(f"gathered{i}") for i in range(GATHERS)]
        k.n_scattered = k.n_gathered = 0
        with_context = ctx.enter_context(ExitStack())
        k.ctxT = Pair.of(Phase(nc, with_context, "context"), "ctxT", [P, KD, N])
        setup_phase(nc, k, io)
        clear_semaphores(nc)
        stage_list = [
            lambda: heads_attention(nc, k, io, 0),
            lambda: moe(nc, k, io, 0),
            lambda: heads_attention(nc, k, io, 1, rope=True),
            lambda: moe(nc, k, io, 1),
            lambda: heads_attention(nc, k, io, 2, masked=True),
            lambda: moe(nc, k, io, 2),
            lambda: whole_attention(nc, k, io),
            lambda: moe(nc, k, io, 3),
        ]
        for s, stage in enumerate(stage_list[:stages]):
            if s < start:
                continue
            if s == len(stage_list) - 1:
                with_context.close()
            stage()
            clear_semaphores(nc)
        store_phase(nc, k, out)


def store_phase(nc, k, out):
    with nc.semaphore("stored") as stored, nc.Block() as block:

        @block.sync
        def _(sp):
            sp.dma_start(out.rearrange("b (t p) d -> p (b t) d", p=P), k.x[:]).then_inc(stored, 16)
            sp.wait_ge(stored, 16)



def laid_out(inputs):
    f = {n: np.ascontiguousarray(a) for n, a in inputs.items()}
    io = {n: f[n] for n in ("x", "ctx_1024", "fside_BxSxS2_0", "mask_Bx1xSxS2_ik0")}

    def column(a, n=KD):
        return np.ascontiguousarray(a.reshape(n, P).T)

    def beside(a, axis):
        return np.concatenate([a, np.zeros_like(a)], axis=axis)

    turn = np.arange(D).reshape(H, 2, DH // 2)[:, ::-1].reshape(D)
    for layer in range(3):
        pre = f"L{layer}_xattn_"
        for w in ("Wq", "Wk", "Wv"):
            io[pre + w] = np.ascontiguousarray(f[pre + w].T)
        for b in ("bq", "bk"):
            io[pre + b] = column(f[pre + b])
        if layer == 1:
            for w in ("Wq", "Wk"):
                io[pre + w + "_turn"] = np.ascontiguousarray(f[pre + w][turn].T)
            for b in ("bq", "bk"):
                io[pre + b + "_turn"] = column(f[pre + b][turn])
        wo = beside(f[pre + "Wo"].T.reshape(NG, GH, DH, D), 2)
        wo[0, 0, DH] = f[pre + "bo"]
        io[pre + "Wo"] = np.ascontiguousarray(wo.reshape(NG, P, D))
        io[pre + "bv"] = column(beside(f[pre + "bv"].reshape(NG, GH, DH), 2).reshape(-1), NG)
    io.update(ffn_layout(f))
    io.update(constants())
    return io


def constants():
    c = {}
    c["c_identf"] = np.eye(P, dtype=np.float32)
    p = np.arange(P)
    row = np.arange(3 * H) % H
    c["c_spread"] = np.ascontiguousarray(((row[:, None, None] // NG == p[None, None, :] // HS)
                                          & (row[:, None, None] % NG == np.arange(NG)[None, :, None])).astype(np.float32))
    c["c_before"] = (p[:, None] < p[None, :]).astype(np.float32)
    c["c_iota"] = np.broadcast_to(np.arange(32, dtype=np.float32), (P, 32)).copy()
    c["c_pick"] = np.ascontiguousarray(np.broadcast_to((np.arange(3 * E32)[:, None] % E32 == np.arange(E32)[None, :])[:, :, None],
                                                       (3 * E32, E32, P))).astype(np.float32)
    inv_freq = (1.0 / np.float32(10000.0) ** (np.arange(0, DH, 2, dtype=np.float32) / np.float32(DH))).astype(np.float32)
    pos = (np.float32(10.0) * (np.arange(S, dtype=np.float32) / np.float32(S))).astype(np.float32)
    freqs = np.outer(pos, inv_freq).astype(np.float32)
    cos, sin = np.cos(freqs).T, np.sin(freqs).T
    cos = np.tile(np.concatenate([cos, cos]), (P // DH, 1)).astype(np.float32)
    sin = np.tile(np.concatenate([-sin, sin]), (P // DH, 1)).astype(np.float32)
    c["c_cosk"], c["c_sink"] = cos, sin
    c["c_cosq"], c["c_sinq"] = cos * np.float32(DH ** -0.5), sin * np.float32(DH ** -0.5)
    return c


def kernel(**inputs):
    import concourse.bacc as bacc
    from concourse.bass_utils import run_bass_kernel_spmd

    nc = bacc.Bacc("TRN2", target_bir_lowering=False, num_devices=1)
    arrays = {f"in_{n}": a for n, a in laid_out(inputs).items()}
    io = {n[3:]: nc.dram_tensor(n, a.shape, mybir.dt.from_np(a.dtype), kind="ExternalInput").ap() for n, a in arrays.items()}
    out = nc.dram_tensor("out_x", (B, S, D), F32, kind="ExternalOutput").ap()
    program(nc, io, out)
    r = run_bass_kernel_spmd(nc, [arrays], core_ids=[0])
    return r.results[0]["out_x"]
```

```python
from contextlib import ExitStack

import numpy as np

import concourse.bass as bass
from concourse import mybir
from concourse.alu_op_type import AluOpType as ALU

ACT = mybir.ActivationFunctionType
F32 = mybir.dt.float32
BF16 = mybir.dt.bfloat16
F32R = mybir.dt.float32r
I32 = mybir.dt.int32
U32 = mybir.dt.uint32
AX = mybir.AxisListType

P = 128
B, S, D = 4, 512, 256
N = B * S
NT = N // P
KD = D // P
TPB = S // P
H, DH = 16, 16
GH = 4
NG = H // GH
HS = 32
PARTS = 3
NPROD = 6
SR = NPROD * DH
MR = 3
EPS = 1e-5
NEG = -float(2 ** 100)


class Phase:

    def __init__(self, nc, ctx, name):
        self.nc, self.ctx, self.name = nc, ctx, name

    def sb(self, name, shape, dt=F32):
        return self.ctx.enter_context(self.nc.sbuf_tensor(f"{self.name}_{name}", shape, dt))

    def ps(self, name, shape, dt=F32):
        return self.ctx.enter_context(self.nc.psum_tensor(f"{self.name}_{name}", shape, dt))

    def sem(self, name):
        return self.ctx.enter_context(self.nc.semaphore(f"{self.name}_{name}"))


class Pair:

    def __init__(self, high, low):
        self.high, self.low = high, low

    def __getitem__(self, key):
        return Pair(self.high[key], self.low[key])

    @classmethod
    def of(cls, ph, name, shape):
        return cls(ph.sb(name + "_high", shape, F32R), ph.sb(name + "_low", shape, F32R))


def low_part(vector, pair, full):
    return vector.tensor_tensor(pair.low, full, pair.high.bitcast(F32), ALU.subtract)


def product(nc, out, lhsT, rhs, start, stop):
    nc.tensor.matmul(out, lhsT.high, rhs.high, start=start, stop=False, skip_group_check=True)
    nc.tensor.matmul(out, lhsT.high, rhs.low, start=False, stop=False, skip_group_check=True)
    return nc.tensor.matmul(out, lhsT.low, rhs.high, start=False, stop=stop, skip_group_check=True)


def clear_semaphores(nc):
    free = sorted(nc.free_semaphores)
    runs = [[free[0], free[0] + 1]]
    for n in free[1:]:
        if n == runs[-1][1]:
            runs[-1][1] = n + 1
        else:
            runs.append([n, n + 1])
    for a, b in runs:
        nc.gpsimd.sem_clear(range(a, b))
    nc.all_engine_barrier()


class Steps:

    def __init__(self, eng, sem):
        self.eng, self.sem, self.n = eng, sem, 0

    def after(self, ins):
        ins.then_inc(self.sem, 1)
        self.n += 1
        self.eng.wait_ge(self.sem, self.n)



def setup_phase(nc, k, io):
    with ExitStack() as ctx:
        ph = Phase(nc, ctx, "setup")
        ctok = ph.sb("ctok", [P, NT, D])
        before = ph.sb("before", [P, P])
        TP = ph.ps("tp", [P, 4, KD, 2 * P])
        x_loaded, consts, ident = ph.sem("x_loaded"), ph.sem("consts"), ph.sem("ident")
        ctx_loaded = [ph.sem(f"ctx_loaded{b}") for b in range(B)]
        turned, taken = ph.sem("turned"), ph.sem("taken")
        high = ph.sem("high")
        with nc.Block() as block:

            @block.sync
            def _(sp):
                sp.dma_start(k.identf[:], io["c_identf"]).then_inc(ident, 16)
                for b in range(B):
                    sp.dma_start(ctok[:, b * TPB:(b + 1) * TPB, :], io["ctx_1024"][b].rearrange("(t p) d -> p t d", p=P)
                                 ).then_inc(ctx_loaded[b], 16)
                sp.dma_start(k.x[:], io["x"].rearrange("b (t p) d -> p (b t) d", p=P)).then_inc(x_loaded, 16)
                sp.dma_start(before[:], io["c_before"]).then_inc(consts, 16)
                sp.dma_start(k.iota[:], io["c_iota"]).then_inc(consts, 16)
                sp.wait_ge(x_loaded, 16)
                sp.wait_ge(consts, 16 * 2)

            @block.gpsimd
            def _(pool):
                nc.gpsimd.memset(k.zero[:], 0.0)
                nc.gpsimd.memset(k.half[:], -0.5)
                nc.gpsimd.memset(k.onesb[:], 1.0)

            @block.tensor
            def _(pe):
                pe.wait_ge(ident, 16)
                for p in range(NT // 2):
                    pe.wait_ge(ctx_loaded[2 * p // TPB], 16)
                    if p >= 4:
                        pe.wait_ge(taken, p - 3)
                    for i in range(2):
                        for c in range(KD):
                            mm = nc.tensor.transpose(TP[:, p % 4, c, i * P:(i + 1) * P],
                                                     ctok[:, 2 * p + i, c * P:(c + 1) * P], k.identf[:])
                    mm.then_inc(turned, 1)

            @block.vector
            def _(dve):
                for p in range(NT // 2):
                    dve.wait_ge(high, p + 1)
                    low_part(nc.vector, k.ctxT[:, :, p * 2 * P:(p + 1) * 2 * P], TP[:, p % 4]).then_inc(taken, 1)
                dve.wait_ge(ident, 16)
                dve.wait_ge(consts, 16 * 2)
                nc.vector.tensor_copy(k.identb[:], k.identf[:])
                nc.vector.tensor_copy(k.before[:], before[:])

            @block.scalar
            def _(act):
                for p in range(NT // 2):
                    act.wait_ge(turned, p + 1)
                    nc.scalar.copy(k.ctxT.high[:, :, p * 2 * P:(p + 1) * 2 * P], TP[:, p % 4]).then_inc(high, 1)



class Weights:

    def __init__(self, ph):
        self.ph, self.cut, self.plain = ph, [], []
        self.experts = 0
        self.also = None

    def pair(self, name, shape, src):
        raw = self.ph.sb(name + "_raw", shape)
        pair = Pair.of(self.ph, name, shape)
        self.cut.append((raw, pair, src))
        return pair

    def gate_of(self, experts, src, logitsT):
        self.experts = experts
        self.gate = self.pair("gate", [P, KD, experts], src)
        self.logitsT = logitsT

    def array(self, name, shape, src):
        full = self.ph.sb(name, shape)
        self.plain.append((full, src))
        return full


def layernorm_phase(nc, k, name, weights):
    HT = NT // 2
    with ExitStack() as ctx:
        ph = Phase(nc, ctx, name)
        st = k.st
        mean, diff, var, rstd = (ph.sb(n, [P, NT]) for n in ("mean", "diff", "var", "rstd"))
        TP = ph.ps("tp", [P, 4, KD, 2 * P])
        E = weights.experts
        LT = ph.ps("LT", [P, N]) if E else None
        lt_ready, fourth_ready = ph.sem("lt_ready"), ph.sem("fourth_ready")

        def normalise(eng, t):
            return eng.tensor_scalar(k.xn[:, t, :], k.x[:, t, :], mean[:, t:t + 1], rstd[:, t:t + 1],
                                     ALU.subtract, ALU.mult)

        dve_step, var_ready, rstd_ready = ph.sem("dve_step"), ph.sem("var_ready"), ph.sem("rstd_ready")
        xn_ready, turned, high, taken = ph.sem("xn_ready"), ph.sem("turned"), ph.sem("high"), ph.sem("taken")
        cut_loaded, plain_loaded, w_high, w_split = (ph.sem(n) for n in ("cut_loaded", "plain_loaded", "w_high", "w_split"))
        with nc.Block() as block:

            @block.sync
            def _(sp):
                for raw, pair, src in weights.cut:
                    sp.dma_start(raw[:], src).then_inc(cut_loaded, 16)
                for full, src in weights.plain:
                    sp.dma_start(full[:], src).then_inc(plain_loaded, 16)
                if weights.also:
                    weights.also(sp)
                if weights.plain:
                    sp.wait_ge(plain_loaded, 16 * len(weights.plain))

            @block.vector
            def _(dve):
                def take_low(p):
                    dve.wait_ge(high, p + 1)
                    low_part(nc.vector, k.xnT[:, :, p * 2 * P:(p + 1) * 2 * P], TP[:, p % 4]).then_inc(taken, 1)

                step = Steps(dve, dve_step)

                def statistics(half):
                    tiles = slice(half * HT, (half + 1) * HT)
                    if not k.st_there:
                        for t in range(half * HT, (half + 1) * HT):
                            ins = nc.vector.bn_stats(st[:, t, :], k.x[:, t, :])
                        step.after(ins)
                    me, se, mo, so = (st[:, tiles, i] for i in (1, 2, 4, 5))
                    m, d, v = mean[:, tiles], diff[:, tiles], var[:, tiles]
                    nc.vector.tensor_tensor(m, me, mo, ALU.add)
                    nc.vector.tensor_tensor(d, me, mo, ALU.subtract)
                    step.after(nc.vector.tensor_tensor(v, se, so, ALU.add))
                    nc.vector.tensor_scalar(m, m, 0.5, None, ALU.mult)
                    nc.vector.tensor_scalar(v, v, 1.0 / D, EPS, ALU.mult, ALU.add)
                    step.after(nc.vector.tensor_tensor(d, d, d, ALU.mult))
                    nc.vector.scalar_tensor_tensor(out=v, in0=d, scalar=0.25, in1=v,
                                                   op0=ALU.mult, op1=ALU.add).then_inc(var_ready, 1)

                statistics(0)
                statistics(1)
                for i, (raw, pair, src) in enumerate(weights.cut):
                    dve.wait_ge(w_high, i + 1)
                    low_part(nc.vector, pair[:], raw[:]).then_inc(w_split, 1)
                for p in range(NT // 2):
                    if p % (NT // 4) == 0:
                        dve.wait_ge(rstd_ready, 2 * p // HT + 1)
                    ins = normalise(nc.vector, 2 * p)
                    if p % 2 == 0:
                        ins = normalise(nc.vector, 2 * p + 1)
                    ins.then_inc(xn_ready, 1)
                    if p > 1:
                        take_low(p - 2)
                for p in range(NT // 2 - 2, NT // 2):
                    take_low(p)

            @block.gpsimd
            def _(pool):
                for half in range(2):
                    tiles = slice(half * HT, (half + 1) * HT)
                    pool.wait_ge(var_ready, half + 1)
                    nc.gpsimd.tensor_tensor(rstd[:, tiles], var[:, tiles], k.half[:, tiles], ALU.pow).then_inc(rstd_ready, 1)
                for n, t in enumerate(range(3, NT, 4)):
                    pool.wait_ge(rstd_ready, t // HT + 1)
                    normalise(nc.gpsimd, t).then_inc(fourth_ready, 1)

            @block.tensor
            def _(pe):
                def logits(p):
                    pe.wait_ge(taken, p + 1)
                    if p == 0:
                        pe.wait_ge(w_split, 1)
                    tokens = slice(p * 2 * P, (p + 1) * 2 * P)
                    for kd in range(KD):
                        mm = product(nc, LT[0:E, tokens], weights.gate[:, kd, :], k.xnT[:, kd, tokens], kd == 0, kd == KD - 1)
                    mm.then_inc(lt_ready, 1)

                for p in range(NT // 2):
                    pe.wait_ge(xn_ready, p + 1)
                    if p % 2:
                        pe.wait_ge(fourth_ready, p // 2 + 1)
                    if p >= 4:
                        pe.wait_ge(taken, p - 3)
                    for i in range(2):
                        for c in range(KD):
                            mm = nc.tensor.transpose(TP[:, p % 4, c, i * P:(i + 1) * P],
                                                     k.xn[:, 2 * p + i, c * P:(c + 1) * P], k.identf[:])
                    mm.then_inc(turned, 1)
                    if E and p:
                        logits(p - 1)
                if E:
                    logits(NT // 2 - 1)

            @block.scalar
            def _(act):
                act.wait_ge(cut_loaded, 16 * len(weights.cut))
                for raw, pair, src in weights.cut:
                    nc.scalar.copy(pair.high[:], raw[:]).then_inc(w_high, 1)

                def take_logits(c):
                    act.wait_ge(lt_ready, 2 * c + 2)
                    nc.scalar.copy(weights.logitsT[:, c * S:(c + 1) * S], LT[0:E, c * S:(c + 1) * S])

                for p in range(NT // 2):
                    act.wait_ge(turned, p + 1)
                    nc.scalar.copy(k.xnT.high[:, :, p * 2 * P:(p + 1) * 2 * P], TP[:, p % 4]).then_inc(high, 1)
                    if E and p >= 3 and p % 2:
                        take_logits(p // 2 - 1)
                if E:
                    take_logits(N // S - 1)



Q_PARTS = (0, 1, 2, 0, 1, 0)
K_PARTS = (0, 0, 0, 1, 1, 2)


def runs_of_parts(order):
    runs = []
    for row, part in enumerate(order):
        if runs and part == runs[-1][1] + runs[-1][2]:
            runs[-1][2] += 1
        else:
            runs.append([row, part, 1])
    return runs


def heads_weights(ph, io, layer, rope):
    pre = f"L{layer}_xattn_"
    w = Weights(ph)
    w.W = {n: w.pair(n, [P, KD, D], io[pre + n].rearrange("(c p) o -> p c o", p=P))
           for n in ["Wk", "Wv", "Wq"] + (["Wk_turn", "Wq_turn"] if rope else [])}
    w.bias = {n: w.array(n, [P, KD], io[pre + n]) for n in ["bq", "bk"] + (["bq_turn", "bk_turn"] if rope else [])}
    w.tabs = {n: w.array(n, [P, S], io["c_" + n]) for n in (("cosq", "sinq", "cosk", "sink") if rope else ())}
    return w


def heads_project_phase(nc, k, w, layer, rope):
    W, bias, tabs = w.W, w.bias, w.tabs
    with ExitStack() as ctx:
        ph = Phase(nc, ctx, f"proj{layer}")
        full = ph.sb("full", [P, 2, S])
        other = ph.sb("other", [P, 2, S]) if rope else None
        rest = ph.sb("rest", [P, 2, S])
        parts = ph.sb("parts", [P, 2, 3, N], BF16)
        QK = ph.ps("qk", [P, 2, S])
        QK2 = ph.ps("qk2", [P, 2, S])
        VP = ph.ps("vp", [P, 2, 2, D])
        qk_ready, qk_taken, v_ready, v_taken = (ph.sem(n) for n in ("qk_ready", "qk_taken", "v_ready", "v_taken"))
        high_ready, rest_ready, mid_ready, low_ready = (ph.sem(n) for n in ("high", "rest", "mid", "low"))
        dve_step = ph.sem("dve_step")
        stored = [ph.sem(f"stored{i}") for i in range(2)]
        units = [(what, m) for what in ("k", "q") for m in range(KD)]
        NC = N // S
        CHUNKS = len(units) * NC
        with nc.Block() as block:

            @block.sync
            def _(sp):
                for u, (what, m) in enumerate(units):
                    dst = k.qparts if what == "q" else k.kparts
                    for half in range(2):
                        sp.wait_ge(low_ready, NC * u + NC // 2 * (half + 1))
                        tokens = slice(half * N // 2, (half + 1) * N // 2)
                        for part in range(PARTS):
                            sp.dma_start(dst[m * 8:(m + 1) * 8, part * DH:(part + 1) * DH, tokens],
                                         parts[:, u % 2, part, tokens]).then_inc(stored[u % 2], 16)
                for i in range(2):
                    sp.wait_ge(stored[i], 2 * 16 * PARTS * 2)

            @block.tensor
            def _(pe):
                def queries_or_keys(s):
                    what, m = units[s // NC]
                    c = s % NC
                    src = k.xnT if what == "q" else k.ctxT
                    if s >= 2:
                        pe.wait_ge(qk_taken, s - 1)
                    for n, ps in (("W" + what, QK), ("W" + what + "_turn", QK2))[:2 if rope else 1]:
                        for kd in range(KD):
                            mm = product(nc, ps[:, s % 2, :], W[n][:, kd, m * P:(m + 1) * P],
                                         src[:, kd, c * S:(c + 1) * S], kd == 0, kd == KD - 1)
                    mm.then_inc(qk_ready, 1)

                def values(t):
                    if t >= 2:
                        pe.wait_ge(v_taken, t - 1)
                    for i in range(2):
                        tok = (2 * t + i) * P
                        for kd in range(KD):
                            mm = product(nc, VP[:, t % 2, i, :], k.ctxT[:, kd, tok:tok + P], W["Wv"][:, kd, :],
                                         kd == 0, kd == KD - 1)
                    mm.then_inc(v_ready, 1)

                for s in range(CHUNKS):
                    queries_or_keys(s)
                    if s % 2:
                        values(s // 2)

            @block.vector
            def _(dve):
                step = Steps(dve, dve_step)

                def what_high_leaves(s):
                    u, c = divmod(s, NC)
                    dve.wait_ge(high_ready, s + 1)
                    if s >= 2:
                        dve.wait_ge(low_ready, s - 1)
                    nc.vector.tensor_tensor(rest[:, s % 2, :], full[:, s % 2, :], parts[:, u % 2, 0, c * S:(c + 1) * S],
                                            ALU.subtract).then_inc(rest_ready, 1)

                for s in range(CHUNKS):
                    what = units[s // NC][0]
                    m = units[s // NC][1]
                    dve.wait_ge(qk_ready, s + 1)
                    if s >= 2:
                        dve.wait_ge(rest_ready, s - 1)
                    f = full[:, s % 2, :]
                    if rope:
                        nc.vector.scalar_tensor_tensor(out=f, in0=QK[:, s % 2, :], scalar=bias["b" + what][:, m:m + 1],
                                                       in1=tabs["cos" + what][:], op0=ALU.add, op1=ALU.mult)
                        step.after(nc.vector.scalar_tensor_tensor(
                            out=other[:, s % 2, :], in0=QK2[:, s % 2, :], scalar=bias["b" + what + "_turn"][:, m:m + 1],
                            in1=tabs["sin" + what][:], op0=ALU.add, op1=ALU.mult))
                        nc.vector.tensor_tensor(f, f, other[:, s % 2, :], ALU.add).then_inc(qk_taken, 1)
                    else:
                        scale = DH ** -0.5 if what == "q" else 1.0
                        nc.vector.tensor_scalar(f, QK[:, s % 2, :], bias["b" + what][:, m:m + 1], scale,
                                                ALU.add, ALU.mult).then_inc(qk_taken, 1)
                    if s:
                        what_high_leaves(s - 1)
                what_high_leaves(CHUNKS - 1)

            @block.scalar
            def _(act):
                def part(s, which):
                    u, c = divmod(s, NC)
                    return parts[:, u % 2, which, c * S:(c + 1) * S]

                def middle(s):
                    act.wait_ge(rest_ready, s + 1)
                    nc.scalar.copy(part(s, 1), rest[:, s % 2, :]).then_inc(mid_ready, 1)

                def copy_values(t):
                    act.wait_ge(v_ready, t + 1)
                    nc.scalar.copy(k.V[:, 2 * t:2 * t + 2, :], VP[:, t % 2]).then_inc(v_taken, 1)

                for s in range(CHUNKS):
                    u = s // NC
                    if s % NC == 0 and u >= 2:
                        act.wait_ge(stored[u % 2], 2 * 16 * PARTS)
                    act.wait_ge(qk_taken, s + 1)
                    nc.scalar.copy(part(s, 0), full[:, s % 2, :]).then_inc(high_ready, 1)
                    if s:
                        middle(s - 1)
                    if s % 2 == 0 and s:
                        copy_values(s // 2 - 1)
                middle(CHUNKS - 1)
                copy_values(CHUNKS // 2 - 1)

            @block.gpsimd
            def _(pool):
                def part(s, which):
                    u, c = divmod(s, NC)
                    return parts[:, u % 2, which, c * S:(c + 1) * S]

                for s in range(CHUNKS):
                    pool.wait_ge(mid_ready, s + 1)
                    nc.gpsimd.tensor_tensor(part(s, 2), rest[:, s % 2, :], part(s, 1), ALU.subtract).then_inc(low_ready, 1)


class MaskRows:

    SLOTS = 3

    def __init__(self, ph, io):
        self.raw = ph.sb("raw", [P, self.SLOTS, TPB, S], I32)
        self.loaded = [ph.sem(f"loaded{i}") for i in range(self.SLOTS)]
        self.src = io["mask_Bx1xSxS2_ik0"]

    def load(self, sp, b):
        sp.dma_start(self.raw[:, b % self.SLOTS], self.src[b, 0].rearrange("(t p) s -> p t s", p=P)
                     ).then_inc(self.loaded[b % self.SLOTS], 16)

    def load_first(self, sp):
        for b in range(self.SLOTS):
            self.load(sp, b)


def mask_phase(nc, k, mask):
    with ExitStack() as ctx:
        ph = Phase(nc, ctx, "mask")
        TP = ph.ps("tp", [P, 4, 2 * S], BF16)
        pen_ready, turned, taken = ph.sem("pen_ready"), ph.sem("turned"), ph.sem("taken")
        with nc.Block() as block:

            @block.sync
            def _(sp):
                for b in range(mask.SLOTS, B):
                    sp.wait_ge(pen_ready, b - mask.SLOTS + 1)
                    mask.load(sp, b)

            @block.vector
            def _(dve):
                for b in range(B):
                    dve.wait_ge(mask.loaded[b % mask.SLOTS], 16 * (b // mask.SLOTS + 1))
                    nc.vector.tensor_scalar(k.pen[:, b * TPB:(b + 1) * TPB, :], mask.raw[:, b % mask.SLOTS], 0.0, NEG,
                                            ALU.is_equal, ALU.mult).then_inc(pen_ready, 1)

            @block.tensor
            def _(pe):
                for b in range(B):
                    pe.wait_ge(pen_ready, b + 1)
                    for kt in range(TPB):
                        i = b * TPB + kt
                        if i >= 4:
                            pe.wait_ge(taken, i - 3)
                        for qt in range(TPB):
                            mm = nc.tensor.transpose(TP[:, i % 4, qt * P:(qt + 1) * P],
                                                     k.pen[:, b * TPB + qt, kt * P:(kt + 1) * P], k.identb[:])
                        mm.then_inc(turned, 1)

            @block.scalar
            def _(act):
                for i in range(NT):
                    act.wait_ge(turned, i + 1)
                    nc.scalar.copy(k.penT[:, i, :], TP[:, i % 4, 0:S]).then_inc(taken, 1)


class OutputNeeds:

    A = P // H
    W = N // A

    def __init__(self, ph, io, layer):
        pre = f"L{layer}_xattn_"
        self.raw = ph.sb("Wo_raw", [P, NG, D])
        self.bv = ph.sb("bv", [P, NG])
        self.spread = ph.sb("spread", [3 * H, NG, P])
        self.sums = ph.sb("sums", [P, self.W])
        self.loads = ((self.spread, io["c_spread"]), (self.bv, io[pre + "bv"]),
                      (self.raw, io[pre + "Wo"].rearrange("g p o -> p g o")))

    def move_sums(self, eng, k, sem, g, first, last):
        per = self.A // B
        for j in range(GH):
            row, h = j * HS + DH, j * NG + g
            eng.dma_start(self.sums[h * self.A + first * per:h * self.A + last * per, :],
                          k.AO[row:row + 1, g, first * S:last * S]).then_inc(sem, 16)


def heads_attend_phase(nc, k, o, layer, masked):
    with ExitStack() as ctx:
        ph = Phase(nc, ctx, f"att{layer}")
        Qs = ph.sb("Qs", [P, NG, GH, S], BF16)
        Ks = ph.sb("Ks", [P, NG, GH, S], BF16)
        Vg = ph.sb("Vg", [P, NG, TPB, GH, HS])
        probs = ph.sb("probs", [P, 2, GH, S])
        M = ph.sb("M", [P, 2, GH * TPB])
        pen = ph.sb("pen", [P, 2, TPB, S], BF16) if masked else None
        masked_scores = ph.sb("masked_scores", [P, 2, S]) if masked else None
        waiter = ph.sb("waiter", [P, GH * TPB])
        pen_copied = [ph.sem(f"pen_copied{i}") for i in range(2)]
        rest = ph.sb("rest", [P, GH * TPB])
        mparts = ph.sb("mparts", [P, 2, P], BF16)
        mT = ph.sb("mT", [MR * GH * TPB, 2, P], BF16)
        SA = ph.ps("SA", [P, 2, S])
        ST = ph.ps("ST", [P, 2, 2, S])
        O = ph.ps("O", [P, S])
        MT = ph.ps("MT", [P, 2 * S], BF16)
        qk_loaded = [ph.sem(f"qk_loaded{g}") for g in range(NG)]
        m_loaded = [ph.sem(f"m_loaded{g}") for g in range(NG)]
        v_copied = [ph.sem(f"v_copied{g}") for g in range(NG)]
        set_up, out_needs = ph.sem("set_up"), ph.sem("out_needs")
        sa_ready, sa_free, split = ph.sem("sa_ready"), ph.sem("sa_free"), ph.sem("split")
        m_turned, m_copied = ph.sem("m_turned"), ph.sem("m_copied")
        st_ready, exp_done, pv_done, o_copied = (ph.sem(n) for n in ("st_ready", "exp_done", "pv_done", "o_copied"))
        SPLIT = 4
        UA = GH * TPB

        LOADS = 16 * (len(runs_of_parts(Q_PARTS)) + len(runs_of_parts(K_PARTS)))

        def load_stack(eng, stack, parts, order, b, g):
            for row, part, n in runs_of_parts(order):
                eng.dma_start(stack[row * DH:(row + n) * DH, g],
                              parts[g * GH:(g + 1) * GH, part * DH:(part + n) * DH, bass.ds(b * S, S)].rearrange("h r t -> r h t")
                              ).then_inc(qk_loaded[g], 16)

        def later(b, g, d):
            return b + (g + d) // NG, (g + d) % NG

        with nc.Block() as block:

            @block.sync
            def _(sp):
                def load_stacks(b, g):
                    load_stack(sp, Qs, k.qparts, Q_PARTS, b, g)
                    load_stack(sp, Ks, k.kparts, K_PARTS, b, g)

                def place_maxima(b, g):
                    sp.wait_ge(m_copied, b * NG + g + 2)
                    sp.dma_start(Qs[SR:SR + MR, g], mT[:, g % 2, :]).then_inc(m_loaded[g], 16)

                def copy_pen(b, half):
                    sp.dma_start(pen[:, half], k.pen[:, bass.ds(b * TPB, TPB), :]).then_inc(pen_copied[half], 16)

                def clear_slots(b, g):
                    rows = k.xg.shape[0] // (B * NG)
                    per = -(-rows // P)
                    while rows % per:
                        per += 1
                    sp.dma_start(k.xg[bass.ds((b * NG + g) * rows, rows), :].rearrange("(p r) d -> p r d", r=per),
                                 k.zero[0:rows // per].unsqueeze(1).to_broadcast([rows // per, per, D])).then_inc(k.cleared, 16)

                def group(b, g, last):
                    if layer == 0:
                        clear_slots(b, g)
                    if masked and not last and g in (0, 2):
                        sp.wait_ge(sa_free, b * (NG * UA) + (g + 2) * UA + 2)
                        copy_pen(b + 1, g // 2)
                    if not (last and g == NG - 1):
                        place_maxima(*later(b, g, 1))
                    if not last:
                        sp.wait_ge(st_ready, b * (8 * NG) + 8 * (g + 1))
                        load_stacks(b + 1, g)

                for g in range(NG):
                    load_stack(sp, Qs, k.qparts, Q_PARTS, 0, g)
                if masked:
                    for half in range(2):
                        copy_pen(0, half)
                place_maxima(0, 0)
                for full, src in o.loads:
                    sp.dma_start(full[:], src).then_inc(out_needs, 16)
                with sp.Fori(0, B - 1) as b:
                    for g in range(NG):
                        group(b, g, False)
                for g in range(NG):
                    group(B - 1, g, True)
                    sp.wait_ge(o_copied, (B - 1) * NG + g + 1)
                    if g == 0:
                        for before in range(NG):
                            o.move_sums(sp, k, out_needs, before, 0, B - 1)
                    else:
                        o.move_sums(sp, k, out_needs, g - 1, B - 1, B)
                sp.wait_ge(o_copied, B * NG + 1)
                o.move_sums(sp, k, out_needs, NG - 1, B - 1, B)
                sp.wait_ge(out_needs, 16 * (len(o.loads) + 2 * H))

            @block.tensor
            def _(pe):
                def maxima_scores(b, g, j, qt):
                    if j == 0 and qt == 0:
                        pe.wait_ge(qk_loaded[g], b * LOADS + LOADS)
                    pe.wait_ge(sa_free, b * (NG * UA) + g * UA + j * TPB + qt + 1)
                    mm = nc.tensor.matmul(SA[:, qt % 2, :], Qs[0:SR, g, j, qt * P:(qt + 1) * P], Ks[0:SR, g, j, :],
                                          start=True, stop=True)
                    mm.then_inc(sa_ready, 1)

                def turn_maxima(b, g):
                    pe.wait_ge(split, b * (NG * SPLIT) + SPLIT * (g + 1))
                    pe.wait_ge(m_copied, b * NG + g + 1)
                    nc.tensor.transpose(MT[:, 0:P], mparts[:, g % 2, :], k.identb[:]
                                        ).then_inc(m_turned, 1)

                def turned_scores(b, g, kt, pair):
                    if kt == 0 and pair == 0:
                        pe.wait_ge(m_loaded[g], 16 * b + 16)
                    pe.wait_ge(exp_done, b * (8 * NG) + 8 * g + 2 * kt + pair + 1)
                    for i in range(2):
                        j = 2 * pair + i
                        mm = nc.tensor.matmul(ST[:, pair, i, :], Ks[0:SR + MR, g, j, kt * P:(kt + 1) * P],
                                              Qs[0:SR + MR, g, j, :], start=True, stop=not masked)
                        if masked:
                            mm = nc.tensor.matmul(ST[:, pair, i, :], k.identb[:], k.penT[:, b * TPB + kt, :],
                                                  start=False, stop=True)
                    mm.then_inc(st_ready, 1)

                def weigh_values(b, g, kt, heads):
                    for j in heads:
                        if kt == 0 and j == 0:
                            pe.wait_ge(o_copied, b * NG + g + 1)
                            pe.wait_ge(v_copied[g], b + 1)
                        if j % 2 == 0:
                            pe.wait_ge(exp_done, b * (8 * NG) + 8 * g + 2 * kt + j // 2 + 3)
                        mm = nc.tensor.matmul(O[j * HS:(j + 1) * HS, :], Vg[:, g, kt, j, :], probs[:, kt % 2, j, :],
                                              start=(kt == 0), stop=(kt == TPB - 1))
                    if heads[-1] == GH - 1:
                        mm.then_inc(pv_done, 1)

                def group(b, g, last):
                    for kt in range(TPB):
                        ahead = None if last and g >= NG - 2 else later(b, g, 2)
                        for i in range(2):
                            if ahead:
                                maxima_scores(*ahead, kt, i)
                            if kt < TPB - 1:
                                turned_scores(b, g, kt + 1, i)
                            elif not (last and g == NG - 1):
                                turned_scores(*later(b, g, 1), 0, i)
                        if ahead:
                            maxima_scores(*ahead, kt, 2)
                        weigh_values(b, g, kt, (0,))
                        if ahead:
                            maxima_scores(*ahead, kt, 3)
                        weigh_values(b, g, kt, (1, 2, 3))
                        if kt == 0 and not (last and g == NG - 1):
                            turn_maxima(*later(b, g, 1))

                pe.sem_inc(pv_done, 2)
                for j in range(GH):
                    for qt in range(TPB):
                        maxima_scores(0, 0, j, qt)
                for j in range(GH):
                    for qt in range(TPB):
                        maxima_scores(0, 1, j, qt)
                    if j == 0:
                        turn_maxima(0, 0)
                pe.wait_ge(set_up, 3)
                for pair in range(2):
                    turned_scores(0, 0, 0, pair)
                with pe.Fori(0, B - 1) as b:
                    for g in range(NG):
                        group(b, g, False)
                for g in range(NG):
                    group(B - 1, g, True)

            @block.vector
            def _(dve):
                def maxima(b, g, j):
                    if masked and j == 0:
                        dve.wait_ge(pen_copied[g // 2], b * 16 + 16)
                    for qt in range(TPB):
                        dve.wait_ge(sa_ready, b * (NG * UA) + g * UA + j * TPB + qt + 1)
                        c = j * TPB + qt
                        if masked:
                            nc.vector.memset(waiter[:, c:c + 1], 0.0)
                            ins = nc.vector.tensor_tensor_reduce(masked_scores[:, qt % 2, :], SA[:, qt % 2, :],
                                                                 pen[:, g // 2, qt, :], 1.0, 2 * NEG, ALU.add, ALU.max,
                                                                 M[:, g % 2, c:c + 1])
                        else:
                            ins = nc.vector.tensor_reduce(M[:, g % 2, c:c + 1], SA[:, qt % 2, :], AX.X, ALU.max)
                        ins.then_inc(sa_free, 1)

                def split_maxima(b, g):
                    m = M[:, g % 2, :]
                    parts = mparts[:, g % 2, 0:MR * UA].rearrange("p (a c) -> p a c", c=UA)
                    done = b * (NG * SPLIT) + SPLIT * g
                    dve.wait_ge(sa_free, b * (NG * UA) + (g + 1) * UA + 2)
                    nc.vector.tensor_scalar(parts[:, 0, :], m, -1.0, None, ALU.mult).then_inc(split, 1)
                    dve.wait_ge(split, done + 1)
                    nc.vector.scalar_tensor_tensor(out=rest[:], in0=m, scalar=-1.0, in1=parts[:, 0, :],
                                                   op0=ALU.mult, op1=ALU.subtract).then_inc(split, 1)
                    dve.wait_ge(split, done + 2)
                    nc.vector.tensor_copy(parts[:, 1, :], rest[:]).then_inc(split, 1)
                    dve.wait_ge(split, done + 3)
                    nc.vector.tensor_tensor(parts[:, 2, :], rest[:], parts[:, 1, :], ALU.subtract).then_inc(split, 1)

                def group(b, g):
                    for j in range(GH):
                        maxima(b, g, j)
                    split_maxima(b, g)

                dve.sem_inc(sa_free, 2)
                nc.vector.memset(mparts[:], 0.0)
                group(0, 0)
                group(0, 1)
                with dve.Fori(0, B - 1) as b:
                    for g in range(NG):
                        group(*later(b, g, 2))
                for g in range(NG - 2):
                    group(*later(B - 1, g, 2))

            @block.scalar
            def _(act):
                def exponentials(b, g, kt):
                    for pair in range(2):
                        act.wait_ge(st_ready, b * (8 * NG) + 8 * g + 2 * kt + pair + 1)
                        act.wait_ge(pv_done, b * (NG * TPB) + g * TPB + kt + 1)
                        nc.scalar.activation(probs[:, kt % 2, 2 * pair:2 * pair + 2, :], ST[:, pair], ACT.Exp
                                             ).then_inc(exp_done, 1)

                def copy_maxima(b, g):
                    act.wait_ge(m_turned, b * NG + g + 1)
                    nc.scalar.copy(mT[:, g % 2, :], MT[0:MR * UA, 0:P]).then_inc(m_copied, 1)

                def copy_out(b, g):
                    act.wait_ge(pv_done, b * (NG * TPB) + (g + 1) * TPB + 2)
                    nc.scalar.copy(k.AO[:, g, bass.ds(b * S, S)], O[:]).then_inc(o_copied, 1)

                def group(b, g, last):
                    for kt in range(TPB):
                        if kt < TPB - 1:
                            exponentials(b, g, kt + 1)
                        elif not (last and g == NG - 1):
                            exponentials(*later(b, g, 1), 0)
                        if kt == 1 and not (last and g == NG - 1):
                            copy_maxima(*later(b, g, 1))
                    copy_out(b, g)

                for g in range(NG):
                    load_stack(act, Ks, k.kparts, K_PARTS, 0, g)
                act.sem_inc(exp_done, 2)
                act.sem_inc(m_copied, 1)
                act.sem_inc(o_copied, 1)
                copy_maxima(0, 0)
                exponentials(0, 0, 0)
                with act.Fori(0, B - 1) as b:
                    for g in range(NG):
                        group(b, g, False)
                for g in range(NG):
                    group(B - 1, g, True)

            @block.gpsimd
            def _(pool):
                def copy_values(b, g):
                    src = k.V[:, bass.ds(b * TPB, TPB), g * GH * DH:(g + 1) * GH * DH]
                    nc.gpsimd.tensor_copy(Vg[:, g, :, :, 0:DH], src.rearrange("p t (j d) -> p t j d", d=DH)
                                          ).then_inc(v_copied[g], 1)

                nc.gpsimd.memset(Ks[SR:SR + MR], 1.0).then_inc(set_up, 1)
                pool.wait_ge(set_up, 1)
                nc.gpsimd.memset(Vg[:], 0.0).then_inc(set_up, 1)
                pool.wait_ge(set_up, 2)
                nc.gpsimd.memset(Vg[:, :, :, :, DH:DH + 1], 1.0).then_inc(set_up, 1)
                pool.wait_ge(set_up, 3)
                for g in range(NG):
                    copy_values(0, g)
                with pool.Fori(0, B - 1) as b:
                    for g in range(NG):
                        pool.wait_ge(pv_done, b * (NG * TPB) + (g + 1) * TPB + 2)
                        copy_values(b + 1, g)


def heads_output_phase(nc, k, o, layer):
    with ExitStack() as ctx:
        ph = Phase(nc, ctx, f"out{layer}")
        Wo = Pair.of(ph, "Wo", [P, NG, D])
        out = Pair.of(ph, "out", [P, 2, NG, S])
        spreadb = ph.sb("spreadb", [3 * H, NG, P], BF16)
        inv = ph.sb("inv", [P, o.W])
        parts = ph.sb("parts", [P, 3, o.W], BF16)
        rows = ph.sb("rows", [3 * H, N], BF16)
        R = ph.ps("R", [P, 2, S])
        Y = ph.ps("Y", [P, 4, S])
        spread_ready, r_ready, scaled, biased, high, split, y_ready, added, dve_step, w_high = (
            ph.sem(n) for n in ("spread_ready", "r_ready", "scaled", "biased", "high", "split", "y_ready", "added",
                                "dve_step", "w_high"))
        rows_there, part_ready = (ph.sem(n) for n in ("rows_there", "part_ready"))
        with nc.Block() as block:

            @block.sync
            def _(sp):
                for part in range(3):
                    sp.wait_ge(part_ready, part + 1)
                    sp.dma_start(rows[part * H:(part + 1) * H, :], parts[:, part, :]).then_inc(rows_there, 16)

            @block.tensor
            def _(pe):
                def spread_inverses(u):
                    c, g = divmod(u, NG)
                    if u >= 2:
                        pe.wait_ge(scaled, u - 1)
                    nc.tensor.matmul(R[:, u % 2, :], spreadb[:, g, :], rows[:, c * S:(c + 1) * S], start=True, stop=True
                                     ).then_inc(r_ready, 1)

                def project(c, i):
                    t = c * TPB + i
                    if i == 0:
                        pe.wait_ge(split, NG * (c + 1))
                    if t >= 4:
                        pe.wait_ge(added, t - 3)
                    for g in range(NG):
                        mm = product(nc, Y[:, t % 4, 0:D], out[:, c % 2, g, i * P:(i + 1) * P], Wo[:, g, :],
                                     g == 0, g == NG - 1)
                    mm.then_inc(y_ready, 1)

                pe.wait_ge(rows_there, 48)
                pe.wait_ge(spread_ready, 1)
                for u in range(NG + 1):
                    spread_inverses(u)
                pe.wait_ge(spread_ready, 2)
                for c in range(B):
                    for i in range(TPB):
                        u = (c + 1) * NG + i + 1
                        if u < (c + 2) * NG and u < B * NG:
                            spread_inverses(u)
                        project(c, i)
                    if (c + 2) * NG < B * NG:
                        spread_inverses((c + 2) * NG)

            @block.vector
            def _(dve):
                v = nc.vector
                step = Steps(dve, dve_step)
                step.after(v.reciprocal(inv[:], o.sums[:]))
                v.tensor_copy(parts[:, 0, :], inv[:]).then_inc(part_ready, 1)
                dve.wait_ge(part_ready, 1)
                step.after(v.tensor_tensor(inv[:], inv[:], parts[:, 0, :], ALU.subtract))
                v.tensor_copy(parts[:, 1, :], inv[:]).then_inc(part_ready, 1)
                dve.wait_ge(part_ready, 2)
                v.tensor_tensor(parts[:, 2, :], inv[:], parts[:, 1, :], ALU.subtract).then_inc(part_ready, 1)
                v.tensor_copy(spreadb[:], o.spread[:]).then_inc(spread_ready, 1)
                dve.wait_ge(w_high, 1)
                low_part(v, Wo[:], o.raw[:]).then_inc(spread_ready, 1)

                def scale(u):
                    c, g = divmod(u, NG)
                    a = k.AO[:, g, c * S:(c + 1) * S]
                    dve.wait_ge(r_ready, u + 1)
                    v.tensor_tensor(a, a, R[:, u % 2, :], ALU.mult).then_inc(scaled, 1)

                def add_out(t):
                    dve.wait_ge(y_ready, t + 1)
                    v.tensor_tensor(k.x[:, t, :], k.x[:, t, :], Y[:, t % 4, 0:D], ALU.add).then_inc(added, 1)
                    if t:
                        statistics(t - 1)

                def statistics(t):
                    dve.wait_ge(added, t + 1)
                    v.bn_stats(k.st[:, t, :], k.x[:, t, :])

                for u in range(NG + 1):
                    scale(u)
                for c in range(B):
                    for i in range(TPB):
                        u = (c + 1) * NG + i + 1
                        if u < (c + 2) * NG and u < B * NG:
                            scale(u)
                        add_out(c * TPB + i)
                    if (c + 2) * NG < B * NG:
                        scale((c + 2) * NG)
                statistics(NT - 1)

            @block.scalar
            def _(act):
                nc.scalar.copy(Wo.high[:], o.raw[:]).then_inc(w_high, 1)
                for u in range(B * NG):
                    c, g = divmod(u, NG)
                    act.wait_ge(scaled, u + 1)
                    if g == 0 and c >= 2:
                        act.wait_ge(y_ready, TPB * (c - 1))
                    a = k.AO[:, g, c * S:(c + 1) * S]
                    nc.scalar.activation(a, a, ACT.Identity, bias=o.bv[:, g:g + 1]).then_inc(biased, 1)
                    act.wait_ge(biased, u + 1)
                    nc.scalar.copy(out.high[:, c % 2, g, :], a).then_inc(high, 1)

            @block.gpsimd
            def _(pool):
                for u in range(B * NG):
                    c, g = divmod(u, NG)
                    pool.wait_ge(high, u + 1)
                    low_part(nc.gpsimd, out[:, c % 2, g, :], k.AO[:, g, c * S:(c + 1) * S]).then_inc(split, 1)


def normalised(nc, k, ctx, name, weights, keep_rows=False):
    ph = Phase(nc, ctx, name + "_kept")
    k.xnT = Pair.of(ph, "xnT", [P, KD, N])
    with ExitStack() as rows:
        k.xn = Phase(nc, ctx if keep_rows else rows, name + "_rows").sb("xn", [P, NT, D])
        layernorm_phase(nc, k, name, weights)


def heads_attention(nc, k, io, layer, rope=False, masked=False):
    with ExitStack() as ctx:
        ph = Phase(nc, ctx, f"heads{layer}")
        k.V = ph.sb("V", [P, NT, D])
        mask_kept = ctx.enter_context(ExitStack())
        if masked:
            k.pen = ph.sb("pen", [P, NT, S], BF16)
            k.penT = ph.sb("penT", [P, NT, S], BF16)
            mask = MaskRows(Phase(nc, mask_kept, "mask_rows"), io)
        with ExitStack() as inner:
            w = heads_weights(Phase(nc, inner, f"proj{layer}_w"), io, layer, rope)
            if masked:
                w.also = mask.load_first
            normalised(nc, k, inner, f"ln_att{layer}", w)
            heads_project_phase(nc, k, w, layer, rope)
        if masked:
            mask_phase(nc, k, mask)
        mask_kept.close()
        k.AO = ph.sb("AO", [P, NG, N])
        o = OutputNeeds(ph, io, layer)
        heads_attend_phase(nc, k, o, layer, masked)
        heads_output_phase(nc, k, o, layer)



def whole_attention(nc, k, io):
    with ExitStack() as ctx:
        ph = Phase(nc, ctx, "whole")
        k.phi = ph.sb("phi", [P, PHIS, S])
        k.phi_loaded = [ph.sem(f"phi_loaded{i}") for i in range(PHIS)]
        k.qT, k.kT = (Pair.of(ph, n, [P, KD, N]) for n in ("qT", "kT"))
        k.V = ph.sb("V", [P, NT, D])
        with ExitStack() as inner:
            w = Weights(Phase(nc, inner, "whole_w"))
            w.W = {n: w.pair(n, [P, KD, D], io["L3_xattn_" + n].rearrange("(c p) o -> p c o", p=P)) for n in ("Wq", "Wk", "Wv")}
            w.bias = {n: w.array(n, [P, KD], io["L3_xattn_" + n]) for n in ("bq", "bk")}
            normalised(nc, k, inner, "ln_whole", w)
            whole_project_phase(nc, k, io, w)
        whole_attend_phase(nc, k, io)


PHIS = 4


def load_phi(sp, k, io, t):
    b, i = divmod(t, TPB)
    sp.dma_start(k.phi[:, t % PHIS], io["fside_BxSxS2_0"][b, i * P:(i + 1) * P, :]).then_inc(k.phi_loaded[t % PHIS], 16)


def whole_project_phase(nc, k, io, w):
    W, bias = w.W, w.bias
    with ExitStack() as ctx:
        ph = Phase(nc, ctx, "whole_project")
        full = ph.sb("full", [P, 2, S])
        A = ph.ps("A", [P, 4, S])
        proj_ready, proj_taken, part_high, part_low = (ph.sem(n) for n in ("proj_ready", "proj_taken", "part_high", "part_low"))
        projections = [(w, m, cc) for w in ("q", "k") for m in range(KD) for cc in range(N // S)]
        NPJ = len(projections)
        with nc.Block() as block:

            @block.sync
            def _(sp):
                for t in range(PHIS):
                    load_phi(sp, k, io, t)

            @block.tensor
            def _(pe):
                for i, (w, m, cc) in enumerate(projections):
                    src = k.xnT if w == "q" else k.ctxT
                    if i >= 4:
                        pe.wait_ge(proj_taken, i - 3)
                    for kd in range(KD):
                        mm = product(nc, A[:, i % 4, :], W["W" + w][:, kd, m * P:(m + 1) * P],
                                     src[:, kd, cc * S:(cc + 1) * S], kd == 0, kd == KD - 1)
                    mm.then_inc(proj_ready, 1)
                for t in range(NT):
                    i = NPJ + t
                    pe.wait_ge(proj_taken, i - 3)
                    for kd in range(KD):
                        mm = product(nc, A[:, i % 4, 0:D], k.ctxT[:, kd, t * P:(t + 1) * P], W["Wv"][:, kd, :],
                                     kd == 0, kd == KD - 1)
                    mm.then_inc(proj_ready, 1)

            @block.vector
            def _(dve):
                for i, (w, m, cc) in enumerate(projections):
                    dve.wait_ge(proj_ready, i + 1)
                    if i >= 2:
                        dve.wait_ge(part_low, i - 1)
                    nc.vector.tensor_scalar(full[:, i % 2, :], A[:, i % 4, :], bias["b" + w][:, m:m + 1],
                                            D ** -0.5 if w == "q" else 1.0, ALU.add, ALU.mult).then_inc(proj_taken, 1)
                for t in range(NT):
                    dve.wait_ge(proj_ready, NPJ + t + 1)
                    nc.vector.tensor_copy(k.V[:, t, :], A[:, (NPJ + t) % 4, 0:D]).then_inc(proj_taken, 1)

            @block.scalar
            def _(act):
                for i, (w, m, cc) in enumerate(projections):
                    act.wait_ge(proj_taken, i + 1)
                    dst = (k.qT if w == "q" else k.kT)[:, m, cc * S:(cc + 1) * S]
                    nc.scalar.copy(dst.high, full[:, i % 2, :]).then_inc(part_high, 1)

            @block.gpsimd
            def _(pool):
                for i, (w, m, cc) in enumerate(projections):
                    pool.wait_ge(part_high, i + 1)
                    dst = (k.qT if w == "q" else k.kT)[:, m, cc * S:(cc + 1) * S]
                    low_part(nc.gpsimd, dst, full[:, i % 2, :]).then_inc(part_low, 1)


def whole_attend_phase(nc, k, io):
    pre = "L3_xattn_"
    with ExitStack() as ctx:
        ph = Phase(nc, ctx, "whole_attend")
        bv = ph.sb("bv", [P, D])
        beta = ph.sb("beta", [P, 3])
        c01, c = ph.sb("c01", [P, 1]), ph.sb("c", [P, 1])
        att = ph.sb("att", [P, 2, S])
        probs = ph.sb("probs", [P, 2, S])
        probsT = ph.sb("probsT", [P, 2, TPB, P])
        top, ntop = ph.sb("top", [P, NT]), ph.sb("ntop", [P, NT])
        total, inv = ph.sb("total", [P, NT]), ph.sb("inv", [P, NT])
        upd = ph.sb("upd", [P, 2, D])
        A = ph.ps("A", [P, 4, S])
        T = ph.ps("T", [P, 2, TPB, P])
        Y = ph.ps("Y", [P, 2, S])
        loaded, dve_step, added = ph.sem("loaded"), ph.sem("dve_step"), ph.sem("added")
        s_ready, s_taken, top_ready, exp_done = (ph.sem(n) for n in ("s_ready", "s_taken", "top_ready", "exp_done"))
        turned, turn_taken, y_ready, y_taken = (ph.sem(n) for n in ("turned", "turn_taken", "y_ready", "y_taken"))
        with nc.Block() as block:

            @block.sync
            def _(sp):
                sp.dma_start(beta[:], io[pre + "beta"]).then_inc(loaded, 16)
                sp.dma_start(bv[:], io[pre + "bv"]).then_inc(loaded, 16)
                for t in range(PHIS, NT):
                    sp.wait_ge(s_taken, t - PHIS + 1)
                    load_phi(sp, k, io, t)

            @block.tensor
            def _(pe):
                def scores(t):
                    if t >= 4:
                        pe.wait_ge(s_taken, t - 3)
                    for kd in range(KD):
                        mm = product(nc, A[:, t % 4, :], k.qT[:, kd, t * P:(t + 1) * P],
                                     k.kT[:, kd, (t // TPB) * S:(t // TPB + 1) * S], kd == 0, kd == KD - 1)
                    mm.then_inc(s_ready, 1)

                def turn(t):
                    pe.wait_ge(exp_done, t + 1)
                    if t >= 2:
                        pe.wait_ge(turn_taken, t - 1)
                    for kt in range(TPB):
                        mm = nc.tensor.transpose(T[:, t % 2, kt, :], probs[:, t % 2, kt * P:(kt + 1) * P], k.identf[:])
                    mm.then_inc(turned, 1)

                def weigh(t):
                    pe.wait_ge(turn_taken, t + 1)
                    if t >= 2:
                        pe.wait_ge(y_taken, t - 1)
                    for kt in range(TPB):
                        mm = nc.tensor.matmul(Y[:, t % 2, 0:D], probsT[:, t % 2, kt, :], k.V[:, (t // TPB) * TPB + kt, :],
                                              start=(kt == 0), stop=(kt == TPB - 1))
                    mm.then_inc(y_ready, 1)

                for t in range(NT + 3):
                    if t < NT:
                        scores(t)
                    if 2 <= t < NT + 2:
                        turn(t - 2)
                    if t >= 3:
                        weigh(t - 3)

            @block.vector
            def _(dve):
                step = Steps(dve, dve_step)
                dve.wait_ge(loaded, 32)
                step.after(nc.vector.tensor_tensor(c01[:], beta[:, 0:1], beta[:, 1:2], ALU.add))
                step.after(nc.vector.tensor_tensor(c[:], c01[:], beta[:, 2:3], ALU.subtract))

                def add_out(t):
                    dve.wait_ge(exp_done, t + 1)
                    step.after(nc.vector.reciprocal(inv[:, t:t + 1], total[:, t:t + 1]))
                    dve.wait_ge(y_ready, t + 1)
                    ins = nc.vector.scalar_tensor_tensor(out=upd[:, t % 2, :], in0=Y[:, t % 2, 0:D], scalar=inv[:, t:t + 1],
                                                         in1=bv[:], op0=ALU.mult, op1=ALU.add)
                    ins.then_inc(y_taken, 1)
                    dve.wait_ge(y_taken, t + 1)
                    nc.vector.tensor_tensor(k.x[:, t, :], k.x[:, t, :], upd[:, t % 2, :], ALU.add).then_inc(added, 1)
                    if t:
                        statistics(t - 1)

                def statistics(t):
                    dve.wait_ge(added, t + 1)
                    nc.vector.bn_stats(k.st[:, t, :], k.x[:, t, :])

                for t in range(NT):
                    dve.wait_ge(k.phi_loaded[t % PHIS], 16 * (t // PHIS + 1))
                    dve.wait_ge(s_ready, t + 1)
                    if t >= 2:
                        dve.wait_ge(exp_done, t - 1)
                    nc.vector.scalar_tensor_tensor(out=att[:, t % 2, :], in0=k.phi[:, t % PHIS, :], scalar=c[:, 0:1],
                                                   in1=A[:, t % 4, :], op0=ALU.mult, op1=ALU.add).then_inc(s_taken, 1)
                    dve.wait_ge(s_taken, t + 1)
                    step.after(nc.vector.tensor_reduce(top[:, t:t + 1], att[:, t % 2, :], AX.X, ALU.max))
                    nc.vector.tensor_scalar(ntop[:, t:t + 1], top[:, t:t + 1], -1.0, None, ALU.mult).then_inc(top_ready, 1)
                    if t >= 3:
                        add_out(t - 3)
                for t in range(NT - 3, NT):
                    add_out(t)
                statistics(NT - 1)

            @block.scalar
            def _(act):
                for t in range(NT):
                    act.wait_ge(top_ready, t + 1)
                    if t >= 2:
                        act.wait_ge(turned, t - 1)
                    nc.scalar.activation(probs[:, t % 2, :], att[:, t % 2, :], ACT.Exp, bias=ntop[:, t:t + 1],
                                         accum_out=total[:, t:t + 1]).then_inc(exp_done, 1)
                    if t >= 1:
                        act.wait_ge(turned, t)
                        nc.scalar.copy(probsT[:, (t - 1) % 2], T[:, (t - 1) % 2]).then_inc(turn_taken, 1)
                act.wait_ge(turned, NT)
                nc.scalar.copy(probsT[:, (NT - 1) % 2], T[:, (NT - 1) % 2]).then_inc(turn_taken, 1)



class Moe:

    def __init__(self, layer, gate, w1, w2, b1, b2, picks, units, size, chunk, func):
        self.layer, self.gate, self.w1, self.w2, self.b1, self.b2 = layer, gate, w1, w2, b1, b2
        self.picks, self.units, self.size, self.chunk, self.func = picks, units, size, chunk, func
        self.slots = units * size
        self.gate_biases = {0: 2, 2: 1, 3: 0}[layer]


E8 = 8
F = 1024
FT = F // P
CAP2 = int(S / E8 * 1.25)
CAP3 = int(2 * 1.25 * N / E8)
CAP3 += CAP3 % 2
SIZE0 = 2 * P
UNITS0 = (N + E8 * (SIZE0 - 1)) // SIZE0
UNITS0 += UNITS0 % 2
SIZE2 = B * CAP2
MOES = {
    0: Moe(0, "L0_ffn_gate_w", "L0_ffn_w1", "L0_ffn_w2", "L0_ffn_b1", "L0_ffn_b2", 1, UNITS0, SIZE0, SIZE0, ACT.Relu),
    2: Moe(2, "L2_ffn_Wr", "L2_ffn_W1", "L2_ffn_W2", "L2_ffn_b1", "L2_ffn_b2", 2, E8, SIZE2, SIZE2, ACT.Relu),
    3: Moe(3, "L3_ffn_w_g", "L3_ffn_c_fc", "L3_ffn_c_proj", None, None, 2, E8, CAP3, CAP3 // 2, ACT.Gelu),
}
GATHERS = 4
FAR = float(1 << 20)


def turn_logits(nc, k, logitsT, L, E):
    for t in range(NT):
        mm = nc.tensor.transpose(L[:, t, :], logitsT[:, t * P:(t + 1) * P], k.identf[0:E, 0:E])
    return mm


def route_phase(nc, k, w, moe, r):
    K = moe.picks
    with ExitStack() as ctx:
        ph = Phase(nc, ctx, f"route{moe.layer}")
        lg = ph.sb("lg", [P, NT, E8])
        tmp = ph.sb("tmp", [P, NT, E8])
        best = ph.sb("best", [P, NT, 8])
        col = ph.sb("col", [P, NT])
        ix = ph.sb("ix", [P, NT, 8], U32)
        ixf = ph.sb("ixf", [P, NT, 8])
        hot = ph.sb("hot", [P, K, NT, E8])
        counted = 1 if moe.layer == 2 else K
        hotb = ph.sb("hotb", [P, counted, NT, E8], BF16)
        rank_in = ph.sb("rank_in", [P, counted, NT, E8])
        runs, run = (B, TPB) if moe.layer == 2 else (1, counted * NT + 1)
        scan = ph.sb("scan", [P, 2, runs, run, E8])
        rank = ph.sb("rank", [P, NT])
        base = ph.sb("base", [P, NT])
        keep = ph.sb("keep", [P, NT])
        slot = ph.sb("slot", [P, NT])
        slot2 = ph.sb("slot2", [P, NT])
        nunit = ph.sb("nunit", [P, E8, 8])
        cnt = ph.sb("cnt", [P, E8])
        uend = ph.sb("uend", [P, E8 + 1])
        utab = ph.sb("utab", [P, moe.units, E8])
        uexp = ph.sb("uexp", [P, moe.units])
        L = ph.ps("L", [P, NT, E8])
        C = ph.ps("C", [P, 512])
        Z = ph.ps("Z", [P, 512])
        l_ready, hot_ready, c_ready, dve_step, act_done, act_asked = (
            ph.sem(n) for n in ("l_ready", "hot_ready", "c_ready", "dve_step", "act_done", "act_asked"))
        biases = moe.gate_biases
        per = E8 * NT
        with nc.Block() as block:

            @block.tensor
            def _(pe):
                turn_logits(nc, k, w.logitsT, L, E8).then_inc(l_ready, 1)
                pe.wait_ge(hot_ready, 1)
                flat = hotb[:].rearrange("p k t e -> p (k t e)")
                nc.tensor.matmul(C[:, 0:counted * per], k.before[:], flat, start=True, stop=True)
                nc.tensor.matmul(Z[:, 0:counted * per], k.onesb[:], flat, start=True, stop=True).then_inc(c_ready, 1)

            @block.scalar
            def _(act):
                if moe.layer == 2:
                    act.wait_ge(act_asked, 1)
                    nc.scalar.activation(lg[:], tmp[:], ACT.Exp).then_inc(act_done, 1)
                if moe.layer == 3:
                    act.wait_ge(act_asked, 1)
                    nc.scalar.activation(keep[:], col[:], ACT.Exp).then_inc(act_done, 1)

            @block.vector
            def _(dve):
                v = nc.vector
                step = Steps(dve, dve_step)
                wide = [P, NT, E8]

                def over(a):
                    return a.unsqueeze(2).to_broadcast(wide)

                dve.wait_ge(l_ready, 1)
                if biases:
                    step.after(v.tensor_tensor(lg[:], L[:], w.gbias[:, 0], ALU.add))
                    if biases == 2:
                        step.after(v.tensor_tensor(lg[:], lg[:], w.gbias[:, 1], ALU.add))
                else:
                    step.after(v.tensor_copy(lg[:], L[:]))
                if moe.layer == 2:
                    step.after(v.tensor_reduce(col[:], lg[:], AX.X, ALU.max))
                    v.tensor_tensor(tmp[:], lg[:], over(col[:]), ALU.subtract).then_inc(act_asked, 1)
                    dve.wait_ge(act_done, 1)
                    step.after(v.tensor_reduce(col[:], lg[:], AX.X, ALU.add))
                    step.after(v.reciprocal(col[:], col[:]))
                    step.after(v.tensor_tensor(lg[:], lg[:], over(col[:]), ALU.mult))
                for t in range(NT):
                    ins = v.max(best[:, t, :], lg[:, t, :])
                step.after(ins)
                for t in range(NT):
                    ins = v.max_index(ix[:, t, :], best[:, t, :], lg[:, t, :])
                step.after(ins)
                step.after(v.tensor_copy(ixf[:], ix[:]))
                if moe.layer == 2:
                    for p in range(K):
                        ins = v.tensor_copy(r.weight[:, p, :], best[:, :, p])
                elif moe.layer == 3:
                    v.tensor_tensor(col[:], best[:, :, 1], best[:, :, 0], ALU.subtract).then_inc(act_asked, 1)
                    dve.wait_ge(act_done, 1)
                    step.after(v.tensor_scalar(col[:], keep[:], 1.0, None, ALU.add))
                    step.after(v.reciprocal(r.weight[:, 0, :], col[:]))
                    ins = v.tensor_tensor(r.weight[:, 1, :], r.weight[:, 0, :], keep[:], ALU.mult)
                else:
                    ins = v.memset(r.weight[:], 1.0)
                step.after(ins)
                iota8 = k.iota[:, 0:E8].unsqueeze(1).to_broadcast(wide)
                for p in range(K):
                    ins = v.tensor_tensor(hot[:, p], iota8, ixf[:, :, p:p + 1].to_broadcast(wide), ALU.is_equal)
                step.after(ins)
                if moe.layer == 2:
                    ins = v.tensor_tensor(hotb[:, 0], hot[:, 0], hot[:, 1], ALU.add)
                else:
                    ins = v.tensor_copy(hotb[:], hot[:])
                ins.then_inc(hot_ready, 1)
                dve.wait_ge(c_ready, 1)
                counts = Z[:, 0:counted * per].rearrange("p (r t e) -> p r t e", r=runs, e=E8)
                v.memset(scan[:, 0, :, 0:1, :], 0.0)
                step.after(v.tensor_copy(scan[:, 0, :, 1:run, :], counts[:, :, 0:run - 1, :]))
                side, d = 0, 1
                while d < run:
                    v.tensor_copy(scan[:, 1 - side, :, 0:d, :], scan[:, side, :, 0:d, :])
                    step.after(v.tensor_tensor(scan[:, 1 - side, :, d:run, :], scan[:, side, :, d:run, :],
                                               scan[:, side, :, 0:run - d, :], ALU.add))
                    side, d = 1 - side, 2 * d
                off = scan[:, side].rearrange("p r t e -> p (r t) e")
                step.after(v.tensor_tensor(rank_in[:].rearrange("p k t e -> p (k t) e"), off[:, 0:counted * NT, :],
                                           C[:, 0:counted * per].rearrange("p (t e) -> p t e", e=E8), ALU.add))
                if moe.layer == 0:
                    step.after(v.tensor_scalar(cnt[:], off[:, NT, :], 1.0 / SIZE0, None, ALU.mult))
                    step.after(v.tensor_tensor(nunit[:], cnt[:].unsqueeze(2).to_broadcast([P, E8, 8]),
                                               k.iota[:, 0:8].unsqueeze(1).to_broadcast([P, E8, 8]), ALU.is_gt))
                    step.after(v.tensor_reduce(cnt[:], nunit[:], AX.X, ALU.add))
                    step.after(v.memset(uend[:], 0.0))
                    for e in range(E8):
                        step.after(v.tensor_tensor(uend[:, e + 1:e + 2], uend[:, e:e + 1], cnt[:, e:e + 1], ALU.add))
                    step.after(v.tensor_tensor(utab[:], k.iota[:, 0:moe.units].unsqueeze(2).to_broadcast([P, moe.units, E8]),
                                               uend[:, 1:].unsqueeze(1).to_broadcast([P, moe.units, E8]), ALU.is_ge))
                    step.after(v.tensor_reduce(uexp[:], utab[:], AX.X, ALU.add))
                    step.after(v.tensor_scalar(uexp[:], uexp[:], E8 - 1.0, None, ALU.min))
                    step.after(v.tensor_copy(r.unit_expert[:], uexp[:]))
                    step.after(v.tensor_tensor(tmp[:], hot[:, 0], uend[:, 0:E8].unsqueeze(1).to_broadcast(wide), ALU.mult))
                    step.after(v.tensor_reduce(base[:], tmp[:], AX.X, ALU.add))
                    step.after(v.tensor_scalar(base[:], base[:], float(SIZE0), None, ALU.mult))
                for p in range(K):
                    step.after(v.tensor_tensor(tmp[:], hot[:, p], rank_in[:, p % counted], ALU.mult))
                    step.after(v.tensor_reduce(rank[:], tmp[:], AX.X, ALU.add))
                    if moe.layer != 0:
                        step.after(v.tensor_scalar(base[:], ixf[:, :, p], float(moe.size), None, ALU.mult))
                    if moe.layer == 2:
                        for b in range(1, B):
                            sl = base[:, b * TPB:(b + 1) * TPB]
                            ins = v.tensor_scalar(sl, sl, float(b * CAP2), None, ALU.add)
                        step.after(ins)
                    cap = {0: float(N + 1), 2: float(CAP2), 3: float(CAP3)}[moe.layer]
                    v.tensor_tensor(slot[:], rank[:], base[:], ALU.add)
                    step.after(v.tensor_scalar(keep[:], rank[:], cap, None, ALU.is_lt))
                    v.tensor_tensor(r.weight[:, p, :], r.weight[:, p, :], keep[:], ALU.mult)
                    step.after(v.tensor_tensor(slot[:], slot[:], keep[:], ALU.mult))
                    v.tensor_copy(r.take[:, p, :], slot[:])
                    step.after(v.tensor_scalar(keep[:], keep[:], -FAR, FAR, ALU.mult, ALU.add))
                    step.after(v.tensor_tensor(slot2[:], slot[:], keep[:], ALU.add))
                    step.after(v.tensor_copy(r.put[:, p, :], slot2[:]))


class Matrices:

    def __init__(self, ph):
        self.raw1, self.raw2 = ph.sb("raw1", [P, 2, KD, F]), ph.sb("raw2", [P, 2, FT, D])
        self.W1, self.W2 = Pair.of(ph, "W1", [P, 2, KD, F]), Pair.of(ph, "W2", [P, 2, FT, D])


def unit_expert(sp, moe, r, u):
    if moe.layer == 0:
        return sp.value_load(r.unit_expert[0:1, bass.ds(u, 1)], min_val=0, max_val=E8 - 1)
    return u


def first_matrix(io, moe, e):
    return io[moe.w1][bass.ds(e, 1)].rearrange("e (c p) f -> p (e c) f", p=P)


def second_matrix(io, moe, e):
    return io[moe.w2][bass.ds(e, 1)].rearrange("e (f p) d -> p (e f) d", p=P)


def dispatch_phase(nc, k, io, moe, r, m):
    k.n_scattered += NT * moe.picks
    with ExitStack() as ctx:
        ph = Phase(nc, ctx, f"dispatch{moe.layer}")
        loaded = [ph.sem(f"loaded{w}") for w in (1, 2)]
        high, split = ph.sem("high"), ph.sem("split")
        matrices = ((m.raw1, m.W1), (m.raw2, m.W2))
        block = ctx.enter_context(nc.Block())

        @block.sync
        def _(sp):
            e = unit_expert(sp, moe, r, 0)
            sp.dma_start(m.raw1[:, 0], first_matrix(io, moe, e)).then_inc(loaded[0], 16)
            sp.dma_start(m.raw2[:, 0], second_matrix(io, moe, e)).then_inc(loaded[1], 16)

        @block.scalar
        def _(act):
            for w, (raw, W) in enumerate(matrices):
                act.wait_ge(loaded[w], 16)
                nc.scalar.copy(W.high[:, 0], raw[:, 0]).then_inc(high, 1)

        @block.vector
        def _(dve):
            for w, (raw, W) in enumerate(matrices):
                dve.wait_ge(high, w + 1)
                low_part(nc.vector, W[:, 0], raw[:, 0]).then_inc(split, 1)
            dve.wait_ge(split, 2)

        @block.gpsimd
        def _(pool):
            for t in range(NT):
                for p in range(moe.picks):
                    if t == 0 and p == 0:
                        pool.wait_ge(k.cleared, 16 * B * NG)
                    pool.indirect_dma_start(out=k.xg[0:moe.slots, :],
                                            out_offset=bass.IndirectOffsetOnAxis(ap=r.put[:, p, t:t + 1], axis=0),
                                            in_=k.xn[:, t, :], in_offset=None, bounds_check=moe.slots - 1,
                                            oob_is_err=False).then_inc(k.scattered, 16)
            pool.wait_ge(k.scattered, 16 * k.n_scattered)


def combine_phase(nc, k, moe, r, out=None):
    with ExitStack() as ctx:
        ph = Phase(nc, ctx, f"combine{moe.layer}")
        g = ph.sb("g", [P, GATHERS, D])
        added, stored = ph.sem("added"), ph.sem("stored")
        todo = [(t, p) for t in range(NT) for p in range(moe.picks)]
        before = k.n_gathered
        k.n_gathered += len(todo) // GATHERS
        with nc.Block() as block:

            @block.gpsimd
            def _(pool):
                for i, (t, p) in enumerate(todo):
                    if i >= GATHERS:
                        pool.wait_ge(added, i - GATHERS + 1)
                    pool.indirect_dma_start(out=g[:, i % GATHERS, :], out_offset=None, in_=k.yg[0:moe.slots, :],
                                            in_offset=bass.IndirectOffsetOnAxis(ap=r.take[:, p, t:t + 1], axis=0),
                                            bounds_check=moe.slots - 1, oob_is_err=False
                                            ).then_inc(k.gathered[i % GATHERS], 16)

            @block.vector
            def _(dve):
                def statistics(t):
                    dve.wait_ge(added, (t + 1) * moe.picks)
                    nc.vector.bn_stats(k.st[:, t, :], k.x[:, t, :])

                for i, (t, p) in enumerate(todo):
                    dve.wait_ge(k.gathered[i % GATHERS], 16 * (before + i // GATHERS + 1))
                    if p:
                        dve.wait_ge(added, i)
                    nc.vector.scalar_tensor_tensor(out=k.x[:, t, :], in0=g[:, i % GATHERS, :],
                                                   scalar=r.weight[:, p, t:t + 1], in1=k.x[:, t, :],
                                                   op0=ALU.mult, op1=ALU.add).then_inc(added, 1)
                    if out is None and p == moe.picks - 1 and t:
                        statistics(t - 1)
                if out is None:
                    statistics(NT - 1)

            @block.sync
            def _(sp):
                if out is not None:
                    for t in range(0, NT, 2):
                        sp.wait_ge(added, (t + 2) * moe.picks)
                        sp.dma_start(out.rearrange("b (t p) d -> p (b t) d", p=P)[:, t:t + 2, :], k.x[:, t:t + 2, :]
                                     ).then_inc(stored, 16)
                    sp.wait_ge(stored, 16 * (NT // 2))


def experts_phase(nc, k, io, moe, r, m):
    n_t = -(-moe.size // P)
    padded = n_t * P
    parted = [(0, moe.size // P * P)] + ([(moe.size // P * P, moe.size)] if moe.size % P else [])
    CH = moe.chunk
    n_ch = moe.size // CH
    biased = moe.b1 is not None
    HR = 4
    with ExitStack() as ctx:
        ph = Phase(nc, ctx, f"experts{moe.layer}")
        raw1, raw2, W1, W2 = m.raw1, m.raw2, m.W1, m.W2
        b1 = ph.sb("b1", [P, 2, FT])
        b2 = ph.sb("b2", [P, 2, D])
        xg = ph.sb("xg", [P, 2, n_t, D])
        xgT = Pair.of(ph, "xgT", [P, 2, KD, padded])
        h = ph.sb("h", [P, HR, CH])
        hT = Pair.of(ph, "hT", [P, FT, padded])
        y = ph.sb("y", [P, 2, n_t, D])
        T = ph.ps("T", [P, 2, KD, 2 * P])
        Hb = ph.ps("Hb", [P, HR, S])
        Y = ph.ps("Y", [P, 2, S])
        w1_loaded, w2_loaded = ([ph.sem(f"w{w}_loaded{i}") for i in range(2)] for w in (1, 2))
        w1_high, w2_high, w1_split, w2_split = (ph.sem(n) for n in ("w1_high", "w2_high", "w1_split", "w2_split"))
        x_loaded = [ph.sem(f"x_loaded{i}") for i in range(2)]
        b_loaded = [ph.sem(f"b_loaded{i}") for i in range(2)]
        stored = [ph.sem(f"stored{i}") for i in range(2)]
        turned, turn_high, turn_taken, h_ready, h_taken, h_high, h_split, y_ready, y_taken = (
            ph.sem(n) for n in ("turned", "turn_high", "turn_taken", "h_ready", "h_taken", "h_high", "h_split",
                                "y_ready", "y_taken"))
        HU = FT * n_ch
        PAIRS = moe.units // 2

        def unit_pairs(eng, unit):
            with eng.Fori(0, PAIRS - 1) as pair:
                for i in range(2):
                    unit(pair, i, False)
            for i in range(2):
                unit(PAIRS - 1, i, i == 1)

        with nc.Block() as block:

            @block.sync
            def _(sp):
                def load_matrices(pair, i):
                    e = unit_expert(sp, moe, r, pair * 2 + i)
                    reused = not isinstance(pair, int) or pair > 0
                    if reused:
                        sp.wait_ge(w1_split, pair * 2 + i - 1)
                    sp.dma_start(raw1[:, i], first_matrix(io, moe, e)).then_inc(w1_loaded[i], 16)
                    if reused:
                        sp.wait_ge(w2_split, pair * 2 + i - 1)
                    sp.dma_start(raw2[:, i], second_matrix(io, moe, e)).then_inc(w2_loaded[i], 16)

                def load_tokens(pair, i):
                    if not isinstance(pair, int) or pair > 0:
                        sp.wait_ge(turned, (pair * 2 + i - 1) * n_t)
                    sp.dma_start(xg[:, i], k.xg[bass.ds((pair * 2 + i) * moe.size, padded), :]
                                 .rearrange("(t p) d -> p t d", p=P)).then_inc(x_loaded[i], 16)

                def load_biases(pair, i):
                    if biased:
                        e = unit_expert(sp, moe, r, pair * 2 + i)
                        sp.dma_start(b1[:, i, :], io[moe.b1][bass.ds(e, 1)].rearrange("e p f -> p (e f)")
                                     ).then_inc(b_loaded[i], 16)
                        sp.dma_start(b2[:, i, :], io[moe.b2][bass.ds(e, 1)].rearrange("e p d -> p (e d)")
                                     ).then_inc(b_loaded[i], 16)

                def store(pair, i):
                    sp.wait_ge(y_taken, pair * (2 * n_t) + (i + 1) * n_t + 2)
                    for lo, hi in parted:
                        rows = min(P, hi - lo)
                        sp.dma_start(k.yg[bass.ds((pair * 2 + i) * moe.size + lo, hi - lo), :]
                                     .rearrange("(t p) d -> p t d", p=rows), y[0:rows, i, lo // P:-(-hi // P)]
                                     ).then_inc(stored[i], 16)

                def around(pair, i, first=False, last=False):
                    if not last:
                        load_matrices(pair + 1, i)
                        load_tokens(pair + 1, i)
                    if not (first and i == 0):
                        store(pair - 1 + i, 1 - i)
                    if not (last and i == 1):
                        load_biases(pair + i, 1 - i)

                for i in range(2):
                    sp.sem_inc((w1_loaded, w2_loaded)[i][0], 16)
                load_tokens(0, 0)
                load_biases(0, 0)
                load_matrices(0, 1)
                load_tokens(0, 1)
                for i in range(2):
                    around(0, i, first=True)
                with sp.Fori(1, PAIRS - 1) as pair:
                    for i in range(2):
                        around(pair, i)
                for i in range(2):
                    around(PAIRS - 1, i, last=True)
                store(PAIRS - 1, 1)
                for i in range(2):
                    sp.wait_ge(stored[i], 16 * len(parted) * (PAIRS + 1))

            @block.tensor
            def _(pe):
                def turn(pair, i, t):
                    j = i * n_t + t
                    if t == 0:
                        pe.wait_ge(x_loaded[i], pair * 16 + 16)
                    pe.wait_ge(turn_taken, pair * (2 * n_t) + j + 1)
                    for c in range(KD):
                        mm = nc.tensor.transpose(T[:, j % 2, c, 0:P], xg[:, i, t, c * P:(c + 1) * P], k.identf[:])
                    mm.then_inc(turned, 1)

                def first(pair, i):
                    pe.wait_ge(w1_split, pair * 2 + i + 1)
                    pe.wait_ge(turn_taken, pair * (2 * n_t) + (i + 1) * n_t + 2)
                    for f in range(FT):
                        for ch in range(n_ch):
                            j = i * HU + f * n_ch + ch
                            pe.wait_ge(h_taken, pair * (2 * HU) + j + 1)
                            for kd in range(KD):
                                mm = product(nc, Hb[:, j % HR, 0:CH], W1[:, i, kd, f * P:(f + 1) * P],
                                             xgT[:, i, kd, ch * CH:(ch + 1) * CH], kd == 0, kd == KD - 1)
                            mm.then_inc(h_ready, 1)

                def second(pair, i, last):
                    pe.wait_ge(w2_split, pair * 2 + i + 1)
                    for t in range(n_t):
                        if not last:
                            turn(pair + i, 1 - i, t)
                        j = i * n_t + t
                        pe.wait_ge(y_taken, pair * (2 * n_t) + j + 1)
                        for f in range(FT):
                            if t == 0:
                                pe.wait_ge(h_split, pair * (2 * HU) + i * HU + (f + 1) * n_ch + HR)
                            mm = product(nc, Y[:, j % 2, 0:D], hT[:, f, t * P:(t + 1) * P], W2[:, i, f, :],
                                         f == 0, f == FT - 1)
                        mm.then_inc(y_ready, 1)

                def unit(pair, i, last):
                    first(pair, i)
                    second(pair, i, last)

                for t in range(n_t):
                    turn(0, 0, t)
                unit_pairs(pe, unit)

            @block.scalar
            def _(act):
                def matrix_high(pair, i, which):
                    raw, W, loaded, high = ((raw1, W1, w1_loaded, w1_high), (raw2, W2, w2_loaded, w2_high))[which]
                    act.wait_ge(loaded[i], pair * 16 + 16)
                    nc.scalar.copy(W.high[:, i], raw[:, i]).then_inc(high, 1)

                def hidden(pair, i):
                    if biased:
                        act.wait_ge(b_loaded[i], pair * 32 + 32)
                    for f in range(FT):
                        for ch in range(n_ch):
                            j = i * HU + f * n_ch + ch
                            act.wait_ge(h_ready, pair * (2 * HU) + j + 1)
                            act.wait_ge(h_split, pair * (2 * HU) + j + 1)
                            nc.scalar.activation(h[:, j % HR, :], Hb[:, j % HR, 0:CH], moe.func,
                                                 bias=b1[:, i, f:f + 1] if biased else 0.0).then_inc(h_taken, 1)

                def turned_high(pair, i, tiles):
                    for t in tiles:
                        j = i * n_t + t
                        act.wait_ge(turned, pair * (2 * n_t) + j + 1)
                        nc.scalar.copy(xgT.high[:, i, :, t * P:(t + 1) * P], T[:, j % 2, :, 0:P]).then_inc(turn_high, 1)

                def unit(pair, i, last):
                    if not last:
                        matrix_high(pair + i, 1 - i, 0)
                    hidden(pair, i)
                    if not last:
                        turned_high(pair + i, 1 - i, range(n_t - 1))
                        matrix_high(pair + i, 1 - i, 1)
                        turned_high(pair + i, 1 - i, [n_t - 1])

                act.sem_inc(h_taken, HR)
                act.sem_inc(w1_high, 1)
                act.sem_inc(w2_high, 1)
                turned_high(0, 0, range(n_t))
                unit_pairs(act, unit)

            @block.gpsimd
            def _(pool):
                def unit(pair, i, last):
                    if not last:
                        pool.wait_ge(w1_high, (pair + i) * 2 + (1 - i) + 1)
                        low_part(nc.gpsimd, W1[:, 1 - i], raw1[:, 1 - i]).then_inc(w1_split, 1)

                pool.sem_inc(w1_split, 1)
                unit_pairs(pool, unit)

            @block.vector
            def _(dve):
                def cut_hidden(pair, i):
                    def part(n):
                        f, ch = divmod(n, n_ch)
                        return hT[:, f, ch * CH:(ch + 1) * CH]

                    for n in range(HU + 1):
                        j = i * HU + n
                        if n < HU:
                            dve.wait_ge(h_taken, pair * (2 * HU) + j + 1 + HR)
                            nc.vector.tensor_copy(part(n).high, h[:, j % HR, :]).then_inc(h_high, 1)
                        if n:
                            dve.wait_ge(h_high, pair * (2 * HU) + j)
                            low_part(nc.vector, part(n - 1), h[:, (j - 1) % HR, :]).then_inc(h_split, 1)

                def take_turned(pair, i, t):
                    j = i * n_t + t
                    dve.wait_ge(turn_high, pair * (2 * n_t) + j + 1)
                    low_part(nc.vector, xgT[:, i, :, t * P:(t + 1) * P], T[:, j % 2, :, 0:P]).then_inc(turn_taken, 1)

                def take_out(pair, i, t):
                    j = i * n_t + t
                    if t == 0:
                        dve.wait_ge(stored[i], (pair + 1) * (16 * len(parted)))
                        if biased:
                            dve.wait_ge(b_loaded[i], pair * 32 + 32)
                    dve.wait_ge(y_ready, pair * (2 * n_t) + j + 1)
                    if biased:
                        ins = nc.vector.tensor_tensor(y[:, i, t, :], Y[:, j % 2, 0:D], b2[:, i, :], ALU.add)
                    else:
                        ins = nc.vector.tensor_copy(y[:, i, t, :], Y[:, j % 2, 0:D])
                    ins.then_inc(y_taken, 1)

                def matrix_low(pair, i):
                    dve.wait_ge(w2_high, pair * 2 + i + 1)
                    low_part(nc.vector, W2[:, i], raw2[:, i]).then_inc(w2_split, 1)

                def unit(pair, i, last):
                    cut_hidden(pair, i)
                    out = 0
                    if not last:
                        for t in range(n_t - 1):
                            take_turned(pair + i, 1 - i, t)
                            if t:
                                take_out(pair, i, out)
                                out += 1
                        matrix_low(pair + i, 1 - i)
                        take_turned(pair + i, 1 - i, n_t - 1)
                    for t in range(out, n_t):
                        take_out(pair, i, t)

                for i in range(2):
                    dve.sem_inc(stored[i], 16 * len(parted))
                if padded > moe.size:
                    for part in (hT.high, hT.low):
                        nc.vector.memset(part[:, :, moe.size:padded].bitcast(F32), 0.0)
                dve.sem_inc(turn_taken, 2)
                dve.sem_inc(y_taken, 2)
                dve.sem_inc(h_split, HR)
                dve.sem_inc(w2_split, 1)
                for t in range(n_t):
                    take_turned(0, 0, t)
                unit_pairs(dve, unit)


class Routes:
    pass


def slot_moe(nc, k, io, moe, out):
    with ExitStack() as ctx:
        ph = Phase(nc, ctx, f"moe{moe.layer}")
        r = Routes()
        r.weight = ph.sb("weight", [P, moe.picks, NT])
        r.take = ph.sb("take", [P, moe.picks, NT], U32)
        r.put = ph.sb("put", [P, moe.picks, NT], U32)
        r.unit_expert = ph.sb("unit_expert", [P, moe.units], I32)
        with ExitStack() as matrices_kept:
            m = Matrices(Phase(nc, matrices_kept, f"matrices{moe.layer}"))
            with ExitStack() as inner:
                w = Weights(Phase(nc, inner, f"route{moe.layer}_w"))
                w.gate_of(E8, io[moe.gate].rearrange("(c p) e -> p c e", p=P), m.raw1[0:E8, 1].rearrange("e c f -> e (c f)"))
                if moe.gate_biases:
                    w.gbias = w.array("gbias", [P, moe.gate_biases, NT, E8], io[f"gbias{moe.layer}"])
                normalised(nc, k, inner, f"ln_moe{moe.layer}", w, keep_rows=True)
                route_phase(nc, k, w, moe, r)
                dispatch_phase(nc, k, io, moe, r, m)
            experts_phase(nc, k, io, moe, r, m)
        combine_phase(nc, k, moe, r, out)


E32, GRP, PICKS1, GRPS = 32, 8, 8, 4
ESZ = E32 // GRP
SCALE1 = 2.5
SHARED = 2


def group_route_phase(nc, k, w, r):
    with ExitStack() as ctx:
        ph = Phase(nc, ctx, "route1")
        gbias = w.gbias
        sc = ph.sb("sc", [P, NT, E32])
        sb = ph.sb("sb", [P, NT, E32])
        ab = [ph.sb(f"ab{i}", [P, NT, GRP]) for i in range(6)]
        grp = ph.sb("grp", [P, NT, GRP])
        best = ph.sb("best", [P, NT, 8])
        ix = ph.sb("ix", [P, NT, 8], U32)
        ixf = ph.sb("ixf", [P, NT, 8])
        gm = ph.sb("gm", [P, NT, GRP])
        one = ph.sb("one", [P, NT, E32])
        comb = ph.sb("comb", [P, NT, E32])
        sums = ph.sb("sums", [P, NT])
        parts = ph.sb("parts", [P, NT, 3, E32], BF16)
        L = ph.ps("L", [P, NT, E32])
        T = ph.ps("T", [3 * E32, 2, 2 * S], BF16)
        l_ready, sig_done, dve_step, parts_ready, turned, taken = (
            ph.sem(n) for n in ("l_ready", "sig_done", "dve_step", "parts_ready", "turned", "taken"))
        with nc.Block() as block:

            @block.tensor
            def _(pe):
                turn_logits(nc, k, w.logitsT, L, E32).then_inc(l_ready, 1)
                pe.wait_ge(parts_ready, 1)
                for q in range(NT // TPB):
                    if q >= 2:
                        pe.wait_ge(taken, q - 1)
                    for i in range(TPB):
                        t = q * TPB + i
                        mm = nc.tensor.transpose(T[:, q % 2, i * P:(i + 1) * P], parts[:, t].rearrange("p a e -> p (a e)"),
                                                 k.identb[:])
                    mm.then_inc(turned, 1)

            @block.scalar
            def _(act):
                act.wait_ge(l_ready, 1)
                nc.scalar.activation(sc[:], L[:], ACT.Sigmoid).then_inc(sig_done, 1)
                for q in range(NT // TPB):
                    act.wait_ge(turned, q + 1)
                    nc.scalar.copy(r.combT[:, q * S:(q + 1) * S], T[:, q % 2, 0:S]).then_inc(taken, 1)

            @block.vector
            def _(dve):
                v = nc.vector
                step = Steps(dve, dve_step)
                dve.wait_ge(sig_done, 1)
                step.after(v.tensor_tensor(sb[:], sc[:], gbias[:], ALU.add))
                s4 = sb[:].rearrange("p t (g m) -> p t g m", m=ESZ)
                v.tensor_tensor(ab[0][:], s4[:, :, :, 0], s4[:, :, :, 1], ALU.max)
                v.tensor_tensor(ab[1][:], s4[:, :, :, 0], s4[:, :, :, 1], ALU.min)
                v.tensor_tensor(ab[2][:], s4[:, :, :, 2], s4[:, :, :, 3], ALU.max)
                step.after(v.tensor_tensor(ab[3][:], s4[:, :, :, 2], s4[:, :, :, 3], ALU.min))
                v.tensor_tensor(ab[4][:], ab[0][:], ab[2][:], ALU.max)
                v.tensor_tensor(ab[5][:], ab[0][:], ab[2][:], ALU.min)
                step.after(v.tensor_tensor(ab[1][:], ab[1][:], ab[3][:], ALU.max))
                step.after(v.tensor_tensor(ab[5][:], ab[5][:], ab[1][:], ALU.max))
                step.after(v.tensor_tensor(grp[:], ab[4][:], ab[5][:], ALU.add))
                for t in range(NT):
                    ins = v.max(best[:, t, :], grp[:, t, :])
                step.after(ins)
                for t in range(NT):
                    ins = v.max_index(ix[:, t, :], best[:, t, :], grp[:, t, :])
                step.after(ins)
                step.after(v.tensor_copy(ixf[:], ix[:]))
                step.after(v.memset(gm[:], 0.0))
                wide = [P, NT, GRP]
                iota8 = k.iota[:, 0:GRP].unsqueeze(1).to_broadcast(wide)
                for p in range(GRPS):
                    step.after(v.tensor_tensor(grp[:], iota8, ixf[:, :, p:p + 1].to_broadcast(wide), ALU.is_equal))
                    step.after(v.tensor_tensor(gm[:], gm[:], grp[:], ALU.add))
                for m in range(ESZ):
                    ins = v.tensor_tensor(s4[:, :, :, m], s4[:, :, :, m], gm[:], ALU.mult)
                step.after(ins)
                for t in range(NT):
                    ins = v.max(best[:, t, :], sb[:, t, :])
                step.after(ins)
                for t in range(NT):
                    ins = v.max_index(ix[:, t, :], best[:, t, :], sb[:, t, :])
                step.after(ins)
                step.after(v.tensor_copy(ixf[:], ix[:]))
                step.after(v.memset(comb[:], 0.0))
                wide = [P, NT, E32]
                iota32 = k.iota[:, 0:E32].unsqueeze(1).to_broadcast(wide)
                for p in range(PICKS1):
                    step.after(v.tensor_tensor(one[:], iota32, ixf[:, :, p:p + 1].to_broadcast(wide), ALU.is_equal))
                    step.after(v.tensor_tensor(comb[:], comb[:], one[:], ALU.add))
                step.after(v.tensor_tensor(comb[:], comb[:], sc[:], ALU.mult))
                step.after(v.tensor_reduce(sums[:], comb[:], AX.X, ALU.add))
                step.after(v.tensor_scalar(sums[:], sums[:], 1e-20, None, ALU.add))
                step.after(v.reciprocal(sums[:], sums[:]))
                step.after(v.tensor_tensor(comb[:], comb[:], sums[:].unsqueeze(2).to_broadcast(wide), ALU.mult))
                step.after(v.tensor_scalar(comb[:], comb[:], SCALE1, None, ALU.mult))
                step.after(v.tensor_copy(parts[:, :, 0, :], comb[:]))
                step.after(v.tensor_tensor(comb[:], comb[:], parts[:, :, 0, :], ALU.subtract))
                step.after(v.tensor_copy(parts[:, :, 1, :], comb[:]))
                v.tensor_tensor(parts[:, :, 2, :], comb[:], parts[:, :, 1, :], ALU.subtract).then_inc(parts_ready, 1)


def gated_experts_phase(nc, k, io, r):
    NE = E32 + SHARED
    NW = 4

    NHID = 3

    def slot_before(e, slots=NW):
        return e - slots if e >= slots else max(f for f in range(NE) if f % slots == e) - NE

    WID = 2 * KD * P + D
    with ExitStack() as ctx:
        ph = Phase(nc, ctx, "experts1")
        raw = ph.sb("raw", [P, NW, WID])
        W = Pair.of(ph, "W", [P, NW, WID])
        sil = ph.sb("sil", [P, 2, S])
        prod = ph.sb("prod", [P, 2, S])
        full = ph.sb("full", [P, 2, S])
        hid = Pair.of(ph, "hid", [P, NHID, S])
        picks = ph.sb("picks", [3 * E32, E32, P])
        pick = ph.sb("pick", [3 * E32, E32, P], BF16)
        G, U = ph.ps("G", [P, 2, S]), ph.ps("U", [P, 2, S])
        CB = ph.ps("CB", [P, 2, S])
        Y = ph.ps("Y", [P, 2, 2, D])
        p_loaded, p_ready = ph.sem("p_loaded"), ph.sem("p_ready")
        w_loaded = [ph.sem(f"w_loaded{i}") for i in range(NW)]
        w_high, w_split, gu_ready, sil_done, prod_done, full_done, hid_high, hid_done, down_done = (
            ph.sem(n) for n in ("w_high", "w_split", "gu_ready", "sil_done", "prod_done", "full_done", "hid_high",
                                "hid_done", "down_done"))
        y_added = ph.sem("y_added")
        NC = N // S

        def matrices(i):
            gate, up = (Pair(*(a[:, i, o * KD * P:(o + 1) * KD * P].rearrange("p (c f) -> p c f", c=KD)
                               for a in (W.high, W.low))) for o in range(2))
            return gate, up, W[:, i, 2 * KD * P:]

        with nc.Block() as block:

            @block.sync
            def _(sp):
                sp.dma_start(picks[:], io["c_pick"]).then_inc(p_loaded, 16)
                with sp.Fori(0, NC) as c:
                    for e in range(NE):
                        sp.wait_ge(w_split, c * NE + slot_before(e) + NW + 1)
                        sp.dma_start(raw[:, e % NW], io["w_gated"][e]).then_inc(w_loaded[e % NW], 16)
                sp.wait_ge(p_loaded, 16)

            @block.tensor
            def _(pe):
                def up(c, e):
                    wg, wu, _ = matrices(e % NW)
                    pe.wait_ge(w_split, c * NE + e + NW + 1)
                    pe.wait_ge(full_done, c * NE + e + 1)
                    for w, ps in ((wg, G), (wu, U)):
                        for kd in range(KD):
                            product(nc, ps[:, e % 2, :], w[:, kd, :], k.xnT[:, kd, bass.ds(c * S, S)], kd == 0, kd == KD - 1)
                    mm = nc.tensor.matmul(CB[:, e % 2, :], pick[:, e % E32, :], r.combT[:, bass.ds(c * S, S)],
                                          start=True, stop=True)
                    mm.then_inc(gu_ready, 1)

                def down(c, e):
                    wd = matrices(e % NW)[2]
                    pe.wait_ge(hid_done, c * NE + e + 1)
                    if e == 0:
                        pe.wait_ge(y_added, c * TPB + TPB)
                    for i in range(TPB):
                        mm = product(nc, Y[:, i // 2, i % 2, :], hid[:, e % NHID, i * P:(i + 1) * P], wd,
                                     e == 0 and i % 2 == 0, e == NE - 1)
                    mm.then_inc(down_done, 1)

                pe.wait_ge(p_ready, 1)
                with pe.Fori(0, NC) as c:
                    for e in range(NE):
                        up(c, e)
                        if e >= 2:
                            down(c, e - 2)
                    down(c, NE - 2)
                    down(c, NE - 1)

            @block.scalar
            def _(act):
                def matrices_high(c, e):
                    uses = len(range(e % NW, NE, NW))
                    act.wait_ge(w_loaded[e % NW], c * (16 * uses) + (e // NW) * 16 + 16)
                    act.wait_ge(down_done, c * NE + slot_before(e) + NW + 1)
                    nc.scalar.copy(W.high[:, e % NW], raw[:, e % NW]).then_inc(w_high, 1)

                def hidden_high(c, e):
                    act.wait_ge(full_done, c * NE + e + 3)
                    act.wait_ge(down_done, c * NE + slot_before(e, NHID) + NW + 1)
                    nc.scalar.copy(hid.high[:, e % NHID, :], full[:, e % 2, :]).then_inc(hid_high, 1)

                act.sem_inc(down_done, NW)
                with act.Fori(0, NC) as c:
                    matrices_high(c, 0)
                    matrices_high(c, 1)
                    for e in range(NE):
                        act.wait_ge(gu_ready, c * NE + e + 1)
                        act.wait_ge(prod_done, c * NE + e + 1)
                        nc.scalar.activation(sil[:, e % 2, :], G[:, e % 2, :], ACT.Silu).then_inc(sil_done, 1)
                        if e + 2 < NE:
                            matrices_high(c, e + 2)
                        hidden_high(c, e)

            @block.gpsimd
            def _(pool):
                with pool.Fori(0, NC) as c:
                    for e in range(NE):
                        pool.wait_ge(w_high, c * NE + e + 1)
                        low_part(nc.gpsimd, W[:, e % NW], raw[:, e % NW]).then_inc(w_split, 1)

            @block.vector
            def _(dve):
                def hidden(c, e):
                    i = e % 2
                    dve.wait_ge(sil_done, c * NE + e + 1)
                    last = full if e >= E32 else prod
                    nc.vector.tensor_tensor(last[:, i, :], sil[:, i, :], U[:, i, :], ALU.mult).then_inc(prod_done, 1)
                    dve.wait_ge(prod_done, c * NE + e + 3)
                    if e >= E32:
                        dve.sem_inc(full_done, 1)
                    else:
                        nc.vector.tensor_tensor(full[:, i, :], prod[:, i, :], CB[:, i, :], ALU.mult).then_inc(full_done, 1)

                def hidden_low(c, e):
                    dve.wait_ge(hid_high, c * NE + e + 1)
                    low_part(nc.vector, hid[:, e % NHID, :], full[:, e % 2, :]).then_inc(hid_done, 1)

                dve.sem_inc(full_done, 2)
                dve.sem_inc(prod_done, 2)
                dve.sem_inc(w_split, NW)
                dve.sem_inc(y_added, TPB)
                dve.wait_ge(p_loaded, 16)
                nc.vector.tensor_copy(pick[:], picks[:]).then_inc(p_ready, 1)
                with dve.Fori(0, NC) as c:
                    for e in range(NE):
                        hidden(c, e)
                        hidden_low(c, e)
                    dve.wait_ge(down_done, c * NE + NE + NW)
                    for i in range(TPB):
                        xt = k.x[:, bass.ds(c * TPB + i, 1), :].rearrange("p t d -> p (t d)")
                        nc.vector.tensor_tensor(xt, xt, Y[:, i // 2, i % 2, :], ALU.add).then_inc(y_added, 1)


def gated_moe(nc, k, io):
    with ExitStack() as ctx:
        ph = Phase(nc, ctx, "moe1")
        r = Routes()
        r.combT = ph.sb("combT", [3 * E32, N], BF16)
        w = Weights(ph)
        w.gate_of(E32, io["L1_ffn_gate_w"].rearrange("(c p) e -> p c e", p=P), ph.sb("logitsT", [E32, N])[:])
        w.gbias = w.array("gbias", [P, NT, E32], io["gbias1"])
        normalised(nc, k, ctx, "ln_moe1", w)
        group_route_phase(nc, k, w, r)
        gated_experts_phase(nc, k, io, r)


def moe(nc, k, io, layer, out=None):
    if layer == 1:
        gated_moe(nc, k, io)
    else:
        slot_moe(nc, k, io, MOES[layer], out)


def ffn_layout(f):
    io = {}

    def each_token(a, *shape):
        return np.ascontiguousarray(np.broadcast_to(a, shape))

    io["L0_ffn_gate_w"] = np.ascontiguousarray(f["L0_ffn_gate_w"].T)
    io["L2_ffn_Wr"], io["L3_ffn_w_g"] = f["L2_ffn_Wr"], f["L3_ffn_w_g"]
    io["gbias0"] = each_token(np.stack([f["L0_ffn_gate_b"], f["L0_ffn_expert_bias"]])[None, :, None, :], P, 2, NT, E8)
    io["gbias2"] = each_token(f["L2_ffn_br"][None, None, None, :], P, 1, NT, E8)
    for m in MOES.values():
        io[m.w1], io[m.w2] = f[m.w1], f[m.w2]
        if m.b1:
            io[m.b1] = np.ascontiguousarray(f[m.b1].reshape(E8, FT, P).transpose(0, 2, 1))
            io[m.b2] = each_token(f[m.b2][:, None, :], E8, P, D)
    io["L1_ffn_gate_w"] = np.ascontiguousarray(f["L1_ffn_gate_w"].T)
    io["gbias1"] = each_token(f["L1_ffn_gate_bias"][None, None, :], P, NT, E32)
    wg = np.concatenate([f["L1_ffn_w_gate"], f["L1_ffn_sh_gate"].reshape(SHARED, P, D)])
    wu = np.concatenate([f["L1_ffn_w_up"], f["L1_ffn_sh_up"].reshape(SHARED, P, D)])
    wd = np.concatenate([f["L1_ffn_w_down"].transpose(0, 2, 1), f["L1_ffn_sh_down"].T.reshape(SHARED, P, D)])
    turned = [w.transpose(0, 2, 1).reshape(-1, KD, P, P).transpose(0, 2, 1, 3).reshape(-1, P, KD * P) for w in (wg, wu)]
    io["w_gated"] = np.ascontiguousarray(np.concatenate(turned + [wd], axis=2))
    pre = "L3_xattn_"
    for w in ("Wq", "Wk", "Wv"):
        io[pre + w] = np.ascontiguousarray(f[pre + w].T)
    for b in ("bq", "bk"):
        io[pre + b] = np.ascontiguousarray(f[pre + b].reshape(KD, P).T)
    io[pre + "bv"] = each_token(f[pre + "bv"][None, :], P, D)
    io[pre + "beta"] = each_token(np.stack([f[pre + "beta_" + n].reshape(()) for n in ("risk", "prio", "impl")])[None, :], P, 3)
    return io



class Kept:
    pass


def program(nc, io, out):
    with ExitStack() as ctx:
        ph = Phase(nc, ctx, "kept")
        k = Kept()
        k.x = ph.sb("x", [P, NT, D])
        k.identf = ph.sb("identf", [P, P])
        k.identb = ph.sb("identb", [P, P], BF16)
        k.before = ph.sb("before", [P, P], BF16)
        k.onesb = ph.sb("onesb", [P, P], BF16)
        k.iota = ph.sb("iota", [P, 32])
        k.half = ph.sb("half", [P, NT])
        k.st = ph.sb("st", [P, NT, 6])
        k.st_there = False
        k.qparts = nc.dram_tensor("qparts", (H, PARTS * DH, N), BF16, kind="Internal").ap()
        k.kparts = nc.dram_tensor("kparts", (H, PARTS * DH, N), BF16, kind="Internal").ap()
        k.xg = nc.dram_tensor("xg", (8 * 640, D), F32, kind="Internal").ap()
        k.yg = nc.dram_tensor("yg", (8 * 640, D), F32, kind="Internal").ap()
        k.cleared, k.zero = ph.sem("cleared"), ph.sb("zero", [P, D])
        k.scattered = ph.sem("scattered")
        k.gathered = [ph.sem(f"gathered{i}") for i in range(GATHERS)]
        k.n_scattered = k.n_gathered = 0
        with_context = ctx.enter_context(ExitStack())
        k.ctxT = Pair.of(Phase(nc, with_context, "context"), "ctxT", [P, KD, N])
        setup_phase(nc, k, io)
        clear_semaphores(nc)
        stage_list = [
            lambda: heads_attention(nc, k, io, 0),
            lambda: moe(nc, k, io, 0),
            lambda: heads_attention(nc, k, io, 1, rope=True),
            lambda: moe(nc, k, io, 1),
            lambda: heads_attention(nc, k, io, 2, masked=True),
            lambda: moe(nc, k, io, 2),
            lambda: whole_attention(nc, k, io),
            lambda: moe(nc, k, io, 3, out),
        ]
        for s, stage in enumerate(stage_list):
            last = s == len(stage_list) - 1
            if last:
                with_context.close()
            stage()
            k.st_there = s != 3
            if not last:
                clear_semaphores(nc)



def laid_out(inputs):
    f = {n: np.ascontiguousarray(a) for n, a in inputs.items()}
    io = {n: f[n] for n in ("x", "ctx_1024", "fside_BxSxS2_0", "mask_Bx1xSxS2_ik0")}

    def column(a, n=KD):
        return np.ascontiguousarray(a.reshape(n, P).T)

    def beside(a, axis):
        return np.concatenate([a, np.zeros_like(a)], axis=axis)

    turn = np.arange(D).reshape(H, 2, DH // 2)[:, ::-1].reshape(D)
    for layer in range(3):
        pre = f"L{layer}_xattn_"
        for w in ("Wq", "Wk", "Wv"):
            io[pre + w] = np.ascontiguousarray(f[pre + w].T)
        for b in ("bq", "bk"):
            io[pre + b] = column(f[pre + b])
        if layer == 1:
            for w in ("Wq", "Wk"):
                io[pre + w + "_turn"] = np.ascontiguousarray(f[pre + w][turn].T)
            for b in ("bq", "bk"):
                io[pre + b + "_turn"] = column(f[pre + b][turn])
        wo = beside(f[pre + "Wo"].T.reshape(NG, GH, DH, D), 2)
        wo[0, 0, DH] = f[pre + "bo"]
        io[pre + "Wo"] = np.ascontiguousarray(wo.reshape(NG, P, D))
        io[pre + "bv"] = column(beside(f[pre + "bv"].reshape(NG, GH, DH), 2).reshape(-1), NG)
    io.update(ffn_layout(f))
    io.update(constants())
    return io


def constants():
    c = {}
    c["c_identf"] = np.eye(P, dtype=np.float32)
    p = np.arange(P)
    row = np.arange(3 * H) % H
    c["c_spread"] = np.ascontiguousarray(((row[:, None, None] // NG == p[None, None, :] // HS)
                                          & (row[:, None, None] % NG == np.arange(NG)[None, :, None])).astype(np.float32))
    c["c_before"] = (p[:, None] < p[None, :]).astype(np.float32)
    c["c_iota"] = np.broadcast_to(np.arange(32, dtype=np.float32), (P, 32)).copy()
    c["c_pick"] = np.ascontiguousarray(np.broadcast_to((np.arange(3 * E32)[:, None] % E32 == np.arange(E32)[None, :])[:, :, None],
                                                       (3 * E32, E32, P))).astype(np.float32)
    inv_freq = (1.0 / np.float32(10000.0) ** (np.arange(0, DH, 2, dtype=np.float32) / np.float32(DH))).astype(np.float32)
    pos = (np.float32(10.0) * (np.arange(S, dtype=np.float32) / np.float32(S))).astype(np.float32)
    freqs = np.outer(pos, inv_freq).astype(np.float32)
    cos, sin = np.cos(freqs).T, np.sin(freqs).T
    cos = np.tile(np.concatenate([cos, cos]), (P // DH, 1)).astype(np.float32)
    sin = np.tile(np.concatenate([-sin, sin]), (P // DH, 1)).astype(np.float32)
    c["c_cosk"], c["c_sink"] = cos, sin
    c["c_cosq"], c["c_sinq"] = cos * np.float32(DH ** -0.5), sin * np.float32(DH ** -0.5)
    return c


def kernel(**inputs):
    import concourse.bacc as bacc
    from concourse.bass_utils import run_bass_kernel_spmd

    nc = bacc.Bacc("TRN2", target_bir_lowering=False, num_devices=1)
    arrays = {f"in_{n}": a for n, a in laid_out(inputs).items()}
    io = {n[3:]: nc.dram_tensor(n, a.shape, mybir.dt.from_np(a.dtype), kind="ExternalInput").ap() for n, a in arrays.items()}
    out = nc.dram_tensor("out_x", (B, S, D), F32, kind="ExternalOutput").ap()
    program(nc, io, out)
    r = run_bass_kernel_spmd(nc, [arrays], core_ids=[0])
    return r.results[0]["out_x"]
```
